# Optimizing a Trainium2 kernel written in Bass

```python
import numpy as np
import jax
import jax.numpy as jnp

def _softmax(x, axis=-1):
    return jax.nn.softmax(x, axis=axis)

def _gelu(x):
    return jax.nn.gelu(x, approximate=True)

def _silu(x):
    return jax.nn.silu(x)

def _sigmoid(x):
    return jax.nn.sigmoid(x)

def _layernorm(x, axis=-1, eps=1e-05):
    m = jnp.mean(x, axis=axis, keepdims=True)
    v = jnp.var(x, axis=axis, keepdims=True)
    return (x - m) / jnp.sqrt(v + eps)

def _scatter_add(tgt, idx, src, axis=0):
    return tgt.at[idx].add(src)

def _segment_sum(src, seg, n):
    return jax.ops.segment_sum(src, seg, n)
kernel_name = 'mk_perceiver_d1_seqx_r4_d4aa80'

def setup_inputs(seed: int=0):
    np.random.seed(seed)
    _w = jnp.asarray

    def _rec_inputs():
        import jax
        import jax.numpy as jnp
        _rk = jax.random.key(seed)
        x = -0.0002928 + 1 * jax.random.normal(jax.random.fold_in(_rk, 1), (8, 64, 256), jnp.float32)
        _lenS = 64 - jax.random.randint(jax.random.fold_in(_rk, 7), (8,), 0, max(1, 64 // 4) + 1, jnp.int32)
        _lenS2 = 1601 - jax.random.randint(jax.random.fold_in(_rk, 8), (8,), 0, max(1, 1601 // 4) + 1, jnp.int32)
        _ctx_1024P = jax.random.normal(jax.random.fold_in(_rk, 11), (8, 16, 256), jnp.float32)
        _ctx_1024c = jax.random.dirichlet(jax.random.fold_in(_rk, 511), 0.3 * jnp.ones((16,), jnp.float32), (8, 1601))
        _ctx_1024t = jnp.einsum('bsk,bkd->bsd', _ctx_1024c, _ctx_1024P)
        _ctx_1024t = _ctx_1024t * jax.lax.rsqrt(jnp.mean(jnp.square(_ctx_1024t)) + 1e-12) * 0.953939
        ctx_1024 = -1.39393e-06 + 0.999914 * (_ctx_1024t + 0.3 * jax.random.normal(jax.random.fold_in(_rk, 611), (8, 1601, 256), jnp.float32))
        return (x, ctx_1024)
    x, ctx_1024 = _rec_inputs()

    def _L0_xattn_setup():
        import jax, jax.numpy as jnp
        import numpy as np
        import math
        EPS = 1e-05

        def _layernorm(x, gamma, beta):
            mu = jnp.mean(x, axis=-1, keepdims=True)
            var = jnp.mean(jnp.square(x - mu), axis=-1, keepdims=True)
            return (x - mu) * jax.lax.rsqrt(var + EPS) * gamma + beta
        key = jax.random.key(seed)
        ks = jax.random.split(key, 8)
        B, Sq, Sk, D = (2, 512, 512, 256)
        s = 1.0 / math.sqrt(D)
        return {'Q': jax.random.normal(ks[0], (B, Sq, D), jnp.float32), 'K': jax.random.normal(ks[1], (B, Sk, D), jnp.float32), 'Wq': jax.random.normal(ks[2], (D, D), jnp.float32) * s, 'bq': jnp.zeros((D,), jnp.float32), 'Wk': jax.random.normal(ks[3], (D, D), jnp.float32) * s, 'bk': jnp.zeros((D,), jnp.float32), 'Wv': jax.random.normal(ks[4], (D, D), jnp.float32) * s, 'bv': jnp.zeros((D,), jnp.float32), 'Wo': jax.random.normal(ks[5], (D, D), jnp.float32) * s, 'bo': jnp.zeros((D,), jnp.float32), 'g0': jnp.ones((D,), jnp.float32), 'b0': jnp.zeros((D,), jnp.float32), 'g1': jnp.ones((D,), jnp.float32), 'b1': jnp.zeros((D,), jnp.float32)}
    _L0_xattn_all = _L0_xattn_setup()
    _L0_xattn_in = {k: v for k, v in _L0_xattn_all.items() if k in ('Wq', 'bq', 'Wk', 'bk', 'Wv', 'bv', 'Wo', 'bo', 'g0', 'b0', 'g1', 'b1')}
    del _L0_xattn_all

    def _L0_attn_setup():
        import jax, jax.numpy as jnp
        import numpy as np
        N_EMBD = 256
        QK_DIM = 16
        key = jax.random.key(seed)
        k1, k2, k3, k4, k5 = jax.random.split(key, 5)
        b, s = (8, 512)
        lim = 1.0 / np.sqrt(N_EMBD)
        return {'x': jax.random.normal(k1, (b, s, N_EMBD), dtype=jnp.float32), 'w_q': jax.random.uniform(k2, (QK_DIM, N_EMBD), minval=-lim, maxval=lim, dtype=jnp.float32), 'b_q': jax.random.uniform(k3, (QK_DIM,), minval=-lim, maxval=lim, dtype=jnp.float32), 'w_k': jax.random.uniform(k4, (QK_DIM, N_EMBD), minval=-lim, maxval=lim, dtype=jnp.float32), 'b_k': jax.random.uniform(k5, (QK_DIM,), minval=-lim, maxval=lim, dtype=jnp.float32)}
    _L0_attn_all = _L0_attn_setup()
    _L0_attn_in = {k: v for k, v in _L0_attn_all.items() if k in ('w_q', 'b_q', 'w_k', 'b_k')}
    del _L0_attn_all

    def _L0_ffn_setup():
        import jax, jax.numpy as jnp
        import numpy as np
        B, S, D, F, E = (4, 512, 256, 1024, 8)
        key = jax.random.key(seed)
        ks = jax.random.split(key, 7)
        s1 = 1.0 / np.sqrt(D)
        s2 = 1.0 / np.sqrt(F)
        x = jax.random.normal(ks[0], (B, S, D), dtype=jnp.float32)
        W1 = jax.random.uniform(ks[1], (E, D, F), jnp.float32, -s1, s1)
        b1 = jax.random.uniform(ks[2], (E, F), jnp.float32, -s1, s1)
        W2 = jax.random.uniform(ks[3], (E, F, D), jnp.float32, -s2, s2)
        b2 = jax.random.uniform(ks[4], (E, D), jnp.float32, -s2, s2)
        Wr = jax.random.uniform(ks[5], (D, E), jnp.float32, -s1, s1)
        br = jax.random.uniform(ks[6], (E,), jnp.float32, -s1, s1)
        return {'x': x, 'W1': W1, 'b1': b1, 'W2': W2, 'b2': b2, 'Wr': Wr, 'br': br}
    _L0_ffn_all = _L0_ffn_setup()
    _L0_ffn_in = {k: v for k, v in _L0_ffn_all.items() if k in ('W1', 'b1', 'W2', 'b2', 'Wr', 'br')}
    del _L0_ffn_all
    return {'x': x, 'ctx_1024': ctx_1024, 'L0_xattn_Wq': _L0_xattn_in['Wq'], 'L0_xattn_bq': _L0_xattn_in['bq'], 'L0_xattn_Wk': _L0_xattn_in['Wk'], 'L0_xattn_bk': _L0_xattn_in['bk'], 'L0_xattn_Wv': _L0_xattn_in['Wv'], 'L0_xattn_bv': _L0_xattn_in['bv'], 'L0_xattn_Wo': _L0_xattn_in['Wo'], 'L0_xattn_bo': _L0_xattn_in['bo'], 'L0_xattn_g0': _L0_xattn_in['g0'], 'L0_xattn_b0': _L0_xattn_in['b0'], 'L0_xattn_g1': _L0_xattn_in['g1'], 'L0_xattn_b1': _L0_xattn_in['b1'], 'L0_attn_w_q': _L0_attn_in['w_q'], 'L0_attn_b_q': _L0_attn_in['b_q'], 'L0_attn_w_k': _L0_attn_in['w_k'], 'L0_attn_b_k': _L0_attn_in['b_k'], 'L0_ffn_W1': _L0_ffn_in['W1'], 'L0_ffn_b1': _L0_ffn_in['b1'], 'L0_ffn_W2': _L0_ffn_in['W2'], 'L0_ffn_b2': _L0_ffn_in['b2'], 'L0_ffn_Wr': _L0_ffn_in['Wr'], 'L0_ffn_br': _L0_ffn_in['br']}

def reference(x, ctx_1024, L0_xattn_Wq, L0_xattn_bq, L0_xattn_Wk, L0_xattn_bk, L0_xattn_Wv, L0_xattn_bv, L0_xattn_Wo, L0_xattn_bo, L0_xattn_g0, L0_xattn_b0, L0_xattn_g1, L0_xattn_b1, L0_attn_w_q, L0_attn_b_q, L0_attn_w_k, L0_attn_b_k, L0_ffn_W1, L0_ffn_b1, L0_ffn_W2, L0_ffn_b2, L0_ffn_Wr, L0_ffn_br):
    import jax
    import jax.numpy as jnp

    def _L0_xattn_ref(Q, K, Wq, bq, Wk, bk, Wv, bv, Wo, bo, g0, b0, g1, b1):
        import jax, jax.numpy as jnp
        import numpy as np
        import math
        EPS = 1e-05

        def _layernorm(x, gamma, beta):
            mu = jnp.mean(x, axis=-1, keepdims=True)
            var = jnp.mean(jnp.square(x - mu), axis=-1, keepdims=True)
            return (x - mu) * jax.lax.rsqrt(var + EPS) * gamma + beta
        H = 16
        B, Sq, D = Q.shape
        dh = D // H
        Qp = Q @ Wq + bq
        Kp = K @ Wk + bk
        Vp = Kp @ Wv + bv
        Qh = Qp.reshape(B, Sq, H, dh).transpose(0, 2, 1, 3)
        Kh = Kp.reshape(B, -1, H, dh).transpose(0, 2, 1, 3)
        Vh = Vp.reshape(B, -1, H, dh).transpose(0, 2, 1, 3)
        scores = jnp.einsum('bhqd,bhkd->bhqk', Qh, Kh) / math.sqrt(dh)
        attn = jax.nn.softmax(scores, axis=-1)
        Oh = Qh + jnp.einsum('bhqk,bhkd->bhqd', attn, Vh)
        O = Oh.transpose(0, 2, 1, 3).reshape(B, Sq, D)
        O = _layernorm(O, g0, b0)
        O = O + jax.nn.gelu(O @ Wo + bo, approximate=False)
        O = _layernorm(O, g1, b1)
        return O

    def _L0_attn_ref(x, w_q, b_q, w_k, b_k):
        import jax, jax.numpy as jnp
        import numpy as np
        N_EMBD = 256
        QK_DIM = 16
        s = x.shape[-2]
        q = jnp.einsum('bsd,ed->bse', x, w_q) + b_q
        k = jnp.einsum('bsd,ed->bse', x, w_k) + b_k
        scale = 1.0 / jnp.sqrt(jnp.asarray(QK_DIM, dtype=x.dtype))
        mask = jnp.arange(s)[:, None] >= jnp.arange(s)[None, :]
        scores = jnp.einsum('bqe,bke->bqk', q, k) * scale
        scores = jnp.where(mask[None], scores, jnp.asarray(-10000.0, dtype=x.dtype))
        probs = jax.nn.softmax(scores, axis=-1)
        return jnp.einsum('bqk,bkv->bqv', probs, x)

    def _L0_ffn_ref(x, W1, b1, W2, b2, Wr, br):
        import jax, jax.numpy as jnp
        import numpy as np
        B, S, D, F, E = (4, 512, 256, 1024, 8)
        b, s, d = x.shape
        e = Wr.shape[1]
        logits = x @ Wr + br
        idx = jnp.argmax(logits, axis=-1)
        probs = jax.nn.softmax(logits, axis=-1)
        gates = jnp.take_along_axis(probs, idx[..., None], axis=-1)[..., 0]
        xf = x.reshape(-1, d)
        idxf = idx.reshape(-1)
        gf = gates.reshape(-1)
        out = jnp.zeros_like(xf)
        for ei in range(e):
            h = jax.nn.gelu(xf @ W1[ei] + b1[ei], approximate=False)
            y = h @ W2[ei] + b2[ei]
            mask = (idxf == ei).astype(xf.dtype)
            out = out + y * (gf * mask)[:, None]
        return out.reshape(b, s, d)
    x = x + _L0_xattn_ref(_layernorm(x, axis=-1), ctx_1024, L0_xattn_Wq, L0_xattn_bq, L0_xattn_Wk, L0_xattn_bk, L0_xattn_Wv, L0_xattn_bv, L0_xattn_Wo, L0_xattn_bo, L0_xattn_g0, L0_xattn_b0, L0_xattn_g1, L0_xattn_b1)
    x = x + _L0_attn_ref(_layernorm(x, axis=-1), L0_attn_w_q, L0_attn_b_q, L0_attn_w_k, L0_attn_b_k)
    x = x + _L0_ffn_ref(_layernorm(x, axis=-1), L0_ffn_W1, L0_ffn_b1, L0_ffn_W2, L0_ffn_b2, L0_ffn_Wr, L0_ffn_br)
    return x

_drawn_inputs = setup_inputs


def setup_inputs(seed=0):
    import zlib

    import numpy as np

    out = dict(_drawn_inputs(seed))
    spreads = {'L0_xattn_bq': (0.0, 0.1),
     'L0_xattn_bk': (0.0, 0.1),
     'L0_xattn_bv': (0.0, 0.1),
     'L0_xattn_bo': (0.0, 0.1),
     'L0_xattn_g0': (1.0, 0.2),
     'L0_xattn_b0': (0.0, 0.1),
     'L0_xattn_g1': (1.0, 0.2),
     'L0_xattn_b1': (0.0, 0.1)}
    factors = {'L0_attn_b_q': 8.0,
     'L0_attn_b_k': 64.0,
     'L0_ffn_b1': 26.882,
     'L0_ffn_b2': 8.0,
     'L0_ffn_br': 8.0}
    for name, (base, spread) in spreads.items():
        noise = np.random.default_rng([zlib.crc32(name.encode()), seed]).standard_normal(out[name].shape)
        drawn = base * np.exp(spread * noise) if base else spread * noise
        out[name] = jnp.asarray(drawn.astype(out[name].dtype))
    for name, factor in factors.items():
        out[name] = (out[name] * factor).astype(out[name].dtype)
    return out
```

```python
from contextlib import ExitStack

import concourse.bass as bass
from concourse import mybir

F32 = mybir.dt.float32
BF16 = mybir.dt.bfloat16
ALU = mybir.AluOpType
ACT = mybir.ActivationFunctionType
AX = mybir.AxisListType
ET = mybir.EngineType
EPS = 1e-5


def perceiver_kernel(nc, x, ctx_in, Wq, bq, Wk, bk, Wv, bv, Wo, bo, g0, b0, g1, b1,
                     w_q, b_q, w_k, b_k, W1, fb1, W2, fb2, Wr, br, out):
    NB, SQ, D = x.shape
    SK = ctx_in.shape[1]
    H, DH = 16, D // 16
    P = 128
    KD = D // P
    NT = NB * SQ // P
    T = NB * SQ
    KT = -(-SK // P)
    KL = SK - (KT - 1) * P
    CH = 4
    NC = -(-KT // CH)
    HG = H // 2
    NPJ = HG // 2
    UG = NPJ * NC
    UB = 2 * UG
    NV = -(-KT // 2)
    NTR = KD * NC
    NKP = 2 * NC
    QR = 6 * DH
    KR = QR + 3
    VW = DH + 1
    RP = 4
    RR = 4
    E_, F_ = W1.shape[0], W1.shape[2]
    FT = F_ // P
    QD = w_q.shape[0]

    def width(c):
        return min(CH * P, SK - c * CH * P)

    def keys(t):
        return min(P, SK - t * P)

    ctx = ExitStack()
    with ctx:
        def sb(name, shape, dt=F32):
            return ctx.enter_context(nc.sbuf_tensor(name, shape, dt))

        def sem(name):
            return ctx.enter_context(nc.semaphore(name))

        bank = [ctx.enter_context(nc.psum_tensor(f"bank{n}", [P, 512], F32)) for n in range(8)]
        bkT = [bank[0], bank[1]]
        bkV = [bank[2], bank[1]]
        bkX = [bank[3], bank[4]]
        bkS = [bank[5], bank[6]]
        bkO = bank[7]

        q_scr = nc.dram_tensor("q_parts", [3, D, T], BF16, kind="Internal").ap()
        k_scr = nc.dram_tensor("k_parts", [3, D, SK], BF16, kind="Internal").ap()

        ident = sb("ident", [P, P])
        identb = sb("identb", [P, P], BF16)
        wq_sb = sb("wq_sb", [P, KD, D])
        wk_sb = sb("wk_sb", [P, KD, D])
        wv_sb = sb("wv_sb", [P, KD, D])
        wo_sb = sb("wo_sb", [P, KD, D])
        wkv = sb("wkv", [P, KD, D])
        bqc = sb("bqc", [P, KD])
        bqs = sb("bqs", [P, KD])
        bkc = sb("bkc", [P, KD])
        rows = sb("rows", [P, 7, D])
        bkv = sb("bkv", [P, D])
        x_sb = sb("x_sb", [P, NT, D])
        xn = sb("xn", [P, NT, D])
        xnT = sb("xnT", [P, KD, T])
        qtok = sb("qtok", [P, NT, D])
        st = sb("st", [P, NT, 6])
        mv = sb("mv", [P, NT, 2])
        rstd = sb("rstd", [P, NT])
        ve = sb("ve", [P, NT])
        nwt = sb("nwt", [P, NT])
        half = sb("half", [P, NT])
        oall = sb("oall", [SQ, NB, D])
        wqk = sb("wqk", [QD, 2, D])
        wqkT = sb("wqkT", [P, 2, KD, QD])
        bqk = sb("bqk", [QD, 2])
        wr_sb = sb("wr_sb", [P, KD, E_])
        br_row = sb("br_row", [P, E_])
        b1_rows = sb("b1_rows", [E_ * FT, P])
        b1c = sb("b1c", [P, E_ * FT])
        b2_sb = sb("b2_sb", [E_, D])
        iota8 = sb("iota8", [P, E_])
        attn = ExitStack()
        def ab(name, shape, dt=F32):
            return attn.enter_context(nc.sbuf_tensor(name, shape, dt))
        cx = ab("cx", [P, KT, D])
        cxT = ab("cxT", [P, KD, SK])
        kp = [ab(f"kp{n}", [P, KD, SK], BF16) for n in range(3)]
        res = ab("res", [P, RR, CH * P])
        kst = ab("kst", [KR, H, SK], BF16)
        qst = ab("qst", [QR, H, T], BF16)
        qb = ab("qb", [KR, H, SQ], BF16)
        vaug = ab("vaug", [P, KT, H, VW])
        osb = ab("osb", [P, H // 4 * P])
        setup = ExitStack()

        def setup_sb(name, shape, dt=F32):
            return setup.enter_context(nc.sbuf_tensor(name, shape, dt))

        wkT = setup_sb("wkT", [P, KD, D])
        qf = setup_sb("qf", [P, KD, T])
        qp = [setup_sb(f"qp{n}", [P, KD, T], BF16) for n in range(3)]
        setup.close()
        prob = ab("prob", [P, RP, CH * P])
        mx = ab("mx", [P, H // 2, NC])
        nm = ab("nm", [P, NPJ])
        nr = ab("nr", [P, NPJ])
        mpt = ab("mpt", [P, NPJ, 4], BF16)
        rec = ab("rec", [P, H // 4, 2])
        attn.close()
        o_sb = sb("o_sb", [P, NT, D])
        q2T = sb("q2T", [QD, T])
        k2T = sb("k2T", [QD, T])
        sc = sb("sc", [P, NT, SQ])
        s4 = sb("s4", [P, NT])
        r4 = sb("r4", [P, NT])
        pblk = sb("pblk", [P, NT, P])
        pT = sb("pT", [P, NT, P])
        lg = sb("lg", [P, NT, E_])
        ex = sb("ex", [P, NT, E_])
        gates = sb("gates", [P, NT, E_])
        gT = sb("gT", [E_, T])
        acc = sb("acc", [P, NT, D])
        w1_sb = [sb(f"w1_sb{n}", [P, KD, F_]) for n in range(2)]
        w2_sb = [sb(f"w2_sb{n}", [P, FT, D]) for n in range(2)]
        hT = sb("hT", [P, FT, T])

        s_const = sem("s_const")
        s_ones = sem("s_ones")
        l_x = sem("l_x")
        l_w = sem("l_w")
        l_rows = sem("l_rows")
        s_chain = sem("s_chain")
        s_var = sem("s_var")
        s_pow = sem("s_pow")
        s_half = sem("s_half")
        s_xn = sem("s_xn")
        s_xtr = sem("s_xtr")
        s_xT = sem("s_xT")
        s_wtr = sem("s_wtr")
        s_wT = sem("s_wT")
        s_wkvp = sem("s_wkvp")
        s_wkv = sem("s_wkv")
        s_bqs = sem("s_bqs")
        s_qps = sem("s_qps")
        s_qf = sem("s_qf")
        s_qtp = sem("s_qtp")
        s_qt = sem("s_qt")
        s_qparts = sem("s_qparts")
        l_qw = sem("l_qw")
        l_qst = sem("l_qst")
        l_ctx = [sem(f"l_ctx{c}") for c in range(NC)]
        s_tr = sem("s_tr")
        s_ctxT = sem("s_ctxT")
        s_kproj = sem("s_kproj")
        s_k1 = sem("s_k1")
        s_res = sem("s_res")
        s_k2 = sem("s_k2")
        s_k3 = sem("s_k3")
        l_kw = [sem(f"l_kw{g}") for g in range(2)]
        l_kst = [sem(f"l_kst{g}") for g in range(2)]
        s_qb = sem("s_qb")
        s_v = sem("s_v")
        s_vev = sem("s_vev")
        s_ms = sem("s_ms")
        s_mx = sem("s_mx")
        s_mp = sem("s_mp")
        s_mstep = sem("s_mstep")
        s_rec = sem("s_rec")
        s_mtr = sem("s_mtr")
        s_mrow = sem("s_mrow")
        s_st = sem("s_st")
        s_exp = sem("s_exp")
        s_pv = sem("s_pv")
        s_ocp = sem("s_ocp")
        s_otr = sem("s_otr")
        s_oev = sem("s_oev")
        l_xa = sem("l_xa")
        l_small = sem("l_small")
        s_iota = sem("s_iota")
        s_pz = sem("s_pz")
        s_smallT = sem("s_smallT")
        s_smallc = sem("s_smallc")
        s_o1 = sem("s_o1")
        s_wo = sem("s_wo")
        s_wob = sem("s_wob")
        s_gelu = sem("s_gelu")
        s_nT = sem("s_nT")
        s_nTc = sem("s_nTc")
        s_xn2 = sem("s_xn2")
        s_qk = sem("s_qk")
        s_qkc = sem("s_qkc")
        s_sc = sem("s_sc")
        s_scc = sem("s_scc")
        s_mask = sem("s_mask")
        s_sub = sem("s_sub")
        s_sexp = sem("s_sexp")
        s_pblk = sem("s_pblk")
        s_pT = sem("s_pT")
        s_pTc = sem("s_pTc")
        s_att = sem("s_att")
        s_xn3 = sem("s_xn3")
        s_lg = sem("s_lg")
        s_lsub = sem("s_lsub")
        s_lexp = sem("s_lexp")
        s_gate = sem("s_gate")
        s_gT = sem("s_gT")
        s_gTc = sem("s_gTc")
        s_b2 = sem("s_b2")
        l_w1 = [sem(f"l_w1_{n}") for n in range(2)]
        l_w2 = [sem(f"l_w2_{n}") for n in range(2)]
        s_h = sem("s_h")
        s_hT = sem("s_hT")
        s_y = sem("s_y")
        s_acc = sem("s_acc")
        l_out = sem("l_out")

        chain = [0]
        norms = [0]

        def link(dve, ins):
            chain[0] += 1
            ins.then_inc(s_chain, 1)
            dve.wait_ge(s_chain, chain[0])

        def layernorm(dve, dst, src, done=None):
            for t in range(NT):
                ins = dve.bn_stats(st[:, t, :], src[:, t, :])
            link(dve, ins)
            for t in range(NT):
                ins = dve.bn_aggr(mv[:, t, :], st[:, t, :])
            link(dve, ins)
            norms[0] += 1
            dve.tensor_scalar(ve[:, :], mv[:, :, 1], EPS, None, ALU.add).then_inc(s_var, 1)
            dve.wait_ge(s_pow, norms[0])
            link(dve, dve.scalar_tensor_tensor(out=nwt[:, :], in0=rstd[:, :], scalar=-0.5, in1=rstd[:, :],
                                               op0=ALU.mult, op1=ALU.mult))
            link(dve, dve.tensor_tensor(nwt[:, :], nwt[:, :], ve[:, :], ALU.mult))
            link(dve, dve.scalar_tensor_tensor(out=rstd[:, :], in0=nwt[:, :], scalar=1.5, in1=rstd[:, :],
                                               op0=ALU.add, op1=ALU.mult))
            for t in range(NT):
                ins = dve.tensor_scalar(dst[:, t, :], src[:, t, :], mv[:, t, 0:1], rstd[:, t:t + 1],
                                        ALU.subtract, ALU.mult)
                if done is not None:
                    ins.then_inc(done, 1)
            if done is None:
                link(dve, ins)

        def row(n):
            return rows[:, n:n + 1, :].broadcast_to([P, NT, D])

        def pool_pow(pool, n):
            pool.wait_ge(s_var, n)
            pool.tensor_tensor(rstd[:, :], ve[:, :], half[:, :], ALU.pow).then_inc(s_pow, 1)

        def tail_loads(sp):
            for e in range(E_):
                if e >= 2:
                    sp.wait_ge(s_h, FT * (e - 1))
                sp.dma_start(w1_sb[e % 2][:, :, :], W1[e].rearrange("(k p) f -> p k f", p=P)
                             ).then_inc(l_w1[e % 2], 16)
                if e >= 2:
                    sp.wait_ge(s_y, FT * (e - 1))
                sp.dma_start(w2_sb[e % 2][:, :, :], W2[e].rearrange("(f p) d -> p f d", p=P)
                             ).then_inc(l_w2[e % 2], 16)
            sp.wait_ge(s_acc, E_ + 1)
            sp.dma_start(out.rearrange("b s d -> (b s) d").rearrange("(t p) d -> p t d", p=P), acc[:, :, :]
                         ).then_inc(l_out, 16)
            sp.wait_ge(l_out, 16)

        def tail_pool(pool):
            pool.wait_ge(s_qb, NB)
            pool.memset(pblk[:, :, :], 0.0).then_inc(s_pz, 1)
            for e in range(E_):
                pool.memset(iota8[:, e:e + 1], float(e)).then_inc(s_iota, 1)
            pool_pow(pool, 2)
            pool_pow(pool, 3)
            pool_pow(pool, 4)
            pool.wait_ge(s_scc, 1)
            for hb in range(2):
                r = hb * SQ
                pool.affine_select(out=sc[r:r + SQ, :, :], in_=sc[r:r + SQ, :, :], compare_op=ALU.is_ge,
                                   fill=-10000.0, base=0, pattern=[[0, NT], [-1, SQ]],
                                   channel_multiplier=1).then_inc(s_mask, 1)
                pool.wait_ge(s_mask, hb + 1)
            pool_pow(pool, 5)

        def evac_T(act, done):
            for k in range(KD):
                act.wait_ge(s_nT, done + k + 1)
                act.activation(xnT[:, k, :], bank[k][:, :], ACT.Copy).then_inc(s_nTc, 1)

        def tail_act(act):
            act.wait_ge(s_smallT, 1)
            act.activation(wqkT[:, :, :, :].rearrange("p a k q -> p (a k q)"), bank[2][:, 0:2 * KD * QD], ACT.Copy
                           ).then_inc(s_smallc, 1)
            act.activation(b1c[:, :], bank[2][:, P:P + E_ * FT], ACT.Copy).then_inc(s_smallc, 1)
            evac_T(act, 0)
            for n in range(2):
                act.wait_ge(s_wob, n + 1)
                act.activation(o_sb[:, 2 * n:2 * n + 2, :], o_sb[:, 2 * n:2 * n + 2, :], ACT.Gelu
                               ).then_inc(s_gelu, 1)
            evac_T(act, 2)
            act.wait_ge(s_qk, 1)
            act.activation(q2T[:, :], bank[4][0:QD, :], ACT.Identity, bias=bqk[:, 0:1]).then_inc(s_qkc, 1)
            act.wait_ge(s_qk, 2)
            act.activation(k2T[:, :], bank[5][0:QD, :], ACT.Identity, bias=bqk[:, 1:2]).then_inc(s_qkc, 1)
            act.wait_ge(s_sc, 1)
            act.activation(sc[:, :, :].rearrange("p t k -> p (t k)"), bank[6][:, 0:NT * SQ], ACT.Copy,
                           scale=QD ** -0.5).then_inc(s_scc, 1)
            act.wait_ge(s_sub, 1)
            act.activation(sc[:, :, :], sc[:, :, :], ACT.Exp).then_inc(s_sexp, 1)
            act.wait_ge(s_pT, 1)
            act.activation(pT[:, :, :].rearrange("p t k -> p (t k)"), bank[7][:, :], ACT.Copy).then_inc(s_pTc, 1)
            evac_T(act, 4)
            act.wait_ge(s_lsub, 1)
            act.activation(ex[:, :, :], lg[:, :, :], ACT.Exp).then_inc(s_lexp, 1)
            act.wait_ge(s_gT, 1)
            act.activation(gT[:, :], bank[4][0:E_, :], ACT.Copy).then_inc(s_gTc, 1)
            for n in range(E_ * FT):
                act.wait_ge(s_h, n + 1)
                if n >= FT:
                    act.wait_ge(s_y, n - FT + 1)
                act.activation(hT[:, n % FT, :], bank[n % 4][:, :], ACT.Gelu, bias=b1c[:, n:n + 1]
                               ).then_inc(s_hT, 1)

        def transpose_x(pe, ready, at):
            pe.wait_ge(ready, at)
            for k in range(KD):
                for t in range(NT):
                    mm = pe.transpose(bank[k][:, t * P:(t + 1) * P], xn[:, t, k * P:(k + 1) * P], ident[:, :])
                mm.then_inc(s_nT, 1)

        def tail_pe(pe):
            pe.wait_ge(l_small, 16 * 8)
            for a in range(2):
                for k in range(KD):
                    pe.transpose(bank[2][:, (a * KD + k) * QD:(a * KD + k + 1) * QD],
                                 wqk[:, a, k * P:(k + 1) * P], ident[0:QD, 0:QD])
            pe.transpose(bank[2][:, P:P + E_ * FT], b1_rows[:, :], ident[0:E_ * FT, 0:E_ * FT]
                         ).then_inc(s_smallT, 1)
            transpose_x(pe, s_o1, 1)
            pe.wait_ge(s_smallc, 2)
            pe.wait_ge(s_nTc, 2)
            for t in range(NT):
                for k in range(KD):
                    mm = pe.matmul(bank[2 + t // 2][:, (t % 2) * D:(t % 2 + 1) * D], xnT[:, k, t * P:(t + 1) * P],
                                   wo_sb[:, k, :], start=(k == 0 and t % 2 == 0), stop=(k == KD - 1),
                                   skip_group_check=True)
                if t % 2:
                    mm.then_inc(s_wo, 1)
            transpose_x(pe, s_xn2, NT)
            pe.wait_ge(s_nTc, 4)
            for a in range(2):
                for k in range(KD):
                    mm = pe.matmul(bank[4 + a][0:QD, :], wqkT[:, a, k, :], xnT[:, k, :],
                                   start=(k == 0), stop=(k == KD - 1))
                mm.then_inc(s_qk, 1)
            pe.wait_ge(s_qkc, 2)
            for t in range(NT):
                for half in range(2):
                    tok = slice(t * P + half * SQ, t * P + (half + 1) * SQ)
                    mm = pe.matmul(bank[6][half * SQ:(half + 1) * SQ, t * SQ:(t + 1) * SQ], q2T[:, tok], k2T[:, tok],
                                   start=True, stop=True)
            mm.then_inc(s_sc, 1)
            pe.wait_ge(s_pblk, 1)
            for t in range(NT):
                mm = pe.transpose(bank[7][:, t * P:(t + 1) * P], pblk[:, t, :], ident[:, :])
            mm.then_inc(s_pT, 1)
            pe.wait_ge(s_pTc, 1)
            for t in range(NT):
                mm = pe.matmul(bank[2 + t // 2][:, (t % 2) * D:(t % 2 + 1) * D], pT[:, t, :], xn[:, t, :],
                               start=True, stop=True)
                if t % 2:
                    mm.then_inc(s_att, 1)
            transpose_x(pe, s_xn3, NT)
            pe.wait_ge(s_nTc, 6)
            for t in range(NT):
                for k in range(KD):
                    mm = pe.matmul(bank[5][:, t * E_:(t + 1) * E_], xnT[:, k, t * P:(t + 1) * P], wr_sb[:, k, :],
                                   start=(t == 0 and k == 0), stop=(k == KD - 1), skip_group_check=True)
            mm.then_inc(s_lg, 1)
            pe.wait_ge(s_gate, 1)
            for t in range(NT):
                mm = pe.transpose(bank[4][0:E_, t * P:(t + 1) * P], gates[:, t, :], ident[:, :])
            mm.then_inc(s_gT, 1)
            pe.wait_ge(s_gTc, 1)
            for t in range(NT):
                mm = pe.matmul(bank[6 + t // 2][:, (t % 2) * D:(t % 2 + 1) * D], gT[:, t * P:(t + 1) * P], b2_sb[:, :],
                               start=True, stop=True)
            mm.then_inc(s_b2, 1)
            for n in range(E_ * FT + 1):
                if n < E_ * FT:
                    e, f = divmod(n, FT)
                    if f == 0:
                        pe.wait_ge(l_w1[e % 2], 16 * (e // 2 + 1))
                    if n >= 4:
                        pe.wait_ge(s_hT, n - 3)
                    for k in range(KD):
                        mm = pe.matmul(bank[n % 4][:, :], w1_sb[e % 2][:, k, f * P:(f + 1) * P], xnT[:, k, :],
                                       start=(k == 0), stop=(k == KD - 1))
                    mm.then_inc(s_h, 1)
                if n:
                    e, f = divmod(n - 1, FT)
                    if f == 0:
                        pe.wait_ge(l_w2[e % 2], 16 * (e // 2 + 1))
                        pe.wait_ge(s_acc, e)
                    pe.wait_ge(s_hT, n)
                    for t in range(NT):
                        mm = pe.matmul(bank[4 + 2 * (e % 2) + t // 2][:, (t % 2) * D:(t % 2 + 1) * D],
                                       hT[:, f, t * P:(t + 1) * P], w2_sb[e % 2][:, f, :],
                                       start=(f == 0 and t % 2 == 0), stop=(f == FT - 1), skip_group_check=True)
                    mm.then_inc(s_y, 1)

        def tail_dve(dve):
            dve.wait_ge(l_xa, 32)
            link(dve, dve.tensor_tensor(o_sb[:, :, :], o_sb[:, :, :], qtok[:, :, :], ALU.add))
            layernorm(dve, xn, o_sb)
            link(dve, dve.tensor_tensor(xn[:, :, :], xn[:, :, :], row(3), ALU.mult))
            dve.tensor_tensor(xn[:, :, :], xn[:, :, :], row(4), ALU.add).then_inc(s_o1, 1)
            for n in range(2):
                dve.wait_ge(s_wo, n + 1)
                dve.tensor_tensor(o_sb[:, 2 * n:2 * n + 2, :], bank[2 + n][:, :].rearrange("p (t d) -> p t d", t=2),
                                  rows[:, 2:3, :].broadcast_to([P, 2, D]), ALU.add).then_inc(s_wob, 1)
            dve.wait_ge(s_gelu, 2)
            dve.wait_ge(s_o1, 1)
            link(dve, dve.tensor_tensor(o_sb[:, :, :], o_sb[:, :, :], xn[:, :, :], ALU.add))
            layernorm(dve, xn, o_sb)
            link(dve, dve.tensor_tensor(xn[:, :, :], xn[:, :, :], row(5), ALU.mult))
            link(dve, dve.tensor_tensor(xn[:, :, :], xn[:, :, :], row(6), ALU.add))
            link(dve, dve.tensor_tensor(x_sb[:, :, :], x_sb[:, :, :], xn[:, :, :], ALU.add))
            layernorm(dve, xn, x_sb, s_xn2)
            dve.wait_ge(s_mask, 2)
            link(dve, dve.tensor_reduce(s4[:, :], sc[:, :, :], AX.X, ALU.max))
            dve.tensor_tensor(sc[:, :, :], sc[:, :, :], s4[:, :].unsqueeze(2).broadcast_to([P, NT, SQ]),
                              ALU.subtract).then_inc(s_sub, 1)
            dve.wait_ge(s_sexp, 1)
            link(dve, dve.tensor_reduce(s4[:, :], sc[:, :, :], AX.X, ALU.add))
            link(dve, dve.reciprocal(r4[:, :], s4[:, :]))
            dve.wait_ge(s_pz, 1)
            for half in range(2):
                r = slice(half * SQ, (half + 1) * SQ)
                ins = dve.tensor_tensor(pblk[r, :, r], sc[r, :, :],
                                        r4[r, :].unsqueeze(2).broadcast_to([SQ, NT, SQ]), ALU.mult)
            ins.then_inc(s_pblk, 1)
            dve.wait_ge(s_xn2, NT)
            for n in range(2):
                dve.wait_ge(s_att, n + 1)
                ins = dve.tensor_tensor(x_sb[:, 2 * n:2 * n + 2, :], bank[2 + n][:, :].rearrange(
                    "p (t d) -> p t d", t=2), x_sb[:, 2 * n:2 * n + 2, :], ALU.add)
            link(dve, ins)
            layernorm(dve, xn, x_sb, s_xn3)
            dve.wait_ge(s_lg, 1)
            dve.wait_ge(s_iota, E_)
            link(dve, dve.tensor_tensor(lg[:, :, :], bank[5][:, 0:NT * E_].rearrange("p (t e) -> p t e", e=E_),
                                        br_row[:, :].unsqueeze(1).broadcast_to([P, NT, E_]), ALU.add))
            link(dve, dve.tensor_reduce(s4[:, :], lg[:, :, :], AX.X, ALU.max))
            wide = [P, NT, E_]
            dve.tensor_tensor(lg[:, :, :], lg[:, :, :], s4[:, :].unsqueeze(2).broadcast_to(wide),
                              ALU.subtract).then_inc(s_lsub, 1)
            dve.wait_ge(s_lsub, 1)
            link(dve, dve.tensor_scalar(gates[:, :, :], lg[:, :, :], 0.0, -float(E_), ALU.is_ge, ALU.mult))
            link(dve, dve.tensor_tensor(gates[:, :, :], gates[:, :, :],
                                        iota8[:, :].unsqueeze(1).broadcast_to(wide), ALU.add))
            link(dve, dve.tensor_reduce(s4[:, :], gates[:, :, :], AX.X, ALU.min))
            link(dve, dve.tensor_tensor(gates[:, :, :], gates[:, :, :],
                                        s4[:, :].unsqueeze(2).broadcast_to(wide), ALU.is_equal))
            dve.wait_ge(s_lexp, 1)
            link(dve, dve.tensor_reduce(s4[:, :], ex[:, :, :], AX.X, ALU.add))
            link(dve, dve.reciprocal(r4[:, :], s4[:, :]))
            dve.tensor_tensor(gates[:, :, :], gates[:, :, :], r4[:, :].unsqueeze(2).broadcast_to(wide),
                              ALU.mult).then_inc(s_gate, 1)
            dve.wait_ge(s_b2, 1)
            for n in range(2):
                ins = dve.tensor_tensor(acc[:, 2 * n:2 * n + 2, :], bank[6 + n][:, :].rearrange(
                    "p (t d) -> p t d", t=2), x_sb[:, 2 * n:2 * n + 2, :], ALU.add)
            ins.then_inc(s_acc, 1)
            for e in range(E_):
                dve.wait_ge(s_y, FT * (e + 1))
                dve.wait_ge(s_acc, e + 1)
                for t in range(NT):
                    ins = dve.scalar_tensor_tensor(
                        out=acc[:, t, :], in0=bank[4 + 2 * (e % 2) + t // 2][:, (t % 2) * D:(t % 2 + 1) * D],
                        scalar=gates[:, t, e:e + 1], in1=acc[:, t, :], op0=ALU.mult, op1=ALU.add)
                ins.then_inc(s_acc, 1)

        block = ctx.enter_context(nc.Block())

        def proj_order():
            order = []
            for c in range(NC):
                order += [("t", c * KD + kt) for kt in range(KD)]
                if c:
                    order.append(("k", c - 1))
            return order + [("k", NC - 1)] + [("k", NC + c) for c in range(NC)]

        def value_order():
            order, w = [("v", 0), ("o", 0)], 0
            for v in range(1, NV):
                order.append(("v", v))
                while w < min(UG, (UG * v + NV - 3) // (NV - 2)):
                    order.append(("b", w))
                    w += 1
                if v == NV - 2:
                    order.append(("p", 0))
            return order + [("m", 0)]

        def score_order(g, beside):
            order, w = [], 0
            for n in range(UG + 1):
                if n < UG:
                    order.append(("s", g * UG + n))
                while beside and w < min(UG, (4 * n + 6) // 3):
                    order.append(("b", UG + w))
                    w += 1
                if beside and n == UG - 2:
                    order.append(("p", 1))
                if n:
                    order.append(("a", g * UG + n - 1))
            return order + ([("m", 1)] if beside else [])

        def batch_order(first):
            return (proj_order() + ([] if first else score_order(1, False)) + value_order()
                    + score_order(0, True))

        TAIL_ORDER = score_order(1, False) + [("o", 0)]

        def over_batches(eng_type, body):
            body(0, True)
            with nc.Fori(1, NB, engines=(eng_type,)) as i:
                body(i, False)

        @block.sync
        def _(sp):
            sp.dma_start(x_sb[:, :, :], x.rearrange("b s d -> (b s) d").rearrange("(t p) d -> p t d", p=P)
                         ).then_inc(l_x, 16)
            for dst, src in ((wq_sb, Wq), (wk_sb, Wk), (wv_sb, Wv), (wo_sb, Wo)):
                sp.dma_start(dst[:, :, :], src.rearrange("(k p) n -> p k n", p=P)).then_inc(l_w, 16)
            sp.dma_start(bqc[:, :], bq.rearrange("(k p) -> p k", p=P), allow_slow_non_contiguous=True).then_inc(l_w, 16)
            sp.dma_start(bkc[:, :], bk.rearrange("(k p) -> p k", p=P), allow_slow_non_contiguous=True).then_inc(l_w, 16)

            for n, vec in enumerate((bq, bv, bo, g0, b0, g1, b1)):
                sp.dma_start(rows[:, n, :], vec.rearrange("(a n) -> a n", a=1).broadcast_to([P, D])
                             ).then_inc(l_rows, 16)
            sp.dma_start(wqk[:, 0, :], w_q).then_inc(l_small, 16)
            sp.dma_start(wqk[:, 1, :], w_k).then_inc(l_small, 16)
            sp.dma_start(bqk[:, 0:1], b_q.rearrange("(p a) -> p a", a=1), allow_slow_non_contiguous=True).then_inc(l_small, 16)
            sp.dma_start(bqk[:, 1:2], b_k.rearrange("(p a) -> p a", a=1), allow_slow_non_contiguous=True).then_inc(l_small, 16)
            sp.dma_start(wr_sb[:, :, :], Wr.rearrange("(k p) e -> p k e", p=P)).then_inc(l_small, 16)
            sp.dma_start(br_row[:, :], br.rearrange("(a n) -> a n", a=1).broadcast_to([P, E_])).then_inc(l_small, 16)
            sp.dma_start(b1_rows[:, :], fb1.rearrange("e (f p) -> (e f) p", p=P)).then_inc(l_small, 16)
            sp.dma_start(b2_sb[:, :], fb2).then_inc(l_small, 16)
            sp.wait_ge(s_qparts, 3)
            for n in range(3):
                sp.dma_start(q_scr[n].rearrange("(k p) t -> p k t", p=P), qp[n][:, :, :]).then_inc(l_qw, 16)
            sp.wait_ge(l_qw, 48)
            for slot, part in enumerate((0, 1, 2, 0, 1, 0)):
                sp.dma_start(qst[slot * DH:(slot + 1) * DH, :, :],
                             q_scr[part].rearrange("(h d) t -> d h t", d=DH)).then_inc(l_qst, 16)

            def body(i, first):
                for g in range(2):
                    if g:
                        sp.wait_ge(s_k3, i * NKP + 2 * NC)
                    if not first:
                        sp.wait_ge(l_kst[g], i * 96)
                    if not g:
                        sp.wait_ge(s_k3, i * NKP + NC)
                    for n in range(3):
                        sp.dma_start(k_scr[n, g * P:(g + 1) * P, :], kp[n][:, g, :]).then_inc(l_kw[g], 16)
                for g in range(2):
                    if not first:
                        sp.wait_ge(s_pv, i * UB - (1 - g) * UG)
                    sp.wait_ge(l_kw[g], i * 48 + 48)
                    for slot, part in enumerate((0, 0, 0, 1, 1, 2)):
                        sp.dma_start(kst[slot * DH:(slot + 1) * DH, g * HG:(g + 1) * HG, :],
                                     k_scr[part, g * P:(g + 1) * P, :].rearrange("(h d) n -> d h n", d=DH)
                                     ).then_inc(l_kst[g], 16)

            over_batches(ET.SP, body)

            sp.wait_ge(s_oev, NB)
            for half in range(2):
                sp.dma_start(o_sb[half * SQ:(half + 1) * SQ, :, :], oall[:, half:NB:2, :]).then_inc(l_xa, 16)
            tail_loads(sp)

        @block.gpsimd
        def _(pool):
            pool.memset(half[:, :], -0.5).then_inc(s_half, 1)
            pool.memset(ident[:, :], 0.0).then_inc(s_const, 1)
            pool.memset(identb[:, :], 0.0).then_inc(s_const, 1)
            pool.wait_ge(s_const, 2)
            for m in (ident, identb):
                pool.affine_select(out=m[:, :], in_=m[:, :], compare_op=ALU.not_equal, fill=1.0, base=0,
                                   pattern=[[-1, P]], channel_multiplier=1).then_inc(s_const, 1)
            pool.wait_ge(s_half, 1)
            pool_pow(pool, 1)
            pool.wait_ge(s_pow, 1)
            pool.memset(kst[QR:KR, :, :], 1.0).then_inc(s_ones, 1)
            pool.wait_ge(s_ones, 1)
            pool.memset(vaug[:, :, :, DH:VW], 1.0).then_inc(s_ones, 1)
            pool.memset(osb[:, :], 0.0).then_inc(s_ones, 1)

            def body(i, first):
                if not first:
                    pool.wait_ge(s_qb, i)
                for k in range(NKP):
                    g, c = divmod(k, NC)
                    pool.wait_ge(s_k2, i * NKP + k + 1)
                    if not first and c == 0:
                        pool.wait_ge(l_kw[g], i * 48)
                    w = width(c)
                    pool.tensor_tensor(kp[2][:, g, c * CH * P:c * CH * P + w], res[:, k % RR, 0:w],
                                       kp[1][:, g, c * CH * P:c * CH * P + w], ALU.subtract).then_inc(s_k3, 1)
                if first:
                    pool.wait_ge(l_qst, 96)
                else:
                    pool.wait_ge(s_pv, i * UB)
                pool.wait_ge(s_k3, i * NKP + NKP)
                pool.tensor_copy(qb[0:QR, :, :], qst[:, :, bass.ds(i * SQ, SQ)]).then_inc(s_qb, 1)

            over_batches(ET.Pool, body)
            tail_pool(pool)

        @block.scalar
        def _(act):
            def load_ctx(b, c):
                full = min(CH, (SK - c * CH * P) // P)
                if full:
                    rows_ = ctx_in[bass.ds(b, 1), c * CH * P:(c * CH + full) * P, :]
                    act.dma_start(cx[:, c * CH:c * CH + full, :],
                                 rows_.rearrange("a (t p) d -> p (a t) d", p=P)).then_inc(l_ctx[c], 16)
                else:
                    act.dma_start(cx[0:KL, KT - 1:KT, :],
                                 ctx_in[bass.ds(b, 1), (KT - 1) * P:SK, :].rearrange("a p d -> p a d")
                                 ).then_inc(l_ctx[c], 16)

            for c in range(NC):
                load_ctx(0, c)
            for n in range(2):
                act.wait_ge(s_xtr, n + 1)
                act.activation(xnT[:, n, :], bank[n][:, :], ACT.Copy).then_inc(s_xT, 1)
            for n in range(2):
                act.wait_ge(s_wtr, n + 1)
                act.activation(wkT[:, n, :], bank[2 + n][:, 0:D], ACT.Copy).then_inc(s_wT, 1)
            act.wait_ge(s_bqs, 1)
            for m in range(KD):
                act.wait_ge(s_qps, m + 1)
                act.activation(qf[:, m, :], bank[4 + m][:, :], ACT.Identity, bias=bqs[:, m:m + 1],
                               scale=DH ** -0.5).then_inc(s_qf, 1)
            act.wait_ge(s_wkvp, 1)
            act.activation(wkv[:, :, :], bank[6][:, :].rearrange("p (k n) -> p k n", k=KD), ACT.Copy
                           ).then_inc(s_wkv, 1)

            def body(i, first, order, more):
                for kind, n in order:
                    if kind == "t":
                        c, kt = divmod(n, KD)
                        act.wait_ge(s_tr, i * NTR + n + 1)
                        if n == 0 and not first:
                            act.wait_ge(s_v, i * NV)
                        w = width(c)
                        act.activation(cxT[:, kt, c * CH * P:c * CH * P + w], bkT[n % 2][:, 0:w], ACT.Copy
                                       ).then_inc(s_ctxT, 1)
                        if kt == KD - 1 and more:
                            load_ctx(i + 1, c)
                    elif kind == "k":
                        g, c = divmod(n, NC)
                        act.wait_ge(s_kproj, i * NKP + n + 1)
                        if c == 0 and not first:
                            act.wait_ge(l_kw[g], i * 48)
                        w = width(c)
                        act.activation(kp[0][:, g, c * CH * P:c * CH * P + w], bkX[n % 2][:, 0:w],
                                       ACT.Identity, bias=bkc[:, g:g + 1]).then_inc(s_k1, 1)
                    elif kind == "m":
                        act.wait_ge(s_mtr, 2 * i + n + 1)
                        act.activation(qb[QR:KR, n * HG:(n + 1) * HG, :],
                                       bank[0][:, 0:HG * SQ // 2].bitcast(BF16)[0:3, :]
                                       .rearrange("p (h q) -> p h q", q=SQ), ACT.Copy).then_inc(s_mrow, 1)
                    elif kind == "s":
                        b = i if n < UG else i - 1
                        c = n % NC
                        act.wait_ge(s_st, b * UB + n + 1)
                        if not (first and n < RP):
                            act.wait_ge(s_pv, b * UB + n - RP + 1)
                        rows_, w = (P, CH * P) if c < NC - 1 or KL == P else (KL, P)
                        act.activation(prob[0:rows_, n % RP, 0:w], bkS[n % 2][0:rows_, 0:w], ACT.Exp
                                       ).then_inc(s_exp, 1)
                    if kind == "s" and n == UB - 1:
                        act.wait_ge(s_pv, i * UB)
                        for half in range(2):
                            r = 64 * half
                            act.activation(osb[r:r + 2 * VW, :], bkO[r:r + 2 * VW, :], ACT.Copy
                                           ).then_inc(s_ocp, 1)

            act.wait_ge(s_ones, 3)
            body(0, True, batch_order(True), True)
            with nc.Fori(1, NB - 1, engines=(ET.Activation,)) as i:
                body(i, False, batch_order(False), True)
            body(NB - 1, False, batch_order(False), False)
            body(NB, False, TAIL_ORDER, False)
            tail_act(act)

        @block.tensor
        def _(pe):
            pe.wait_ge(s_const, 4)
            pe.wait_ge(s_ones, 3)
            pe.wait_ge(s_xn, NT)
            for k in range(KD):
                for t in range(NT):
                    mm = pe.transpose(bank[k][:, t * P:(t + 1) * P], xn[:, t, k * P:(k + 1) * P], ident[:, :])
                mm.then_inc(s_xtr, 1)
            pe.wait_ge(l_w, 96)
            for k in range(KD):
                for t in range(KD):
                    mm = pe.transpose(bank[2 + k][:, t * P:(t + 1) * P], wk_sb[:, t, k * P:(k + 1) * P], ident[:, :])
                mm.then_inc(s_wtr, 1)
            pe.wait_ge(s_xT, 2)
            for m in range(KD):
                for k in range(KD):
                    mm = pe.matmul(bank[4 + m][:, :], wq_sb[:, k, m * P:(m + 1) * P], xnT[:, k, :],
                                   start=(k == 0), stop=(k == KD - 1))
                mm.then_inc(s_qps, 1)
            pe.wait_ge(s_wT, 2)
            for m in range(KD):
                for k in range(KD):
                    mm = pe.matmul(bank[6][:, m * D:(m + 1) * D], wkT[:, k, m * P:(m + 1) * P], wv_sb[:, k, :],
                                   start=(k == 0 and m == 0), stop=(k == KD - 1), skip_group_check=True)
            mm.then_inc(s_wkvp, 1)
            for t in range(NT):
                for k in range(KD):
                    mm = pe.matmul(bank[t // 2][:, (t % 2) * D:(t % 2 + 1) * D], xnT[:, k, t * P:(t + 1) * P],
                                   wq_sb[:, k, :], start=(k == 0 and t % 2 == 0), stop=(k == KD - 1),
                                   skip_group_check=True)
                if t % 2:
                    mm.then_inc(s_qtp, 1)
            for k in range(KD):
                mm = pe.matmul(bank[7][:, 0:D], bkc[:, k:k + 1].broadcast_to([P, P]), wv_sb[:, k, :],
                               start=(k == 0), stop=(k == KD - 1))
            mm.then_inc(s_qtp, 1)
            pe.wait_ge(s_wkv, 1)
            pe.wait_ge(s_qf, 2)
            pe.wait_ge(s_qt, 3)

            def body(i, first, order):
                for kind, n in order:
                    if kind == "t":
                        c, kt = divmod(n, KD)
                        if kt == 0:
                            pe.wait_ge(l_ctx[c], i * 16 + 16)
                        if n >= 2:
                            pe.wait_ge(s_ctxT, i * NTR + n - 1)
                        elif not first:
                            if n == 0:
                                pe.wait_ge(s_mrow, 2 * i)
                            else:
                                pe.wait_ge(s_vev, i * NV)
                        for t in range(c * CH, min(KT, (c + 1) * CH)):
                            mm = pe.transpose(bkT[n % 2][:, (t % CH) * P:(t % CH) * P + keys(t)],
                                              cx[0:keys(t), t, kt * P:(kt + 1) * P],
                                              ident[0:keys(t), 0:keys(t)])
                        mm.then_inc(s_tr, 1)
                    elif kind == "k":
                        g, c = divmod(n, NC)
                        pe.wait_ge(s_ctxT, i * NTR + min(NTR, KD * (c + 1)))
                        if n >= 2:
                            pe.wait_ge(s_res, i * NKP + n - 1)
                        elif not first:
                            pe.wait_ge(s_mx, i * UB)
                        w = width(c)
                        for k in range(KD):
                            mm = pe.matmul(bkX[n % 2][:, 0:w], wk_sb[:, k, g * P:(g + 1) * P],
                                           cxT[:, k, c * CH * P:c * CH * P + w],
                                           start=(k == 0), stop=(k == KD - 1))
                        mm.then_inc(s_kproj, 1)
                    elif kind == "v":
                        if n >= 2:
                            pe.wait_ge(s_vev, i * NV + n - 1)
                        elif n == 0 and not first:
                            pe.wait_ge(s_vev, i * NV)
                        elif n == 1:
                            pe.wait_ge(s_ctxT, i * NTR + NTR)
                        tiles = range(2 * n, min(KT, 2 * n + 2))
                        for t in tiles:
                            for k in range(KD):
                                mm = pe.matmul(bkV[n % 2][0:keys(t), (t % 2) * D:(t % 2 + 1) * D],
                                               cxT[:, k, t * P:t * P + keys(t)], wkv[:, k, :],
                                               start=(k == 0 and t % 2 == 0), stop=(k == KD - 1),
                                               skip_group_check=True)
                        mm.then_inc(s_v, 1)
                    elif kind == "b":
                        g, u = divmod(n, UG)
                        j, c = divmod(u, NC)
                        if u == 0:
                            pe.wait_ge(l_kst[g], i * 96 + 96)
                            pe.wait_ge(s_qb, i + 1)
                        if n >= 2:
                            pe.wait_ge(s_mx, i * UB + n - 1)
                        else:
                            pe.wait_ge(s_res, i * NKP + NKP - 1 + n)
                        w = width(c)
                        for e in range(2):
                            h = g * HG + 2 * j + e
                            mm = pe.matmul(bkX[n % 2][64 * e:64 * e + SQ, 0:w], qb[0:QR, h, :],
                                           kst[0:QR, h, c * CH * P:c * CH * P + w], start=True, stop=True)
                        mm.then_inc(s_ms, 1)
                    elif kind == "m":
                        pe.wait_ge(s_mp, 2 * i + n + 1)
                        if n == 0:
                            pe.wait_ge(s_ctxT, i * NTR + NTR)
                            if not first:
                                pe.wait_ge(s_oev, i)
                        else:
                            pe.wait_ge(s_mrow, 2 * i + 1)
                        for j in range(NPJ):
                            mm = pe.transpose(bank[0][:, 0:HG * SQ // 2].bitcast(BF16)[0:3, j * P:(j + 1) * P],
                                              mpt[:, j, 0:3], identb[:, :])
                        mm.then_inc(s_mtr, 1)
                    elif kind == "s":
                        b = i if n < UG else i - 1
                        g, u = divmod(n, UG)
                        j, c = divmod(u, NC)
                        if u == 0:
                            pe.wait_ge(s_mrow, 2 * b + g + 1)
                        if not (first and n < 2):
                            pe.wait_ge(s_exp, b * UB + n - 1)
                        for t in range(c * CH, min(KT, (c + 1) * CH)):
                            for e in range(2):
                                h = g * HG + 2 * j + e
                                at = (t % CH) * P + e * SQ
                                mm = pe.matmul(bkS[n % 2][0:keys(t), at:at + SQ],
                                               kst[0:KR, h, t * P:t * P + keys(t)], qb[0:KR, h, :],
                                               start=True, stop=True)
                        mm.then_inc(s_st, 1)
                    elif kind == "a":
                        b = i if n < UG else i - 1
                        g, u = divmod(n, UG)
                        j, c = divmod(u, NC)
                        if n == 0:
                            pe.wait_ge(s_vev, i * NV + NV)
                            if not first:
                                pe.wait_ge(s_ocp, 2 * i)
                        pe.wait_ge(s_exp, b * UB + n + 1)
                        jj = g * NPJ + j
                        r = 64 * (jj % 2)
                        for t in range(c * CH, min(KT, (c + 1) * CH)):
                            mm = pe.matmul(bkO[r:r + 2 * VW, (jj // 2) * P:(jj // 2 + 1) * P],
                                           vaug[0:keys(t), t, 2 * jj:2 * jj + 2, :].rearrange("p h v -> p (h v)"),
                                           prob[0:keys(t), n % RP, (t % CH) * P:(t % CH + 1) * P],
                                           start=(t == 0 and jj < 2), stop=(t == KT - 1),
                                           skip_group_check=True)
                        mm.then_inc(s_pv, 1)
                    elif kind == "o" and not first:
                        pe.wait_ge(s_ocp, 2 * i)
                        if order is not TAIL_ORDER:
                            pe.wait_ge(s_ctxT, i * NTR + NTR)
                        else:
                            pe.wait_ge(s_mrow, 2 * i)
                        for blk in range(H // 4):
                            mm = pe.transpose(bank[0][:, blk * P:(blk + 1) * P], osb[:, blk * P:(blk + 1) * P],
                                              ident[:, :])
                        mm.then_inc(s_otr, 1)

            over_batches(ET.PE, lambda i, first: body(i, first, batch_order(first)))
            body(NB, False, TAIL_ORDER)
            tail_pe(pe)

        @block.vector
        def _(dve):
            dve.wait_ge(l_x, 16)
            layernorm(dve, xn, x_sb, s_xn)
            dve.wait_ge(l_w, 96)
            dve.tensor_scalar(bqs[:, :], bqc[:, :], DH ** -0.5, None, ALU.mult).then_inc(s_bqs, 1)
            dve.wait_ge(s_qf, 2)
            link(dve, dve.tensor_copy(qp[0][:, :, :], qf[:, :, :]))
            link(dve, dve.tensor_tensor(qf[:, :, :], qf[:, :, :], qp[0][:, :, :], ALU.subtract))
            link(dve, dve.tensor_copy(qp[1][:, :, :], qf[:, :, :]))
            dve.tensor_tensor(qp[2][:, :, :], qf[:, :, :], qp[1][:, :, :], ALU.subtract).then_inc(s_qparts, 3)
            dve.wait_ge(l_rows, 16 * 7)
            dve.wait_ge(s_qtp, 3)
            dve.tensor_tensor(bkv[:, :], bank[7][:, 0:D], rows[:, 1, :], ALU.add).then_inc(s_qt, 1)
            for n in range(2):
                ins = dve.tensor_tensor(qtok[:, 2 * n:2 * n + 2, :],
                                        bank[n][:, :].rearrange("p (t d) -> p t d", t=2),
                                        rows[:, 0:1, :].broadcast_to([P, 2, D]), ALU.add)
                ins.then_inc(s_qt, 1)
            dve.wait_ge(s_qt, 3)
            link(dve, dve.tensor_tensor(qtok[:, :, :], qtok[:, :, :],
                                        bkv[:, :].unsqueeze(1).broadcast_to([P, NT, D]), ALU.add))

            def body(i, first, order):
                for kind, n in order:
                    if kind == "k":
                        g, c = divmod(n, NC)
                        w = width(c)
                        at = slice(c * CH * P, c * CH * P + w)
                        dve.wait_ge(s_k1, i * NKP + n + 1)
                        if not (first and n < RR):
                            dve.wait_ge(s_k3, i * NKP + n - RR + 1)
                        dve.scalar_tensor_tensor(out=res[:, n % RR, 0:w], in0=bkX[n % 2][:, 0:w],
                                                 scalar=bkc[:, g:g + 1], in1=kp[0][:, g, at],
                                                 op0=ALU.add, op1=ALU.subtract).then_inc(s_res, 1)
                        dve.wait_ge(s_res, i * NKP + n + 1)
                        if c == 0 and not first:
                            dve.wait_ge(l_kw[g], i * 48)
                        dve.tensor_copy(kp[1][:, g, at], res[:, n % RR, 0:w]).then_inc(s_k2, 1)
                    elif kind == "v":
                        dve.wait_ge(s_v, i * NV + n + 1)
                        if n == 0 and not first:
                            dve.wait_ge(s_pv, i * UB)
                        t = 2 * n
                        if t + 1 < KT:
                            two, rows_ = 2, P
                        else:
                            two, rows_ = 1, keys(t)
                        dve.tensor_copy(vaug[0:rows_, t:t + two, :, 0:DH],
                                        bkV[n % 2][0:rows_, 0:two * D].rearrange(
                                            "p (t h d) -> p t h d", t=two, d=DH)).then_inc(s_vev, 1)
                    elif kind == "b":
                        j, c = divmod(n, NC)
                        dve.wait_ge(s_ms, i * UB + n + 1)
                        dve.tensor_reduce(mx[:, j, c:c + 1], bkX[n % 2][:, 0:width(c)], AX.X, ALU.max
                                          ).then_inc(s_mx, 1)
                    elif kind == "p":
                        dve.wait_ge(s_mx, i * UB + (n + 1) * UG)
                        if n or not first:
                            dve.wait_ge(s_mtr, 2 * i + n)
                        m0 = i * 8 + n * 4
                        dve.tensor_reduce(nm[:, :], mx[:, n * NPJ:(n + 1) * NPJ, :], AX.X, ALU.max, negate=True
                                          ).then_inc(s_mstep, 1)
                        dve.wait_ge(s_mstep, m0 + 1)
                        dve.tensor_copy(mpt[:, :, 0], nm[:, :]).then_inc(s_mstep, 1)
                        dve.wait_ge(s_mstep, m0 + 2)
                        dve.tensor_tensor(nr[:, :], nm[:, :], mpt[:, :, 0], ALU.subtract).then_inc(s_mstep, 1)
                        dve.wait_ge(s_mstep, m0 + 3)
                        dve.tensor_copy(mpt[:, :, 1], nr[:, :]).then_inc(s_mstep, 1)
                        dve.wait_ge(s_mstep, m0 + 4)
                        dve.tensor_tensor(mpt[:, :, 2], nr[:, :], mpt[:, :, 1], ALU.subtract).then_inc(s_mp, 1)
                    elif kind == "o" and not first:
                        dve.wait_ge(s_otr, i)
                        got = [bank[0][e * SQ:(e + 1) * SQ, :].rearrange("q (k j r) -> q k j r", k=H // 4, j=2)
                               for e in range(2)]
                        for e in range(2):
                            dve.reciprocal(rec[e * SQ:(e + 1) * SQ, :, :], got[e][:, :, :, e * VW + DH]
                                           ).then_inc(s_rec, 1)
                        dve.wait_ge(s_rec, 2 * i)
                        heads = oall[:, bass.ds(i - 1, 1), :].rearrange("q a (k j e d) -> q (a k) j e d", k=H // 4,
                                                                        j=2, e=2)
                        for e in range(2):
                            mul = dve.tensor_tensor(
                                heads[:, :, :, e, :], got[e][:, :, :, e * VW:e * VW + DH],
                                rec[e * SQ:(e + 1) * SQ, :, :].unsqueeze(3).broadcast_to([SQ, H // 4, 2, DH]),
                                ALU.mult)
                        mul.then_inc(s_oev, 1)

            dve.wait_ge(s_ones, 3)
            over_batches(ET.DVE, lambda i, first: body(i, first, batch_order(first)))
            body(NB, False, TAIL_ORDER)
            tail_dve(dve)


_INS = ["x", "ctx_1024", "L0_xattn_Wq", "L0_xattn_bq", "L0_xattn_Wk", "L0_xattn_bk", "L0_xattn_Wv", "L0_xattn_bv",
        "L0_xattn_Wo", "L0_xattn_bo", "L0_xattn_g0", "L0_xattn_b0", "L0_xattn_g1", "L0_xattn_b1",
        "L0_attn_w_q", "L0_attn_b_q", "L0_attn_w_k", "L0_attn_b_k",
        "L0_ffn_W1", "L0_ffn_b1", "L0_ffn_W2", "L0_ffn_b2", "L0_ffn_Wr", "L0_ffn_br"]


def kernel(**inputs):
    import numpy as _np
    import concourse.bacc as _bacc
    from concourse import mybir as _mybir
    from concourse.bass_utils import run_bass_kernel_spmd as _run

    nc = _bacc.Bacc("TRN2", target_bir_lowering=False, num_devices=1)
    arrays, args = {}, []
    for name in _INS:
        a = _np.ascontiguousarray(inputs[name])
        arrays[f"in_{name}"] = a
        args.append(nc.dram_tensor(f"in_{name}", a.shape, _mybir.dt.from_np(a.dtype), kind="ExternalInput").ap())
    shape = inputs["x"].shape
    args.append(nc.dram_tensor("out_0", shape, _mybir.dt.float32, kind="ExternalOutput").ap())
    perceiver_kernel(nc, *args)
    r = _run(nc, [arrays], core_ids=[0])
    return r.results[0]["out_0"]
```

```python
from contextlib import ExitStack

import concourse.bass as bass
from concourse import mybir

F32 = mybir.dt.float32
BF16 = mybir.dt.bfloat16
ALU = mybir.AluOpType
ACT = mybir.ActivationFunctionType
AX = mybir.AxisListType
ET = mybir.EngineType
EPS = 1e-5


def perceiver_kernel(nc, x, ctx_in, Wq, bq, Wk, bk, Wv, bv, Wo, bo, g0, b0, g1, b1,
                     w_q, b_q, w_k, b_k, W1, fb1, W2, fb2, Wr, br, out):
    NB, SQ, D = x.shape
    SK = ctx_in.shape[1]
    H, DH = 16, D // 16
    P = 128
    KD = D // P
    NT = NB * SQ // P
    T = NB * SQ
    KT = -(-SK // P)
    KL = SK - (KT - 1) * P
    CH = 4
    NC = -(-KT // CH)
    HG = H // 2
    NPJ = HG // 2
    FC = NC - 1
    UG = NPJ * FC + 1
    UB = 2 * UG
    NV = -(-KT // 2)
    NTR = KD * NC
    NKP = 2 * NC
    QR = 6 * DH
    KR = QR + 3
    VW = DH + 1
    RP = 4
    assert KT == FC * CH + 1 and NPJ * P <= 512
    RR = 4
    E_, F_ = W1.shape[0], W1.shape[2]
    FT = F_ // P
    QD = w_q.shape[0]
    NS = NT + E_ - 1
    assert NS % 2 == 1

    def width(c):
        return min(CH * P, SK - c * CH * P)

    def keys(t):
        return min(P, SK - t * P)

    def unit(u):
        if u < UG - 1:
            j, c = divmod(u, FC)
            return [(j, c * CH + t, t) for t in range(CH)]
        return [(j, KT - 1, j) for j in range(NPJ)]

    def ring_free(n, b, first):
        if n >= RP:
            return b * UB + n - RP + 1
        if first:
            return None
        return (b - 1) * UB + max(m for m in range(UB) if m % RP == n) + 1

    ctx = ExitStack()
    with ctx:
        def sb(name, shape, dt=F32):
            return ctx.enter_context(nc.sbuf_tensor(name, shape, dt))

        def sem(name):
            return ctx.enter_context(nc.semaphore(name))

        bank = [ctx.enter_context(nc.psum_tensor(f"bank{n}", [P, 512], F32)) for n in range(8)]
        bkT = [bank[0], bank[1]]
        bkV = [bank[2], bank[1]]
        bkX = [bank[3], bank[4]]
        bkS = [bank[5], bank[6]]
        bkK = [bank[5], bank[6], bank[3], bank[4]]
        bkH = [bank[2], bank[3], bank[6], bank[7]]
        bkO = bank[7]

        q_scr = nc.dram_tensor("q_parts", [3, D, T], BF16, kind="Internal").ap()
        k_scr = nc.dram_tensor("k_parts", [3, D, SK], BF16, kind="Internal").ap()

        x_scr = nc.dram_tensor("x_slots", [NS * P, D], F32, kind="Internal").ap()
        y_scr = nc.dram_tensor("y_slots", [NS * P, D], F32, kind="Internal").ap()

        ident = sb("ident", [P, P])
        identb = sb("identb", [P, P], BF16)
        wq_sb = sb("wq_sb", [P, KD, D])
        wk_sb = sb("wk_sb", [P, KD, D])
        wv_sb = sb("wv_sb", [P, KD, D])
        wo_sb = sb("wo_sb", [P, KD, D])
        wkv = sb("wkv", [P, KD, D])
        bqc = sb("bqc", [P, KD])
        bqs = sb("bqs", [P, KD])
        bkc = sb("bkc", [P, KD])
        rows = sb("rows", [P, 7, D])
        bkv = sb("bkv", [P, D])
        x_sb = sb("x_sb", [P, NT, D])
        xn = sb("xn", [P, NT, D])
        xnT = sb("xnT", [P, KD, T])
        qtok = sb("qtok", [P, NT, D])
        st = sb("st", [P, NT, 6])
        mv = sb("mv", [P, NT, 2])
        rstd = sb("rstd", [P, NT])
        ve = sb("ve", [P, NT])
        nwt = sb("nwt", [P, NT])
        half = sb("half", [P, NT])
        oall = sb("oall", [SQ, NB, D])
        wqk = sb("wqk", [QD, 2, D])
        wqkT = sb("wqkT", [P, 2, KD, QD])
        bqk = sb("bqk", [QD, 2])
        wr_sb = sb("wr_sb", [P, KD, E_])
        br_row = sb("br_row", [P, E_])
        b1_rows = sb("b1_rows", [E_ * FT, P])
        b1c = sb("b1c", [P, E_ * FT])
        b2_sb = sb("b2_sb", [E_, D])
        iota = sb("iota", [P, NS])
        iota8 = iota[:, 0:E_]
        before = sb("before", [P, P])
        all1 = sb("all1", [P, P])
        lower = sb("lower", [P, E_, E_])
        zero = sb("zero", [P, D])
        attn = ExitStack()
        def ab(name, shape, dt=F32):
            return attn.enter_context(nc.sbuf_tensor(name, shape, dt))
        cx = ab("cx", [P, KT, D])
        cxT = ab("cxT", [P, KD, SK])
        kp = [ab(f"kp{n}", [P, KD, SK], BF16) for n in range(3)]
        res = ab("res", [P, RR, CH * P])
        kst = ab("kst", [KR, H, SK], BF16)
        qst = ab("qst", [QR, H, T], BF16)
        qb = ab("qb", [KR, H, SQ], BF16)
        vaug = ab("vaug", [P, KT, H, VW])
        osb = ab("osb", [P, H // 4 * P])
        setup = ExitStack()

        def setup_sb(name, shape, dt=F32):
            return setup.enter_context(nc.sbuf_tensor(name, shape, dt))

        wkT = setup_sb("wkT", [P, KD, D])
        qf = setup_sb("qf", [P, KD, T])
        qp = [setup_sb(f"qp{n}", [P, KD, T], BF16) for n in range(3)]
        setup.close()
        prob = ab("prob", [P, RP, CH * P])
        mx = ab("mx", [P, H // 2, NC])
        nm = ab("nm", [P, NPJ])
        nr = ab("nr", [P, NPJ])
        mpt = ab("mpt", [P, NPJ, 4], BF16)
        rec = ab("rec", [P, H // 4, 2])
        attn.close()
        o_sb = sb("o_sb", [P, NT, D])
        q2T = sb("q2T", [QD, T])
        k2T = sb("k2T", [QD, T])
        sc = sb("sc", [P, NT, SQ])
        s4 = sb("s4", [P, NT])
        r4 = sb("r4", [P, NT])
        pblk = sb("pblk", [P, NT, P])
        pT = sb("pT", [P, NT, P])
        lg = sb("lg", [P, NT, E_])
        ex = sb("ex", [P, NT, E_])
        gates = sb("gates", [P, NT, E_])
        gT = sb("gT", [E_, T])
        acc = sb("acc", [P, NT, D])
        chosen = sb("chosen", [P, NT, E_])
        earlier = sb("earlier", [P, NT + 1, E_])
        ntiles = sb("ntiles", [P, E_])
        scan = sb("scan", [P, E_, E_])
        base = sb("base", [P, E_])
        rank = sb("rank", [P, NT, E_])
        slot_f = sb("slot_f", [P, NT])
        slot = sb("slot", [P, NT], mybir.dt.uint32)
        past = sb("past", [P, NS, E_])
        expert_f = sb("expert_f", [P, NS])
        expert = sb("expert", [P, NS], mybir.dt.int32)
        w1_sb = [sb(f"w1_sb{n}", [P, KD, F_]) for n in range(2)]
        w2_sb = [sb(f"w2_sb{n}", [P, FT, D]) for n in range(2)]
        xg = sb("xg", [P, 2, D])
        xgT = sb("xgT", [P, KD, P])
        h_sb = sb("h_sb", [P, F_])
        hT = sb("hT", [P, FT, P])
        y_sb = sb("y_sb", [P, NS, D])
        yg = sb("yg", [P, NT, D])

        s_const = sem("s_const")
        s_ones = sem("s_ones")
        s_kones = sem("s_kones")
        l_x = sem("l_x")
        l_wk = sem("l_wk")
        l_w = sem("l_w")
        l_rows = sem("l_rows")
        s_chain = sem("s_chain")
        s_var = sem("s_var")
        s_pow = sem("s_pow")
        s_half = sem("s_half")
        s_xn = sem("s_xn")
        s_xtr = sem("s_xtr")
        s_xT = sem("s_xT")
        s_wtr = sem("s_wtr")
        s_wT = sem("s_wT")
        s_wkvp = sem("s_wkvp")
        s_wkv = sem("s_wkv")
        s_bqs = sem("s_bqs")
        s_qps = sem("s_qps")
        s_qf = sem("s_qf")
        s_qtp = sem("s_qtp")
        s_qt = sem("s_qt")
        s_qparts = sem("s_qparts")
        l_qw = sem("l_qw")
        l_qst = sem("l_qst")
        l_ctx = [sem(f"l_ctx{c}") for c in range(NC)]
        s_tr = sem("s_tr")
        s_ctxT = [sem(f"s_ctxT{k}") for k in range(KD)]
        s_kproj = sem("s_kproj")
        s_k1 = sem("s_k1")
        s_res = sem("s_res")
        s_k2 = sem("s_k2")
        s_k3 = sem("s_k3")
        l_kw = [sem(f"l_kw{g}") for g in range(2)]
        l_kst = [sem(f"l_kst{g}") for g in range(2)]
        s_qb = sem("s_qb")
        s_v = sem("s_v")
        s_vev = sem("s_vev")
        s_ms = sem("s_ms")
        s_mx = sem("s_mx")
        s_mp = sem("s_mp")
        s_mstep = sem("s_mstep")
        s_rec = sem("s_rec")
        s_mtr = sem("s_mtr")
        s_mrow = sem("s_mrow")
        s_st = sem("s_st")
        s_exp = sem("s_exp")
        s_pv = sem("s_pv")
        s_ocp = sem("s_ocp")
        s_otr = sem("s_otr")
        s_oev = sem("s_oev")
        l_xa = sem("l_xa")
        l_small = sem("l_small")
        s_iota = sem("s_iota")
        s_pz = sem("s_pz")
        s_smallT = sem("s_smallT")
        s_smallc = sem("s_smallc")
        s_o1 = sem("s_o1")
        s_wo = sem("s_wo")
        s_wob = sem("s_wob")
        s_gelu = sem("s_gelu")
        s_nT = sem("s_nT")
        s_nTc = sem("s_nTc")
        s_xn2 = sem("s_xn2")
        s_qk = sem("s_qk")
        s_qkc = sem("s_qkc")
        s_sc = sem("s_sc")
        s_scc = sem("s_scc")
        s_mask = sem("s_mask")
        s_sub = sem("s_sub")
        s_sexp = sem("s_sexp")
        s_pblk = sem("s_pblk")
        s_pT = sem("s_pT")
        s_pTc = sem("s_pTc")
        s_att = sem("s_att")
        s_xn3 = sem("s_xn3")
        s_lg = sem("s_lg")
        s_lsub = sem("s_lsub")
        s_lexp = sem("s_lexp")
        s_gate = sem("s_gate")
        s_gT = sem("s_gT")
        s_gTc = sem("s_gTc")
        s_b2 = sem("s_b2")
        l_w1 = [sem(f"l_w1_{n}") for n in range(2)]
        l_w2 = [sem(f"l_w2_{n}") for n in range(2)]
        s_zero = sem("s_zero")
        s_route = sem("s_route")
        l_zero = sem("l_zero")
        s_chosen = sem("s_chosen")
        s_rank = sem("s_rank")
        s_slot = sem("s_slot")
        s_expert = sem("s_expert")
        l_slots = sem("l_slots")
        l_xg = [sem(f"l_xg{n}") for n in range(2)]
        s_xg = sem("s_xg")
        s_xgT = sem("s_xgT")
        s_h = sem("s_h")
        s_hc = sem("s_hc")
        s_ht = sem("s_ht")
        s_gelu2 = sem("s_gelu2")
        s_y = sem("s_y")
        s_yc = sem("s_yc")
        l_y = sem("l_y")
        l_yg = sem("l_yg")
        s_acc = sem("s_acc")
        l_out = sem("l_out")

        chain = [0]
        norms = [0]

        def link(dve, ins):
            chain[0] += 1
            ins.then_inc(s_chain, 1)
            dve.wait_ge(s_chain, chain[0])

        def layernorm(dve, dst, src, done=None):
            for t in range(NT):
                ins = dve.bn_stats(st[:, t, :], src[:, t, :])
            link(dve, ins)
            for t in range(NT):
                ins = dve.bn_aggr(mv[:, t, :], st[:, t, :])
            link(dve, ins)
            norms[0] += 1
            dve.tensor_scalar(ve[:, :], mv[:, :, 1], EPS, None, ALU.add).then_inc(s_var, 1)
            dve.wait_ge(s_pow, norms[0])
            link(dve, dve.scalar_tensor_tensor(out=nwt[:, :], in0=rstd[:, :], scalar=-0.5, in1=rstd[:, :],
                                               op0=ALU.mult, op1=ALU.mult))
            link(dve, dve.tensor_tensor(nwt[:, :], nwt[:, :], ve[:, :], ALU.mult))
            link(dve, dve.scalar_tensor_tensor(out=rstd[:, :], in0=nwt[:, :], scalar=1.5, in1=rstd[:, :],
                                               op0=ALU.add, op1=ALU.mult))
            for t in range(NT):
                ins = dve.tensor_scalar(dst[:, t, :], src[:, t, :], mv[:, t, 0:1], rstd[:, t:t + 1],
                                        ALU.subtract, ALU.mult)
                if done is not None:
                    ins.then_inc(done, 1)
            if done is None:
                link(dve, ins)

        def row(n):
            return rows[:, n:n + 1, :].broadcast_to([P, NT, D])

        def pool_pow(pool, n):
            pool.wait_ge(s_var, n)
            pool.tensor_tensor(rstd[:, :], ve[:, :], half[:, :], ALU.pow).then_inc(s_pow, 1)

        def over_tiles(eng_type, step):
            step(0, 0, True)
            with nc.Fori(0, (NS - 3) // 2, engines=(eng_type,)) as i:
                step(2 * i + 1, 1, True)
                step(2 * i + 2, 0, True)
            step(NS - 2, 1, False)
            step(NS - 1, 0, False)

        def tail_loads(sp):
            sp.wait_ge(s_zero, 1)
            sp.dma_start(x_scr.rearrange("(s p) d -> p s d", p=P), zero[:, :].unsqueeze(1).broadcast_to([P, NS, D])
                         ).then_inc(l_zero, 16)

            def load_w1(e, ring):
                sp.dma_start(w1_sb[ring][:, :, :], W1[e].rearrange("a (k p) f -> p (a k) f", p=P)
                             ).then_inc(l_w1[ring], 16)

            def load_w2(e, ring):
                sp.dma_start(w2_sb[ring][:, :, :], W2[e].rearrange("a (f p) d -> p (a f) d", p=P)
                             ).then_inc(l_w2[ring], 16)

            def expert_of(tile):
                return bass.ds(sp.value_load(expert[0:1, bass.ds(tile, 1)], min_val=0, max_val=E_ - 1), 1)

            load_w1(slice(0, 1), 0)
            load_w2(slice(0, 1), 0)
            sp.wait_ge(s_expert, 1)
            e = expert_of(1)
            sp.wait_ge(l_slots, NT * 16)
            for s in range(2):
                sp.dma_start(xg[:, s, :], x_scr[s * P:(s + 1) * P, :]).then_inc(l_xg[s], 16)
            load_w1(e, 1)
            load_w2(e, 1)

            def step(s, ring, more):
                if more:
                    e = expert_of(s + 2)
                    sp.wait_ge(s_xg, s + 1)
                    sp.dma_start(xg[:, ring, :], x_scr[bass.ds((s + 2) * P, P), :]).then_inc(l_xg[ring], 16)
                    sp.wait_ge(s_h, 2 * s + 2)
                    load_w1(e, ring)
                sp.wait_ge(s_y, s + 1)
                if more:
                    load_w2(e, ring)
                sp.wait_ge(s_yc, s + 1)
                sp.dma_start(y_scr[bass.ds(s * P, P), :], y_sb[:, bass.ds(s, 1), :].rearrange("p a d -> p (a d)")
                             ).then_inc(l_y, 16)

            over_tiles(ET.SP, step)
            sp.wait_ge(s_acc, 2)
            sp.dma_start(out.rearrange("b s d -> (b s) d").rearrange("(t p) d -> p t d", p=P), acc[:, :, :]
                         ).then_inc(l_out, 16)
            sp.wait_ge(l_out, 16)

        def tail_pool(pool):
            pool.wait_ge(s_qb, NB)
            pool.memset(pblk[:, :, :], 0.0).then_inc(s_pz, 1)
            pool.memset(zero[:, :], 0.0).then_inc(s_zero, 1)
            for n in range(NS):
                pool.memset(iota[:, n:n + 1], float(n)).then_inc(s_iota, 1)
            pool.memset(all1[:, :], 1.0).then_inc(s_route, 1)
            pool.memset(before[:, :], 1.0).then_inc(s_route, 1)
            pool.memset(lower[:, :, :], 1.0).then_inc(s_route, 1)
            pool.wait_ge(s_route, 3)
            pool.affine_select(out=before[:, :], in_=before[:, :], compare_op=ALU.is_gt, fill=0.0, base=0,
                               pattern=[[1, P]], channel_multiplier=-1).then_inc(s_route, 1)
            pool.affine_select(out=lower[:, :, :], in_=lower[:, :, :], compare_op=ALU.is_gt, fill=0.0, base=0,
                               pattern=[[1, E_], [-1, E_]], channel_multiplier=0).then_inc(s_route, 1)
            pool_pow(pool, 2)
            pool_pow(pool, 3)
            pool_pow(pool, 4)
            pool.wait_ge(s_scc, 1)
            for hb in range(2):
                r = hb * SQ
                pool.affine_select(out=sc[r:r + SQ, :, :], in_=sc[r:r + SQ, :, :], compare_op=ALU.is_ge,
                                   fill=-10000.0, base=0, pattern=[[0, NT], [-1, SQ]],
                                   channel_multiplier=1).then_inc(s_mask, 1)
                pool.wait_ge(s_mask, hb + 1)
            pool_pow(pool, 5)
            pool.wait_ge(l_zero, 16)
            pool.wait_ge(s_xn3, NT)
            pool.wait_ge(s_slot, 1)
            for t in range(NT):
                pool.indirect_dma_start(x_scr[:, :], bass.IndirectOffsetOnAxis(ap=slot[:, t:t + 1], axis=0),
                                        xn[:, t, :], None).then_inc(l_slots, 16)
            pool.wait_ge(l_y, NS * 16)
            for t in range(NT):
                pool.indirect_dma_start(yg[:, t, :], None, y_scr[:, :],
                                        bass.IndirectOffsetOnAxis(ap=slot[:, t:t + 1], axis=0)).then_inc(l_yg, 16)

        def evac_T(act, done):
            for k in range(KD):
                act.wait_ge(s_nT, done + k + 1)
                act.activation(xnT[:, k, :], bank[k][:, :], ACT.Copy).then_inc(s_nTc, 1)

        def tail_act(act):
            act.wait_ge(s_smallT, 1)
            act.activation(wqkT[:, :, :, :].rearrange("p a k q -> p (a k q)"), bank[2][:, 0:2 * KD * QD], ACT.Copy
                           ).then_inc(s_smallc, 1)
            act.activation(b1c[:, :], bank[2][:, P:P + E_ * FT], ACT.Copy).then_inc(s_smallc, 1)
            evac_T(act, 0)
            for n in range(2):
                act.wait_ge(s_wob, n + 1)
                act.activation(o_sb[:, 2 * n:2 * n + 2, :], o_sb[:, 2 * n:2 * n + 2, :], ACT.Gelu
                               ).then_inc(s_gelu, 1)
            evac_T(act, 2)
            act.wait_ge(s_qk, 1)
            act.activation(q2T[:, :], bank[4][0:QD, :], ACT.Identity, bias=bqk[:, 0:1]).then_inc(s_qkc, 1)
            act.wait_ge(s_qk, 2)
            act.activation(k2T[:, :], bank[5][0:QD, :], ACT.Identity, bias=bqk[:, 1:2]).then_inc(s_qkc, 1)
            act.wait_ge(s_sc, 1)
            act.activation(sc[:, :, :].rearrange("p t k -> p (t k)"), bank[6][:, 0:NT * SQ], ACT.Copy,
                           scale=QD ** -0.5).then_inc(s_scc, 1)
            act.wait_ge(s_sub, 1)
            act.activation(sc[:, :, :], sc[:, :, :], ACT.Exp).then_inc(s_sexp, 1)
            act.wait_ge(s_pT, 1)
            act.activation(pT[:, :, :].rearrange("p t k -> p (t k)"), bank[7][:, :], ACT.Copy).then_inc(s_pTc, 1)
            evac_T(act, 4)
            act.wait_ge(s_lsub, 1)
            act.activation(ex[:, :, :], lg[:, :, :], ACT.Exp).then_inc(s_lexp, 1)
            act.wait_ge(s_gT, 1)
            act.activation(gT[:, :], bank[4][0:E_, :], ACT.Copy).then_inc(s_gTc, 1)
            act.wait_ge(s_expert, 1)

            def step(s, ring, more):
                e = act.value_load(expert[0:1, bass.ds(s, 1)], min_val=0, max_val=E_ - 1)
                for f in range(FT):
                    if f % 2 == 0:
                        act.wait_ge(s_ht, s * FT // 2 + f // 2 + 1)
                    act.activation(hT[:, f, :], bkH[f // 2][:, f % 2 * P:(f % 2 + 1) * P], ACT.Gelu,
                                   bias=b1c[:, bass.ds(e * FT + f, 1)]).then_inc(s_gelu2, 1)

            over_tiles(ET.Activation, step)

        def transpose_x(pe, ready, at):
            pe.wait_ge(ready, at)
            for k in range(KD):
                for t in range(NT):
                    mm = pe.transpose(bank[k][:, t * P:(t + 1) * P], xn[:, t, k * P:(k + 1) * P], ident[:, :])
                mm.then_inc(s_nT, 1)

        def tail_pe(pe):
            pe.wait_ge(l_small, 16 * 8)
            for a in range(2):
                for k in range(KD):
                    pe.transpose(bank[2][:, (a * KD + k) * QD:(a * KD + k + 1) * QD],
                                 wqk[:, a, k * P:(k + 1) * P], ident[0:QD, 0:QD])
            pe.transpose(bank[2][:, P:P + E_ * FT], b1_rows[:, :], ident[0:E_ * FT, 0:E_ * FT]
                         ).then_inc(s_smallT, 1)
            transpose_x(pe, s_o1, 1)
            pe.wait_ge(s_smallc, 2)
            pe.wait_ge(s_nTc, 2)
            for t in range(NT):
                for k in range(KD):
                    mm = pe.matmul(bank[2 + t // 2][:, (t % 2) * D:(t % 2 + 1) * D], xnT[:, k, t * P:(t + 1) * P],
                                   wo_sb[:, k, :], start=(k == 0 and t % 2 == 0), stop=(k == KD - 1),
                                   skip_group_check=True)
                if t % 2:
                    mm.then_inc(s_wo, 1)
            transpose_x(pe, s_xn2, NT)
            pe.wait_ge(s_nTc, 4)
            for a in range(2):
                for k in range(KD):
                    mm = pe.matmul(bank[4 + a][0:QD, :], wqkT[:, a, k, :], xnT[:, k, :],
                                   start=(k == 0), stop=(k == KD - 1))
                mm.then_inc(s_qk, 1)
            pe.wait_ge(s_qkc, 2)
            for t in range(NT):
                for half in range(2):
                    tok = slice(t * P + half * SQ, t * P + (half + 1) * SQ)
                    mm = pe.matmul(bank[6][half * SQ:(half + 1) * SQ, t * SQ:(t + 1) * SQ], q2T[:, tok], k2T[:, tok],
                                   start=True, stop=True)
            mm.then_inc(s_sc, 1)
            pe.wait_ge(s_pblk, 1)
            for t in range(NT):
                mm = pe.transpose(bank[7][:, t * P:(t + 1) * P], pblk[:, t, :], ident[:, :])
            mm.then_inc(s_pT, 1)
            pe.wait_ge(s_pTc, 1)
            for t in range(NT):
                mm = pe.matmul(bank[2 + t // 2][:, (t % 2) * D:(t % 2 + 1) * D], pT[:, t, :], xn[:, t, :],
                               start=True, stop=True)
                if t % 2:
                    mm.then_inc(s_att, 1)
            transpose_x(pe, s_xn3, NT)
            pe.wait_ge(s_nTc, 6)
            for t in range(NT):
                for k in range(KD):
                    mm = pe.matmul(bank[5][:, t * E_:(t + 1) * E_], xnT[:, k, t * P:(t + 1) * P], wr_sb[:, k, :],
                                   start=(t == 0 and k == 0), stop=(k == KD - 1), skip_group_check=True)
            mm.then_inc(s_lg, 1)
            pe.wait_ge(s_route, 5)
            pe.wait_ge(s_chosen, 1)
            pe.matmul(bank[6][:, 0:NT * E_], before[:, :], chosen[:, :, :].rearrange("p t e -> p (t e)"),
                      start=True, stop=False, skip_group_check=True)
            pe.matmul(bank[6][:, 0:NT * E_], all1[:, :], earlier[:, 0:NT, :].rearrange("p t e -> p (t e)"),
                      start=False, stop=True, skip_group_check=True)
            pe.matmul(bank[7][:, 0:E_], all1[:, :], earlier[:, NT, :], start=True, stop=True).then_inc(s_rank, 1)
            pe.wait_ge(s_gate, 1)
            for t in range(NT):
                mm = pe.transpose(bank[4][0:E_, t * P:(t + 1) * P], gates[:, t, :], ident[:, :])
            mm.then_inc(s_gT, 1)
            pe.wait_ge(s_gTc, 1)
            for t in range(NT):
                mm = pe.matmul(bank[2 + t // 2][:, (t % 2) * D:(t % 2 + 1) * D], gT[:, t * P:(t + 1) * P], b2_sb[:, :],
                               start=True, stop=True)
            mm.then_inc(s_b2, 1)

            def tokens(s, ring):
                pe.wait_ge(l_xg[ring], 8 * (s - ring) + 16)
                for k in range(KD):
                    mm = pe.transpose(bank[4][:, k * P:(k + 1) * P], xg[:, ring, k * P:(k + 1) * P], ident[:, :])
                mm.then_inc(s_xg, 1)

            def hidden(s, ring):
                pe.wait_ge(l_w1[ring], 8 * (s - ring) + 16)
                pe.wait_ge(s_xgT, s + 1)
                for n in range(2):
                    for k in range(KD):
                        mm = pe.matmul(bank[n][:, :], xgT[:, k, :], w1_sb[ring][:, k, n * 512:(n + 1) * 512],
                                       start=(k == 0), stop=(k == KD - 1))
                    mm.then_inc(s_h, 1)

            def turn(s):
                for f in range(FT):
                    if f % 4 == 0:
                        pe.wait_ge(s_hc, 2 * s + f // 4 + 1)
                    mm = pe.transpose(bkH[f // 2][:, f % 2 * P:(f % 2 + 1) * P], h_sb[:, f * P:(f + 1) * P],
                                      ident[:, :])
                    if f % 2:
                        mm.then_inc(s_ht, 1)

            def result(s, ring):
                pe.wait_ge(l_w2[ring], 8 * (s - ring) + 16)
                for f in range(FT):
                    pe.wait_ge(s_gelu2, s * FT + f + 1)
                    mm = pe.matmul(bank[5][:, 0:D], hT[:, f, :], w2_sb[ring][:, f, :],
                                   start=(f == 0), stop=(f == FT - 1))
                mm.then_inc(s_y, 1)

            pe.wait_ge(s_acc, 1)
            tokens(0, 0)
            hidden(0, 0)

            def step(s, ring, more):
                last = isinstance(s, int) and s == NS - 1
                if not last:
                    tokens(s + 1, 1 - ring)
                turn(s)
                if not last:
                    hidden(s + 1, 1 - ring)
                if not (isinstance(s, int) and s == 0):
                    pe.wait_ge(s_yc, s)
                result(s, ring)

            over_tiles(ET.PE, step)

        def tail_dve(dve):
            dve.wait_ge(l_xa, 32)
            link(dve, dve.tensor_tensor(o_sb[:, :, :], o_sb[:, :, :], qtok[:, :, :], ALU.add))
            layernorm(dve, xn, o_sb)
            link(dve, dve.tensor_tensor(xn[:, :, :], xn[:, :, :], row(3), ALU.mult))
            dve.tensor_tensor(xn[:, :, :], xn[:, :, :], row(4), ALU.add).then_inc(s_o1, 1)
            for n in range(2):
                dve.wait_ge(s_wo, n + 1)
                dve.tensor_tensor(o_sb[:, 2 * n:2 * n + 2, :], bank[2 + n][:, :].rearrange("p (t d) -> p t d", t=2),
                                  rows[:, 2:3, :].broadcast_to([P, 2, D]), ALU.add).then_inc(s_wob, 1)
            dve.wait_ge(s_gelu, 2)
            dve.wait_ge(s_o1, 1)
            link(dve, dve.tensor_tensor(o_sb[:, :, :], o_sb[:, :, :], xn[:, :, :], ALU.add))
            layernorm(dve, xn, o_sb)
            link(dve, dve.tensor_tensor(xn[:, :, :], xn[:, :, :], row(5), ALU.mult))
            link(dve, dve.tensor_tensor(xn[:, :, :], xn[:, :, :], row(6), ALU.add))
            link(dve, dve.tensor_tensor(x_sb[:, :, :], x_sb[:, :, :], xn[:, :, :], ALU.add))
            layernorm(dve, xn, x_sb, s_xn2)
            dve.wait_ge(s_mask, 2)
            link(dve, dve.tensor_reduce(s4[:, :], sc[:, :, :], AX.X, ALU.max))
            dve.tensor_tensor(sc[:, :, :], sc[:, :, :], s4[:, :].unsqueeze(2).broadcast_to([P, NT, SQ]),
                              ALU.subtract).then_inc(s_sub, 1)
            dve.wait_ge(s_sexp, 1)
            link(dve, dve.tensor_reduce(s4[:, :], sc[:, :, :], AX.X, ALU.add))
            link(dve, dve.reciprocal(r4[:, :], s4[:, :]))
            dve.wait_ge(s_pz, 1)
            for half in range(2):
                r = slice(half * SQ, (half + 1) * SQ)
                ins = dve.tensor_tensor(pblk[r, :, r], sc[r, :, :],
                                        r4[r, :].unsqueeze(2).broadcast_to([SQ, NT, SQ]), ALU.mult)
            ins.then_inc(s_pblk, 1)
            dve.wait_ge(s_xn2, NT)
            for n in range(2):
                dve.wait_ge(s_att, n + 1)
                ins = dve.tensor_tensor(x_sb[:, 2 * n:2 * n + 2, :], bank[2 + n][:, :].rearrange(
                    "p (t d) -> p t d", t=2), x_sb[:, 2 * n:2 * n + 2, :], ALU.add)
            link(dve, ins)
            layernorm(dve, xn, x_sb, s_xn3)
            dve.wait_ge(s_lg, 1)
            dve.wait_ge(s_iota, NS)
            link(dve, dve.tensor_tensor(lg[:, :, :], bank[5][:, 0:NT * E_].rearrange("p (t e) -> p t e", e=E_),
                                        br_row[:, :].unsqueeze(1).broadcast_to([P, NT, E_]), ALU.add))
            link(dve, dve.tensor_reduce(s4[:, :], lg[:, :, :], AX.X, ALU.max))
            wide = [P, NT, E_]
            dve.tensor_tensor(lg[:, :, :], lg[:, :, :], s4[:, :].unsqueeze(2).broadcast_to(wide),
                              ALU.subtract).then_inc(s_lsub, 1)
            dve.wait_ge(s_lsub, 1)
            link(dve, dve.tensor_scalar(gates[:, :, :], lg[:, :, :], 0.0, -float(E_), ALU.is_ge, ALU.mult))
            link(dve, dve.tensor_tensor(gates[:, :, :], gates[:, :, :],
                                        iota8[:, :].unsqueeze(1).broadcast_to(wide), ALU.add))
            link(dve, dve.tensor_reduce(s4[:, :], gates[:, :, :], AX.X, ALU.min))
            link(dve, dve.tensor_tensor(chosen[:, :, :], gates[:, :, :],
                                        s4[:, :].unsqueeze(2).broadcast_to(wide), ALU.is_equal))
            link(dve, dve.memset(earlier[:, 0, :], 0.0))
            for t in range(NT):
                ins = dve.tensor_tensor(earlier[:, t + 1, :], earlier[:, t, :], chosen[:, t, :], ALU.add)
                if t < NT - 1:
                    link(dve, ins)
            ins.then_inc(s_chosen, 1)
            dve.wait_ge(s_lexp, 1)
            link(dve, dve.tensor_reduce(s4[:, :], ex[:, :, :], AX.X, ALU.add))
            link(dve, dve.reciprocal(r4[:, :], s4[:, :]))
            dve.tensor_tensor(gates[:, :, :], chosen[:, :, :], r4[:, :].unsqueeze(2).broadcast_to(wide),
                              ALU.mult).then_inc(s_gate, 1)
            dve.wait_ge(s_rank, 1)
            dve.wait_ge(s_route, 5)
            count = bank[7][:, 0:E_]
            link(dve, dve.tensor_scalar(ntiles[:, :], count, float(P), 1.0, ALU.is_gt, ALU.add))
            for n in range(2, NT):
                link(dve, dve.scalar_tensor_tensor(out=ntiles[:, :], in0=count, scalar=float(n * P),
                                                   in1=ntiles[:, :], op0=ALU.is_gt, op1=ALU.add))
            link(dve, dve.tensor_tensor(scan[:, :, :], lower[:, :, :],
                                        ntiles[:, :].unsqueeze(1).broadcast_to([P, E_, E_]), ALU.mult))
            link(dve, dve.tensor_reduce(base[:, :], scan[:, :, :], AX.X, ALU.add))
            link(dve, dve.scalar_tensor_tensor(
                out=rank[:, :, :], in0=base[:, :].unsqueeze(1).broadcast_to(wide), scalar=float(P),
                in1=bank[6][:, 0:NT * E_].rearrange("p (t e) -> p t e", e=E_), op0=ALU.mult, op1=ALU.add))
            link(dve, dve.tensor_tensor(rank[:, :, :], rank[:, :, :], chosen[:, :, :], ALU.mult))
            link(dve, dve.tensor_reduce(slot_f[:, :], rank[:, :, :], AX.X, ALU.add))
            dve.tensor_copy(slot[:, :], slot_f[:, :]).then_inc(s_slot, 1)
            link(dve, dve.tensor_tensor(ntiles[:, :], ntiles[:, :], base[:, :], ALU.add))
            link(dve, dve.tensor_tensor(past[:, :, :], iota[:, :].unsqueeze(2).broadcast_to([P, NS, E_]),
                                        ntiles[:, :].unsqueeze(1).broadcast_to([P, NS, E_]), ALU.is_ge))
            link(dve, dve.tensor_reduce(expert_f[:, :], past[:, :, :], AX.X, ALU.add))
            dve.tensor_scalar(expert[:, :], expert_f[:, :], float(E_ - 1), None, ALU.min).then_inc(s_expert, 1)
            dve.wait_ge(s_b2, 1)
            for n in range(2):
                ins = dve.tensor_tensor(acc[:, 2 * n:2 * n + 2, :], bank[2 + n][:, :].rearrange(
                    "p (t d) -> p t d", t=2), x_sb[:, 2 * n:2 * n + 2, :], ALU.add)
            ins.then_inc(s_acc, 1)

            def tokens(s):
                dve.wait_ge(s_xg, s + 1)
                dve.tensor_copy(xgT[:, :, :].rearrange("p k t -> p (k t)"), bank[4][:, 0:D]).then_inc(s_xgT, 1)

            def hidden(s):
                for n in range(2):
                    dve.wait_ge(s_h, 2 * s + n + 1)
                    dve.tensor_copy(h_sb[:, n * 512:(n + 1) * 512], bank[n][:, :]).then_inc(s_hc, 1)

            tokens(0)
            hidden(0)

            def step(s, ring, more):
                if not (isinstance(s, int) and s == NS - 1):
                    tokens(s + 1)
                    hidden(s + 1)
                dve.wait_ge(s_y, s + 1)
                dve.tensor_copy(y_sb[:, bass.ds(s, 1), :].rearrange("p a d -> p (a d)"), bank[5][:, 0:D]
                                ).then_inc(s_yc, 1)

            over_tiles(ET.DVE, step)
            dve.wait_ge(s_acc, 1)
            dve.wait_ge(l_yg, NT * 16)
            for t in range(NT):
                ins = dve.scalar_tensor_tensor(out=acc[:, t, :], in0=yg[:, t, :], scalar=r4[:, t:t + 1],
                                               in1=acc[:, t, :], op0=ALU.mult, op1=ALU.add)
            ins.then_inc(s_acc, 1)

        block = ctx.enter_context(nc.Block())

        def proj_order():
            order = []
            for c in range(NC):
                order += [("t", c * KD + kt) for kt in range(KD)]
                if c:
                    order.append(("k", c - 1))
            return order + [("k", NC - 1)] + [("k", NC + c) for c in range(NC)]

        def value_order():
            order, w = [("v", 0), ("o", 0)], 0
            for t in range(1, KT):
                order.append(("v", t))
                while w < min(UG, (UG * t + KT - 5) // (KT - 4)):
                    order.append(("b", w))
                    w += 1
                if t == KT - 3:
                    order.append(("p", 0))
            return order + [("m", 0)]

        def score_order(g, beside):
            order, w = [], 0
            for n in range(UG + 2):
                if n < UG:
                    order.append(("s", g * UG + n))
                while beside and w < min(UG, (4 * n + 6) // 3):
                    order.append(("b", UG + w))
                    w += 1
                if beside and n == UG - 2:
                    order.append(("p", 1))
                if n >= 2:
                    order.append(("a", g * UG + n - 2))
            return order + ([("m", 1)] if beside else [])

        def batch_order(first):
            return ([] if first else proj_order() + score_order(1, False)) + value_order() + score_order(0, True)

        TAIL_ORDER = score_order(1, False) + [("o", 0)]

        def over_batches(eng_type, body):
            body(0, True)
            with nc.Fori(1, NB, engines=(eng_type,)) as i:
                body(i, False)

        @block.sync
        def _(sp):
            sp.dma_start(wk_sb[:, :, :], Wk.rearrange("(k p) n -> p k n", p=P)).then_inc(l_wk, 16)
            sp.dma_start(bkc[:, :], bk.rearrange("(k p) -> p k", p=P), allow_slow_non_contiguous=True).then_inc(l_wk, 16)
            sp.dma_start(x_sb[:, :, :], x.rearrange("b s d -> (b s) d").rearrange("(t p) d -> p t d", p=P)
                         ).then_inc(l_x, 16)
            for dst, src in ((wq_sb, Wq), (wv_sb, Wv), (wo_sb, Wo)):
                sp.dma_start(dst[:, :, :], src.rearrange("(k p) n -> p k n", p=P)).then_inc(l_w, 16)
            sp.dma_start(bqc[:, :], bq.rearrange("(k p) -> p k", p=P), allow_slow_non_contiguous=True).then_inc(l_w, 16)

            for n, vec in enumerate((bq, bv, bo, g0, b0, g1, b1)):
                sp.dma_start(rows[:, n, :], vec.rearrange("(a n) -> a n", a=1).broadcast_to([P, D])
                             ).then_inc(l_rows, 16)
            sp.dma_start(wqk[:, 0, :], w_q).then_inc(l_small, 16)
            sp.dma_start(wqk[:, 1, :], w_k).then_inc(l_small, 16)
            sp.dma_start(bqk[:, 0:1], b_q.rearrange("(p a) -> p a", a=1), allow_slow_non_contiguous=True).then_inc(l_small, 16)
            sp.dma_start(bqk[:, 1:2], b_k.rearrange("(p a) -> p a", a=1), allow_slow_non_contiguous=True).then_inc(l_small, 16)
            sp.dma_start(wr_sb[:, :, :], Wr.rearrange("(k p) e -> p k e", p=P)).then_inc(l_small, 16)
            sp.dma_start(br_row[:, :], br.rearrange("(a n) -> a n", a=1).broadcast_to([P, E_])).then_inc(l_small, 16)
            sp.dma_start(b1_rows[:, :], fb1.rearrange("e (f p) -> (e f) p", p=P)).then_inc(l_small, 16)
            sp.dma_start(b2_sb[:, :], fb2).then_inc(l_small, 16)
            def write_keys(i, g, first):
                if g:
                    sp.wait_ge(s_k3, i * NKP + 2 * NC)
                if not first:
                    sp.wait_ge(l_kst[g], i * 96)
                if not g:
                    sp.wait_ge(s_k3, i * NKP + NC)
                for n in range(3):
                    sp.dma_start(k_scr[n, g * P:(g + 1) * P, :], kp[n][:, g, :]).then_inc(l_kw[g], 16)

            def stack_keys(i, g, first):
                if not first:
                    sp.wait_ge(s_pv, i * UB - (1 - g) * UG)
                sp.wait_ge(l_kw[g], i * 48 + 48)
                for slot, part in enumerate((0, 0, 0, 1, 1, 2)):
                    sp.dma_start(kst[slot * DH:(slot + 1) * DH, g * HG:(g + 1) * HG, :],
                                 k_scr[part, g * P:(g + 1) * P, :].rearrange("(h d) n -> d h n", d=DH)
                                 ).then_inc(l_kst[g], 16)

            for g in range(2):
                write_keys(0, g, True)
            stack_keys(0, 0, True)
            sp.wait_ge(s_qparts, 3)
            for n in range(3):
                sp.dma_start(q_scr[n].rearrange("(k p) t -> p k t", p=P), qp[n][:, :, :]).then_inc(l_qw, 16)
            sp.wait_ge(l_qw, 48)
            for slot, part in enumerate((0, 1, 2, 0, 1, 0)):
                sp.dma_start(qst[slot * DH:(slot + 1) * DH, :, :],
                             q_scr[part].rearrange("(h d) t -> d h t", d=DH)).then_inc(l_qst, 16)
            stack_keys(0, 1, True)
            with nc.Fori(1, NB, engines=(ET.SP,)) as i:
                for g in range(2):
                    write_keys(i, g, False)
                for g in range(2):
                    stack_keys(i, g, False)

            sp.wait_ge(s_oev, NB)
            for half in range(2):
                sp.dma_start(o_sb[half * SQ:(half + 1) * SQ, :, :], oall[:, half:NB:2, :]).then_inc(l_xa, 16)
            tail_loads(sp)

        @block.gpsimd
        def _(pool):
            pool.memset(half[:, :], -0.5).then_inc(s_half, 1)
            pool.memset(ident[:, :], 0.0).then_inc(s_const, 1)
            pool.memset(identb[:, :], 0.0).then_inc(s_const, 1)
            pool.wait_ge(s_const, 2)
            for m in (ident, identb):
                pool.affine_select(out=m[:, :], in_=m[:, :], compare_op=ALU.not_equal, fill=1.0, base=0,
                                   pattern=[[-1, P]], channel_multiplier=1).then_inc(s_const, 1)
            pool.wait_ge(s_half, 1)
            pool_pow(pool, 1)
            pool.wait_ge(s_pow, 1)
            pool.memset(vaug[:, :, :, DH:VW], 1.0).then_inc(s_ones, 1)
            pool.memset(osb[:, :], 0.0).then_inc(s_ones, 1)

            def body(i, first):
                if not first:
                    pool.wait_ge(s_qb, i)
                for k in range(NKP):
                    g, c = divmod(k, NC)
                    pool.wait_ge(s_k2, i * NKP + k + 1)
                    if not first and c == 0:
                        pool.wait_ge(l_kw[g], i * 48)
                    w = width(c)
                    pool.tensor_tensor(kp[2][:, g, c * CH * P:c * CH * P + w], res[:, k % RR, 0:w],
                                       kp[1][:, g, c * CH * P:c * CH * P + w], ALU.subtract).then_inc(s_k3, 1)
                if first:
                    pool.wait_ge(l_qst, 96)
                else:
                    pool.wait_ge(s_pv, i * UB)
                pool.wait_ge(s_k3, i * NKP + NKP)
                pool.tensor_copy(qb[0:QR, :, :], qst[:, :, bass.ds(i * SQ, SQ)]).then_inc(s_qb, 1)
                if first:
                    pool.wait_ge(s_qb, 1)
                    pool.memset(kst[QR:KR, :, :], 1.0).then_inc(s_kones, 1)
                    pool.wait_ge(s_kones, 1)

            over_batches(ET.Pool, body)
            tail_pool(pool)

        @block.scalar
        def _(act):
            def load_ctx(b, c):
                full = min(CH, (SK - c * CH * P) // P)
                if full:
                    rows_ = ctx_in[bass.ds(b, 1), c * CH * P:(c * CH + full) * P, :]
                    act.dma_start(cx[:, c * CH:c * CH + full, :],
                                 rows_.rearrange("a (t p) d -> p (a t) d", p=P)).then_inc(l_ctx[c], 16)
                else:
                    act.dma_start(cx[0:KL, KT - 1:KT, :],
                                 ctx_in[bass.ds(b, 1), (KT - 1) * P:SK, :].rearrange("a p d -> p a d")
                                 ).then_inc(l_ctx[c], 16)

            for c in range(NC):
                load_ctx(0, c)
            def body(i, first, order, more):
                for kind, n in order:
                    if kind == "t":
                        c, kt = divmod(n, KD)
                        act.wait_ge(s_tr, i * NTR + n + 1)
                        if kt == 1:
                            if more:
                                load_ctx(i + 1, c)
                            continue
                        if n == 0 and not first:
                            act.wait_ge(s_v, i * NV)
                        w = width(c)
                        act.activation(cxT[:, kt, c * CH * P:c * CH * P + w], bkT[n % 2][:, 0:w], ACT.Copy
                                       ).then_inc(s_ctxT[kt], 1)
                    elif kind == "k":
                        g, c = divmod(n, NC)
                        act.wait_ge(s_kproj, i * NKP + n + 1)
                        if c == 0 and not first:
                            act.wait_ge(l_kw[g], i * 48)
                        w = width(c)
                        act.activation(kp[0][:, g, c * CH * P:c * CH * P + w], bkK[n % 4][:, 0:w],
                                       ACT.Identity, bias=bkc[:, g:g + 1]).then_inc(s_k1, 1)
                    elif kind == "m":
                        act.wait_ge(s_mtr, 2 * i + n + 1)
                        act.activation(qb[QR:KR, n * HG:(n + 1) * HG, :],
                                       bank[0][:, 0:HG * SQ // 2].bitcast(BF16)[0:3, :]
                                       .rearrange("p (h q) -> p h q", q=SQ), ACT.Copy).then_inc(s_mrow, 1)
                    elif kind == "s":
                        b = i if n < UG else i - 1
                        act.wait_ge(s_st, b * UB + n + 1)
                        used = ring_free(n, b, first)
                        if used is not None:
                            act.wait_ge(s_pv, used)
                        rows_ = P if n % UG < UG - 1 else KL
                        act.activation(prob[0:rows_, n % RP, :], bkS[n % 2][0:rows_, :], ACT.Exp
                                       ).then_inc(s_exp, 1)
                    elif kind == "v" and (n % 2 or n == KT - 1):
                        v = n // 2
                        act.wait_ge(s_v, i * NV + v + 1)
                        if v == 0 and not first:
                            act.wait_ge(s_pv, i * UB)
                        t, two, rows_ = 2 * v, n % 2 + 1, keys(n)
                        act.activation(vaug[0:rows_, t:t + two, :, 0:DH],
                                       bkV[v % 2][0:rows_, 0:two * D].rearrange("p (t h d) -> p t h d", t=two, d=DH),
                                       ACT.Copy).then_inc(s_vev, 1)
                    if kind == "a" and n == UB - 1:
                        act.wait_ge(s_pv, i * UB)
                        for half in range(2):
                            r = 64 * half
                            act.activation(osb[r:r + 2 * VW, :], bkO[r:r + 2 * VW, :], ACT.Copy
                                           ).then_inc(s_ocp, 1)

            act.wait_ge(l_wk, 32)
            body(0, True, proj_order(), True)
            for n in range(2):
                act.wait_ge(s_xtr, n + 1)
                act.activation(xnT[:, n, :], bank[n][:, :], ACT.Copy).then_inc(s_xT, 1)
            for n in range(2):
                act.wait_ge(s_wtr, n + 1)
                act.activation(wkT[:, n, :], bank[2 + n][:, 0:D], ACT.Copy).then_inc(s_wT, 1)
            act.wait_ge(s_bqs, 1)
            for m in range(KD):
                act.wait_ge(s_qps, m + 1)
                act.activation(qf[:, m, :], bank[4 + m][:, :], ACT.Identity, bias=bqs[:, m:m + 1],
                               scale=DH ** -0.5).then_inc(s_qf, 1)
            act.wait_ge(s_wkvp, 1)
            act.activation(wkv[:, :, :], bank[6][:, :].rearrange("p (k n) -> p k n", k=KD), ACT.Copy
                           ).then_inc(s_wkv, 1)

            act.wait_ge(s_ones, 2)
            body(0, True, batch_order(True), True)
            with nc.Fori(1, NB - 1, engines=(ET.Activation,)) as i:
                body(i, False, batch_order(False), True)
            body(NB - 1, False, batch_order(False), False)
            body(NB, False, TAIL_ORDER, False)
            tail_act(act)

        @block.tensor
        def _(pe):
            pe.wait_ge(s_const, 4)
            def body(i, first, order):
                for kind, n in order:
                    if kind == "t":
                        c, kt = divmod(n, KD)
                        if kt == 0:
                            pe.wait_ge(l_ctx[c], i * 16 + 16)
                        if n >= 2:
                            pe.wait_ge(s_ctxT[kt], i * NC + c)
                        elif not first:
                            if n == 0:
                                pe.wait_ge(s_mrow, 2 * i)
                            else:
                                pe.wait_ge(s_vev, i * NV)
                        for t in range(c * CH, min(KT, (c + 1) * CH)):
                            mm = pe.transpose(bkT[n % 2][:, (t % CH) * P:(t % CH) * P + keys(t)],
                                              cx[0:keys(t), t, kt * P:(kt + 1) * P],
                                              ident[0:keys(t), 0:keys(t)])
                        mm.then_inc(s_tr, 1)
                    elif kind == "k":
                        g, c = divmod(n, NC)
                        if not g:
                            for k in range(KD):
                                pe.wait_ge(s_ctxT[k], i * NC + c + 1)
                        if n >= 4:
                            pe.wait_ge(s_res, i * NKP + n - 3)
                        elif n == 2 and not first:
                            pe.wait_ge(s_mx, i * UB)
                        elif n == 0 and not first:
                            pe.wait_ge(s_exp, i * UB - UG)
                        w = width(c)
                        for k in range(KD):
                            mm = pe.matmul(bkK[n % 4][:, 0:w], wk_sb[:, k, g * P:(g + 1) * P],
                                           cxT[:, k, c * CH * P:c * CH * P + w],
                                           start=(k == 0), stop=(k == KD - 1))
                        mm.then_inc(s_kproj, 1)
                    elif kind == "v":
                        v = n // 2
                        if n % 2 == 0 and v >= 2:
                            pe.wait_ge(s_vev, i * NV + v - 1)
                        elif n == 0 and not first:
                            pe.wait_ge(s_vev, i * NV)
                        elif n == 2:
                            pe.wait_ge(s_ctxT[1], i * NC + NC)
                        for k in range(KD):
                            mm = pe.matmul(bkV[v % 2][0:keys(n), (n % 2) * D:(n % 2 + 1) * D],
                                           cxT[:, k, n * P:n * P + keys(n)], wkv[:, k, :],
                                           start=(k == 0 and n % 2 == 0), stop=(k == KD - 1),
                                           skip_group_check=True)
                        if n % 2 or n == KT - 1:
                            mm.then_inc(s_v, 1)
                    elif kind == "b":
                        g, u = divmod(n, UG)
                        if u == 0:
                            pe.wait_ge(l_kst[g], i * 96 + 96)
                            pe.wait_ge(s_qb, i + 1)
                        if n >= 2:
                            pe.wait_ge(s_mx, i * UB + n - 1)
                        else:
                            pe.wait_ge(s_res, i * NKP + NKP - 1 + n)
                        if u < UG - 1:
                            j, c = divmod(u, FC)
                            parts = [(j, c * CH * P, CH * P, 0)]
                        else:
                            parts = [(j, (KT - 1) * P, KL, j * KL) for j in range(NPJ)]
                        for j, key, w, at in parts:
                            for e in range(2):
                                h = g * HG + 2 * j + e
                                mm = pe.matmul(bkX[n % 2][64 * e:64 * e + SQ, at:at + w], qb[0:QR, h, :],
                                               kst[0:QR, h, key:key + w], start=True, stop=True)
                        mm.then_inc(s_ms, 1)
                    elif kind == "m":
                        pe.wait_ge(s_mp, 2 * i + n + 1)
                        if n == 0:
                            pe.wait_ge(s_ctxT[0], i * NC + NC)
                            if not first:
                                pe.wait_ge(s_oev, i)
                        else:
                            pe.wait_ge(s_mrow, 2 * i + 1)
                        for j in range(NPJ):
                            mm = pe.transpose(bank[0][:, 0:HG * SQ // 2].bitcast(BF16)[0:3, j * P:(j + 1) * P],
                                              mpt[:, j, 0:3], identb[:, :])
                        mm.then_inc(s_mtr, 1)
                    elif kind == "s":
                        b = i if n < UG else i - 1
                        g, u = divmod(n, UG)
                        if u == 0:
                            pe.wait_ge(s_mrow, 2 * b + g + 1)
                            if first:
                                pe.wait_ge(s_kones, 1)
                            if order is not TAIL_ORDER:
                                pe.wait_ge(s_res, i * NKP + NKP - 2)
                        if not (first and n < 2):
                            pe.wait_ge(s_exp, b * UB + n - 1)
                        for j, t, place in unit(u):
                            for e in range(2):
                                h = g * HG + 2 * j + e
                                at = place * P + e * SQ
                                mm = pe.matmul(bkS[n % 2][0:keys(t), at:at + SQ],
                                               kst[0:KR, h, t * P:t * P + keys(t)], qb[0:KR, h, :],
                                               start=True, stop=True)
                        mm.then_inc(s_st, 1)
                    elif kind == "a":
                        b = i if n < UG else i - 1
                        g, u = divmod(n, UG)
                        if n == 0:
                            pe.wait_ge(s_vev, i * NV + NV)
                            if not first:
                                pe.wait_ge(s_ocp, 2 * i)
                        pe.wait_ge(s_exp, b * UB + n + 1)
                        for j, t, place in unit(u):
                            jj = g * NPJ + j
                            r = 64 * (jj % 2)
                            mm = pe.matmul(bkO[r:r + 2 * VW, (jj // 2) * P:(jj // 2 + 1) * P],
                                           vaug[0:keys(t), t, 2 * jj:2 * jj + 2, :].rearrange("p h v -> p (h v)"),
                                           prob[0:keys(t), n % RP, place * P:(place + 1) * P],
                                           start=(t == 0 and jj < 2), stop=(t == KT - 1),
                                           skip_group_check=True)
                        mm.then_inc(s_pv, 1)
                    elif kind == "o" and not first:
                        pe.wait_ge(s_ocp, 2 * i)
                        if order is not TAIL_ORDER:
                            pe.wait_ge(s_ctxT[0], i * NC + NC)
                        else:
                            pe.wait_ge(s_mrow, 2 * i)
                        for blk in range(H // 4):
                            mm = pe.transpose(bank[0][:, blk * P:(blk + 1) * P], osb[:, blk * P:(blk + 1) * P],
                                              ident[:, :])
                        mm.then_inc(s_otr, 1)

            pe.wait_ge(l_wk, 32)
            body(0, True, proj_order())
            for k in range(KD):
                pe.wait_ge(s_ctxT[k], NC)
            pe.wait_ge(s_res, NKP)
            pe.wait_ge(s_xn, NT)
            for k in range(KD):
                for t in range(NT):
                    mm = pe.transpose(bank[k][:, t * P:(t + 1) * P], xn[:, t, k * P:(k + 1) * P], ident[:, :])
                mm.then_inc(s_xtr, 1)
            pe.wait_ge(l_w, 64)
            for k in range(KD):
                for t in range(KD):
                    mm = pe.transpose(bank[2 + k][:, t * P:(t + 1) * P], wk_sb[:, t, k * P:(k + 1) * P], ident[:, :])
                mm.then_inc(s_wtr, 1)
            pe.wait_ge(s_xT, 2)
            for m in range(KD):
                for k in range(KD):
                    mm = pe.matmul(bank[4 + m][:, :], wq_sb[:, k, m * P:(m + 1) * P], xnT[:, k, :],
                                   start=(k == 0), stop=(k == KD - 1))
                mm.then_inc(s_qps, 1)
            pe.wait_ge(s_wT, 2)
            for m in range(KD):
                for k in range(KD):
                    mm = pe.matmul(bank[6][:, m * D:(m + 1) * D], wkT[:, k, m * P:(m + 1) * P], wv_sb[:, k, :],
                                   start=(k == 0 and m == 0), stop=(k == KD - 1), skip_group_check=True)
            mm.then_inc(s_wkvp, 1)
            for t in range(NT):
                for k in range(KD):
                    mm = pe.matmul(bank[t // 2][:, (t % 2) * D:(t % 2 + 1) * D], xnT[:, k, t * P:(t + 1) * P],
                                   wq_sb[:, k, :], start=(k == 0 and t % 2 == 0), stop=(k == KD - 1),
                                   skip_group_check=True)
                if t % 2:
                    mm.then_inc(s_qtp, 1)
            for k in range(KD):
                mm = pe.matmul(bank[7][:, 0:D], bkc[:, k:k + 1].broadcast_to([P, P]), wv_sb[:, k, :],
                               start=(k == 0), stop=(k == KD - 1))
            mm.then_inc(s_qtp, 1)
            pe.wait_ge(s_wkv, 1)
            pe.wait_ge(s_qf, 2)
            pe.wait_ge(s_qt, 3)

            over_batches(ET.PE, lambda i, first: body(i, first, batch_order(first)))
            body(NB, False, TAIL_ORDER)
            tail_pe(pe)

        @block.vector
        def _(dve):
            dve.wait_ge(l_x, 16)
            layernorm(dve, xn, x_sb, s_xn)
            def body(i, first, order):
                for kind, n in order:
                    if kind == "t" and n % KD == 1:
                        c = n // KD
                        dve.wait_ge(s_tr, i * NTR + n + 1)
                        if n == 1 and not first:
                            dve.wait_ge(s_v, i * NV)
                        w = width(c)
                        dve.tensor_copy(cxT[:, 1, c * CH * P:c * CH * P + w], bkT[1][:, 0:w]).then_inc(s_ctxT[1], 1)
                    elif kind == "k":
                        g, c = divmod(n, NC)
                        w = width(c)
                        at = slice(c * CH * P, c * CH * P + w)
                        dve.wait_ge(s_k1, i * NKP + n + 1)
                        if not (first and n < RR):
                            dve.wait_ge(s_k3, i * NKP + n - RR + 1)
                        dve.scalar_tensor_tensor(out=res[:, n % RR, 0:w], in0=bkK[n % 4][:, 0:w],
                                                 scalar=bkc[:, g:g + 1], in1=kp[0][:, g, at],
                                                 op0=ALU.add, op1=ALU.subtract).then_inc(s_res, 1)
                        dve.wait_ge(s_res, i * NKP + n + 1)
                        if c == 0 and not first:
                            dve.wait_ge(l_kw[g], i * 48)
                        dve.tensor_copy(kp[1][:, g, at], res[:, n % RR, 0:w]).then_inc(s_k2, 1)
                    elif kind == "b":
                        g, u = divmod(n, UG)
                        dve.wait_ge(s_ms, i * UB + n + 1)
                        if u < UG - 1:
                            j, c = divmod(u, FC)
                            dve.tensor_reduce(mx[:, g * NPJ + j, c:c + 1], bkX[n % 2][:, :], AX.X, ALU.max
                                              ).then_inc(s_mx, 1)
                        else:
                            dve.tensor_reduce(mx[:, g * NPJ:(g + 1) * NPJ, FC],
                                              bkX[n % 2][:, 0:NPJ * KL].rearrange("p (j k) -> p j k", j=NPJ),
                                              AX.X, ALU.max).then_inc(s_mx, 1)
                    elif kind == "p":
                        dve.wait_ge(s_mx, i * UB + (n + 1) * UG)
                        if n or not first:
                            dve.wait_ge(s_mtr, 2 * i + n)
                        m0 = i * 8 + n * 4
                        dve.tensor_reduce(nm[:, :], mx[:, n * NPJ:(n + 1) * NPJ, :], AX.X, ALU.max, negate=True
                                          ).then_inc(s_mstep, 1)
                        dve.wait_ge(s_mstep, m0 + 1)
                        dve.tensor_copy(mpt[:, :, 0], nm[:, :]).then_inc(s_mstep, 1)
                        dve.wait_ge(s_mstep, m0 + 2)
                        dve.tensor_tensor(nr[:, :], nm[:, :], mpt[:, :, 0], ALU.subtract).then_inc(s_mstep, 1)
                        dve.wait_ge(s_mstep, m0 + 3)
                        dve.tensor_copy(mpt[:, :, 1], nr[:, :]).then_inc(s_mstep, 1)
                        dve.wait_ge(s_mstep, m0 + 4)
                        dve.tensor_tensor(mpt[:, :, 2], nr[:, :], mpt[:, :, 1], ALU.subtract).then_inc(s_mp, 1)
                    elif kind == "o" and not first:
                        dve.wait_ge(s_otr, i)
                        got = [bank[0][e * SQ:(e + 1) * SQ, :].rearrange("q (k j r) -> q k j r", k=H // 4, j=2)
                               for e in range(2)]
                        for e in range(2):
                            dve.reciprocal(rec[e * SQ:(e + 1) * SQ, :, :], got[e][:, :, :, e * VW + DH]
                                           ).then_inc(s_rec, 1)
                        dve.wait_ge(s_rec, 2 * i)
                        heads = oall[:, bass.ds(i - 1, 1), :].rearrange("q a (k j e d) -> q (a k) j e d", k=H // 4,
                                                                        j=2, e=2)
                        for e in range(2):
                            mul = dve.tensor_tensor(
                                heads[:, :, :, e, :], got[e][:, :, :, e * VW:e * VW + DH],
                                rec[e * SQ:(e + 1) * SQ, :, :].unsqueeze(3).broadcast_to([SQ, H // 4, 2, DH]),
                                ALU.mult)
                        mul.then_inc(s_oev, 1)

            dve.wait_ge(l_wk, 32)
            body(0, True, proj_order())
            dve.wait_ge(l_w, 64)
            dve.tensor_scalar(bqs[:, :], bqc[:, :], DH ** -0.5, None, ALU.mult).then_inc(s_bqs, 1)
            dve.wait_ge(s_qf, 2)
            link(dve, dve.tensor_copy(qp[0][:, :, :], qf[:, :, :]))
            link(dve, dve.tensor_tensor(qf[:, :, :], qf[:, :, :], qp[0][:, :, :], ALU.subtract))
            link(dve, dve.tensor_copy(qp[1][:, :, :], qf[:, :, :]))
            dve.tensor_tensor(qp[2][:, :, :], qf[:, :, :], qp[1][:, :, :], ALU.subtract).then_inc(s_qparts, 3)
            dve.wait_ge(l_rows, 16 * 7)
            dve.wait_ge(s_qtp, 3)
            dve.tensor_tensor(bkv[:, :], bank[7][:, 0:D], rows[:, 1, :], ALU.add).then_inc(s_qt, 1)
            for n in range(2):
                ins = dve.tensor_tensor(qtok[:, 2 * n:2 * n + 2, :],
                                        bank[n][:, :].rearrange("p (t d) -> p t d", t=2),
                                        rows[:, 0:1, :].broadcast_to([P, 2, D]), ALU.add)
                ins.then_inc(s_qt, 1)
            dve.wait_ge(s_qt, 3)
            link(dve, dve.tensor_tensor(qtok[:, :, :], qtok[:, :, :],
                                        bkv[:, :].unsqueeze(1).broadcast_to([P, NT, D]), ALU.add))

            dve.wait_ge(s_ones, 2)
            over_batches(ET.DVE, lambda i, first: body(i, first, batch_order(first)))
            body(NB, False, TAIL_ORDER)
            tail_dve(dve)


_INS = ["x", "ctx_1024", "L0_xattn_Wq", "L0_xattn_bq", "L0_xattn_Wk", "L0_xattn_bk", "L0_xattn_Wv", "L0_xattn_bv",
        "L0_xattn_Wo", "L0_xattn_bo", "L0_xattn_g0", "L0_xattn_b0", "L0_xattn_g1", "L0_xattn_b1",
        "L0_attn_w_q", "L0_attn_b_q", "L0_attn_w_k", "L0_attn_b_k",
        "L0_ffn_W1", "L0_ffn_b1", "L0_ffn_W2", "L0_ffn_b2", "L0_ffn_Wr", "L0_ffn_br"]


def kernel(**inputs):
    import numpy as _np
    import concourse.bacc as _bacc
    from concourse import mybir as _mybir
    from concourse.bass_utils import run_bass_kernel_spmd as _run

    nc = _bacc.Bacc("TRN2", target_bir_lowering=False, num_devices=1)
    arrays, args = {}, []
    for name in _INS:
        a = _np.ascontiguousarray(inputs[name])
        arrays[f"in_{name}"] = a
        args.append(nc.dram_tensor(f"in_{name}", a.shape, _mybir.dt.from_np(a.dtype), kind="ExternalInput").ap())
    shape = inputs["x"].shape
    args.append(nc.dram_tensor("out_0", shape, _mybir.dt.float32, kind="ExternalOutput").ap())
    perceiver_kernel(nc, *args)
    r = _run(nc, [arrays], core_ids=[0])
    return r.results[0]["out_0"]
```

```python
from contextlib import ExitStack

import concourse.bass as bass
from concourse import mybir

F32 = mybir.dt.float32
BF16 = mybir.dt.bfloat16
F32R = mybir.dt.float32r
ALU = mybir.AluOpType
ACT = mybir.ActivationFunctionType
AX = mybir.AxisListType
ET = mybir.EngineType
EPS = 1e-5


def perceiver_kernel(nc, x, ctx_in, Wq, bq, Wk, bk, Wv, bv, Wo, bo, g0, b0, g1, b1,
                     w_q, b_q, w_k, b_k, W1, fb1, W2, fb2, Wr, br, out):
    NB, SQ, D = x.shape
    SK = ctx_in.shape[1]
    H, DH = 16, D // 16
    P = 128
    KD = D // P
    NT = NB * SQ // P
    T = NB * SQ
    KT = -(-SK // P)
    KL = SK - (KT - 1) * P
    CH = 4
    NC = -(-KT // CH)
    HG = H // 2
    NPJ = HG // 2
    FC = NC - 1
    UG = NPJ * FC + 1
    UB = 2 * UG
    NV = -(-KT // 2)
    NTR = KD * NC
    NKP = 2 * NC
    QR = 6 * DH
    KR = QR + 3
    VW = DH + 1
    CUT = NC // 2 * CH * P
    RP = 4
    assert KT == FC * CH + 1 and NPJ * P <= 512
    RR = 3
    E_, F_ = W1.shape[0], W1.shape[2]
    FT = F_ // P
    QD = w_q.shape[0]
    NS = NT + E_ - 1
    NF = NS - 2
    assert NF % 2 == 1

    def width(c):
        return min(CH * P, SK - c * CH * P)

    def keys(t):
        return min(P, SK - t * P)

    def unit(u):
        if u < UG - 1:
            c, j = divmod(u, NPJ)
            return [(j, c * CH + t, t) for t in range(CH)]
        return [(j, KT - 1, j) for j in range(NPJ)]

    def ring_free(n, b, first):
        if n >= RP:
            return b * UB + n - RP + 1
        if first:
            return None
        return (b - 1) * UB + max(m for m in range(UB) if m % RP == n) + 1

    PRODUCTS = ((0, 0), (1, 0), (0, 1))

    ctx = ExitStack()
    with ctx:
        def sb(name, shape, dt=F32):
            return ctx.enter_context(nc.sbuf_tensor(name, shape, dt))

        def sem(name):
            return ctx.enter_context(nc.semaphore(name))

        bank = [ctx.enter_context(nc.psum_tensor(f"bank{n}", [P, 512], F32)) for n in range(8)]
        bkT = [bank[1], bank[0]]
        bkV = [bank[2], bank[1]]
        bkX = [bank[3], bank[4]]
        bkS = [bank[5], bank[6]]
        bkK = [bank[3], bank[4], bank[2]]
        bkH = [bank[2], bank[3], bank[6], bank[7]]
        bkO = bank[7]

        q_scr = nc.dram_tensor("q_parts", [3, D, T], BF16, kind="Internal").ap()
        k_scr = nc.dram_tensor("k_parts", [3, D, SK], BF16, kind="Internal").ap()

        x_scr = nc.dram_tensor("x_slots", [NS * P, D], F32, kind="Internal").ap()
        a_scr = nc.dram_tensor("a_slots", [NS * P, D + 2], F32, kind="Internal").ap()

        ident = sb("ident", [P, P])
        identb = sb("identb", [P, P], BF16)
        wo_sb = sb("wo_sb", [P, KD, D])
        wk2 = [sb(f"wk_part{n}", [P, KD, D], F32R) for n in range(2)]
        wkv2 = [sb(f"wkv_part{n}", [P, KD, D], F32R) for n in range(2)]
        bqc = sb("bqc", [P, KD])
        bqs = sb("bqs", [P, KD])
        bkc = sb("bkc", [P, KD])
        rows = sb("rows", [P, 7, D])
        bkv = sb("bkv", [P, D])
        x_sb = sb("x_sb", [P, NT, D])
        xn = sb("xn", [P, NT, D])
        xnT = sb("xnT", [P, KD, T])
        qtok = sb("qtok", [P, NT, D])
        st = sb("st", [P, NT, 6])
        mv = sb("mv", [P, NT, 2])
        rstd = sb("rstd", [P, NT])
        ve = sb("ve", [P, NT])
        nwt = sb("nwt", [P, NT])
        half = sb("half", [P, NT])
        oall = sb("oall", [SQ, NB, D])
        wqk = sb("wqk", [QD, 2, D])
        wqkT = sb("wqkT", [P, 2, KD, QD])
        bqk = sb("bqk", [QD, 2])
        wr_sb = sb("wr_sb", [P, KD, E_])
        br_row = sb("br_row", [P, E_])
        b1_rows = sb("b1_rows", [E_ * FT, P])
        b1c = sb("b1c", [P, E_ * FT])
        b2_sb = sb("b2_sb", [E_, D])
        iota = sb("iota", [P, NS])
        iota8 = iota[:, 0:E_]
        before = sb("before", [P, P])
        all1 = sb("all1", [P, P])
        lower = sb("lower", [P, E_, E_])
        empty = sb("empty", [P, D + 2])
        number = sb("number", [P, NT], mybir.dt.int32)
        most = sb("most", [P, SQ])
        least = sb("least", [P, SQ])
        attn = ExitStack()
        def ab(name, shape, dt=F32):
            return attn.enter_context(nc.sbuf_tensor(name, shape, dt))
        cx = ab("cx", [P, KT, D])
        cxT = [ab(f"cxT_part{n}", [P, KD, SK + SK % 2], F32R) for n in range(2)]
        kp = [ab(f"kp{n}", [P, KD, SK], BF16) for n in range(3)]
        res = ab("res", [P, RR, CH * P])
        kst = ab("kst", [KR, H, SK], BF16)
        qst = ab("qst", [KR, H, T], BF16)
        qb = ab("qb", [QR, H, SQ], BF16)
        setup = ExitStack()

        def setup_sb(name, shape, dt=F32):
            return setup.enter_context(nc.sbuf_tensor(name, shape, dt))

        wk_sb = setup_sb("wk_sb", [P, KD, D])
        wq_sb = setup_sb("wq_sb", [P, KD, D])
        wv_sb = setup_sb("wv_sb", [P, KD, D])
        wkT = setup_sb("wkT", [P, KD, D])
        qf = setup_sb("qf", [P, KD, T])
        qp = [setup_sb(f"qp{n}", [P, KD, T], BF16) for n in range(3)]
        setup.close()
        vaug = ab("vaug", [P, KT, H, VW])
        osb = ab("osb", [P, H // 4 * P])
        prob = ab("prob", [P, RP, CH * P])
        mx = ab("mx", [P, H // 2, NC])
        nm = ab("nm", [P, NPJ])
        nr = ab("nr", [P, NPJ])
        mpt = ab("mpt", [P, NPJ, 4], BF16)
        rec = ab("rec", [P, H // 4, 2])
        attn.close()
        o_sb = sb("o_sb", [P, NT, D])
        u_sb = sb("u_sb", [P, NT, D])
        q2T = sb("q2T", [QD, T])
        k2T = sb("k2T", [QD, T])
        sc = sb("sc", [P, NT, SQ])
        s4 = sb("s4", [P, NT])
        r4 = sb("r4", [P, NT])
        pblk = sb("pblk", [P, NT, P])
        pT = sb("pT", [P, NT, P])
        lg = sb("lg", [P, NT, E_])
        ex = sb("ex", [P, NT, E_])
        gates = sb("gates", [P, NT, E_])
        gT = sb("gT", [E_, T])
        extra = sb("extra", [P, NT, D + 2])
        chosen = sb("chosen", [P, NT, E_])
        earlier = sb("earlier", [P, NT + 1, E_])
        ntiles = sb("ntiles", [P, E_])
        scan = sb("scan", [P, E_, E_])
        base = sb("base", [P, E_])
        rank = sb("rank", [P, NT, E_])
        slot_f = sb("slot_f", [P, NT])
        slot = sb("slot", [P, NT], mybir.dt.uint32)
        past = sb("past", [P, NS, E_])
        expert_f = sb("expert_f", [P, NS])
        expert = sb("expert", [P, NS], mybir.dt.int32)
        w1_sb = [sb(f"w1_sb{n}", [P, KD, F_]) for n in range(2)]
        w2_sb = [sb(f"w2_sb{n}", [P, FT, D]) for n in range(2)]
        xg = sb("xg", [P, 2, D])
        xgT = sb("xgT", [P, KD, P])
        total = sb("total", [P, 1], mybir.dt.int32)
        h_sb = sb("h_sb", [P, F_])
        hT = sb("hT", [P, FT, P])
        eg = sb("eg", [P, 2, D + 2])
        id_u = sb("id_u", [P, 2, 1], mybir.dt.uint32)
        y_sb = sb("y_sb", [P, 2, D])

        s_const = sem("s_const")
        s_ones = sem("s_ones")
        s_kones = sem("s_kones")
        l_kones = sem("l_kones")
        l_x = sem("l_x")
        l_wk = sem("l_wk")
        l_w = sem("l_w")
        l_rows = sem("l_rows")
        s_chain = sem("s_chain")
        s_var = sem("s_var")
        s_pow = sem("s_pow")
        s_half = sem("s_half")
        s_xn = sem("s_xn")
        s_xtr = sem("s_xtr")
        s_xT = sem("s_xT")
        s_wtr = sem("s_wtr")
        s_wT = sem("s_wT")
        s_wkvp = sem("s_wkvp")
        s_wkv = sem("s_wkv")
        s_bqs = sem("s_bqs")
        s_qps = sem("s_qps")
        s_qf = sem("s_qf")
        s_qtp = sem("s_qtp")
        s_qt = sem("s_qt")
        s_qparts = sem("s_qparts")
        l_qw = sem("l_qw")
        l_qst = sem("l_qst")
        l_ctx = [sem(f"l_ctx{c}") for c in range(NC)]
        s_tr = sem("s_tr")
        s_pad = sem("s_pad")
        s_wk1 = sem("s_wk1")
        s_wk2 = sem("s_wk2")
        s_wkv2 = sem("s_wkv2")
        s_chigh = sem("s_chigh")
        s_ctxT = [sem(f"s_ctxT{k}") for k in range(KD)]
        s_kproj = sem("s_kproj")
        s_k1 = sem("s_k1")
        s_res = sem("s_res")
        s_k2 = sem("s_k2")
        s_k3 = sem("s_k3")
        l_kw = [sem(f"l_kw{g}") for g in range(2)]
        l_kst = [sem(f"l_kst{g}") for g in range(2)]
        s_v = sem("s_v")
        s_vev = sem("s_vev")
        s_qb = sem("s_qb")
        s_ms = sem("s_ms")
        s_mx = sem("s_mx")
        s_mp = sem("s_mp")
        s_mstep = sem("s_mstep")
        s_rec = sem("s_rec")
        s_mtr = sem("s_mtr")
        s_mrow = sem("s_mrow")
        s_st = sem("s_st")
        s_exp = sem("s_exp")
        s_pv = sem("s_pv")
        s_ocp = sem("s_ocp")
        s_otr = sem("s_otr")
        s_oev = sem("s_oev")
        l_xa = [sem(f"l_xa{h}") for h in range(2)]
        l_small = sem("l_small")
        s_iota = sem("s_iota")
        s_pz = sem("s_pz")
        s_xb = sem("s_xb")
        s_smallT = sem("s_smallT")
        s_smallc = sem("s_smallc")
        s_o1 = sem("s_o1")
        s_wo = sem("s_wo")
        s_gelu = sem("s_gelu")
        s_nT = sem("s_nT")
        s_nTc = sem("s_nTc")
        s_xn2 = sem("s_xn2")
        s_qk = sem("s_qk")
        s_qkc = sem("s_qkc")
        s_sc = sem("s_sc")
        s_sub = sem("s_sub")
        s_sexp = sem("s_sexp")
        s_pblk = sem("s_pblk")
        s_pT = sem("s_pT")
        s_pTc = sem("s_pTc")
        s_att = sem("s_att")
        s_xn3 = sem("s_xn3")
        s_lg = sem("s_lg")
        s_lsub = sem("s_lsub")
        s_lexp = sem("s_lexp")
        s_gate = sem("s_gate")
        s_gT = sem("s_gT")
        s_gTc = sem("s_gTc")
        s_b2 = sem("s_b2")
        l_w1 = [sem(f"l_w1_{n}") for n in range(2)]
        l_w2 = [sem(f"l_w2_{n}") for n in range(2)]
        s_zero = sem("s_zero")
        s_route = sem("s_route")
        l_zero = sem("l_zero")
        s_chosen = sem("s_chosen")
        s_rank = sem("s_rank")
        s_slot = sem("s_slot")
        s_expert = sem("s_expert")
        l_slots = sem("l_slots")
        l_xg = [sem(f"l_xg{n}") for n in range(2)]
        s_xg = sem("s_xg")
        s_xgT = sem("s_xgT")
        s_h = sem("s_h")
        s_hc = sem("s_hc")
        s_ht = sem("s_ht")
        s_gelu2 = sem("s_gelu2")
        s_y = sem("s_y")
        s_yc = sem("s_yc")
        s_acc = sem("s_acc")
        l_extra = sem("l_extra")
        l_eg = [sem(f"l_eg{n}") for n in range(2)]
        l_out = [sem(f"l_out{n}") for n in range(2)]

        chain = [0]
        norms = [0]
        norm_of = {}
        transposed = [0]
        turned = [0]
        turned_at = {}

        def link(dve, ins):
            chain[0] += 1
            ins.then_inc(s_chain, 1)
            dve.wait_ge(s_chain, chain[0])

        def norm_stats(dve, src, tiles):
            for t in tiles:
                ins = dve.bn_stats(st[:, t, :], src[:, t, :])
            link(dve, ins)
            for t in tiles:
                ins = dve.bn_aggr(mv[:, t, :], st[:, t, :])
            link(dve, ins)
            norms[0] += 1
            norm_of[tiles[0]] = norms[0]
            dve.tensor_scalar(ve[:, tiles[0]:tiles[-1] + 1], mv[:, tiles[0]:tiles[-1] + 1, 1], EPS, None, ALU.add
                              ).then_inc(s_var, 1)

        def norm_factor(dve, tiles):
            at = slice(tiles[0], tiles[-1] + 1)
            dve.wait_ge(s_pow, norm_of[tiles[0]])
            link(dve, dve.scalar_tensor_tensor(out=nwt[:, at], in0=rstd[:, at], scalar=-0.5, in1=rstd[:, at],
                                               op0=ALU.mult, op1=ALU.mult))
            link(dve, dve.tensor_tensor(nwt[:, at], nwt[:, at], ve[:, at], ALU.mult))
            link(dve, dve.scalar_tensor_tensor(out=rstd[:, at], in0=nwt[:, at], scalar=1.5, in1=rstd[:, at],
                                               op0=ALU.add, op1=ALU.mult))

        def norm_apply(dve, dst, src, tiles, done):
            for t in tiles:
                dve.tensor_scalar(dst[:, t, :], src[:, t, :], mv[:, t, 0:1], rstd[:, t:t + 1],
                                  ALU.subtract, ALU.mult).then_inc(done, 1)

        def norm_apply_gain(dve, dst, src, tiles, gain, added):
            for t in tiles:
                ins = dve.scalar_tensor_tensor(out=u_sb[:, t, :], in0=src[:, t, :], scalar=mv[:, t, 0:1],
                                               in1=rows[:, gain, :], op0=ALU.subtract, op1=ALU.mult)
            link(dve, ins)
            for t in tiles:
                ins = dve.scalar_tensor_tensor(out=dst[:, t, :], in0=u_sb[:, t, :], scalar=rstd[:, t:t + 1],
                                               in1=added(t), op0=ALU.mult, op1=ALU.add)
            return ins

        def pool_pow(pool, n, tiles):
            at = slice(tiles[0], tiles[-1] + 1)
            pool.wait_ge(s_var, n)
            pool.tensor_tensor(rstd[:, at], ve[:, at], half[:, at], ALU.pow).then_inc(s_pow, 1)

        def tiles_of(h):
            return list(range(h * NT // 2, (h + 1) * NT // 2))

        CHAIN_EARLY = {1: "a0", 4: "a1", 6: "a2", 8: "a3"}
        CHAIN = [("g", 0), ("b0", 0), ("a0", 1), ("a1", 1), ("b1", 0), ("a2", 1), ("a3", 1), ("g", 1), ("b2", 0),
                 ("c0", 0), ("c1", 0), ("b0", 1), ("c2", 0), ("b1", 1), ("c3", 0), ("b2", 1), ("c4", 0), ("c0", 1),
                 ("c1", 1), ("c5", 0), ("c2", 1), ("c6", 0), ("c3", 1), ("c4", 1), ("d0", 0), ("c5", 1), ("c6", 1),
                 ("d1", 0), ("d2", 0), ("d0", 1), ("d1", 1), ("d3", 0), ("d2", 1), ("d3", 1)]

        def over_tiles(eng, eng_type, step, start=None):
            if start:
                start(0)
            step(0, 0, True, False)
            with nc.Fori(0, (NF - 3) // 2, engines=(eng_type,)) as i:
                step(2 * i + 1, 1, True, False)
                step(2 * i + 2, 0, True, False)
            step(NF - 2, 1, False, False)
            step(NF - 1, 0, False, True)
            used = eng.value_load(total[0:1, 0:1], min_val=1, max_val=NS)
            with eng.If(used > NF):
                if start:
                    start(NF)
                for s in range(NF, NS):
                    step(s, s % 2, False, s == NS - 1)

        def tail_loads(sp):
            sp.wait_ge(s_v, NB * NV)
            for g in range(2):
                sp.wait_ge(l_kw[g], NB * 96)
            for h in range(2):
                sp.wait_ge(s_oev, (h + 1) * NB // 2)
                for odd in range(2):
                    sp.dma_start(o_sb[odd * SQ:(odd + 1) * SQ, tiles_of(h)[0]:tiles_of(h)[-1] + 1, :],
                                 oall[:, h * NB // 2 + odd:(h + 1) * NB // 2:2, :]).then_inc(l_xa[h], 16)
            sp.wait_ge(s_zero, 2)
            sp.dma_start(x_scr.rearrange("(s p) d -> p s d", p=P),
                         empty[:, 0:D].unsqueeze(1).broadcast_to([P, NS, D])).then_inc(l_zero, 16)
            sp.dma_start(a_scr.rearrange("(s p) d -> p s d", p=P),
                         empty[:, :].unsqueeze(1).broadcast_to([P, NS, D + 2])).then_inc(l_zero, 16)

            def load_w1(e, ring):
                sp.dma_start(w1_sb[ring][:, :, :], W1[e].rearrange("a (k p) f -> p (a k) f", p=P)
                             ).then_inc(l_w1[ring], 16)

            def load_w2(e, ring):
                sp.dma_start(w2_sb[ring][:, :, :], W2[e].rearrange("a (f p) d -> p (a f) d", p=P)
                             ).then_inc(l_w2[ring], 16)

            def expert_of(tile):
                return bass.ds(sp.value_load(expert[0:1, bass.ds(tile, 1)], min_val=0, max_val=E_ - 1), 1)

            load_w1(slice(0, 1), 0)
            load_w2(slice(0, 1), 0)
            sp.wait_ge(s_expert, 1)
            e = expert_of(1)
            sp.wait_ge(l_slots, NT * 16)
            for s in range(2):
                sp.dma_start(xg[:, s, :], x_scr[s * P:(s + 1) * P, :]).then_inc(l_xg[s], 16)
            load_w1(e, 1)
            load_w2(e, 1)
            sp.wait_ge(l_extra, NT * 16)
            for s in range(2):
                sp.dma_start(eg[:, s, :], a_scr[s * P:(s + 1) * P, :]).then_inc(l_eg[s], 16)

            def step(s, ring, more, last):
                if more:
                    e = expert_of(s + 2)
                    sp.wait_ge(s_xg, s + 1)
                    sp.dma_start(xg[:, ring, :], x_scr[bass.ds((s + 2) * P, P), :]).then_inc(l_xg[ring], 16)
                    sp.wait_ge(s_h, 2 * s + 2)
                    load_w1(e, ring)
                    sp.wait_ge(s_y, s + 1)
                    load_w2(e, ring)
                    sp.wait_ge(s_yc, s + 1)
                    sp.dma_start(eg[:, ring, :], a_scr[bass.ds((s + 2) * P, P), :]).then_inc(l_eg[ring], 16)
                if last:
                    for r in range(2):
                        sp.wait_ge(l_out[r], (s + 2 - r) // 2 * 16)

            def start(s):
                if s:
                    sp.wait_ge(s_yc, s)
                    for t in range(s, NS):
                        e = expert_of(t)
                        sp.dma_start(xg[:, t % 2, :], x_scr[t * P:(t + 1) * P, :]).then_inc(l_xg[t % 2], 16)
                        load_w1(e, t % 2)
                        load_w2(e, t % 2)
                        sp.dma_start(eg[:, t % 2, :], a_scr[t * P:(t + 1) * P, :]).then_inc(l_eg[t % 2], 16)

            over_tiles(sp, ET.SP, step, start)

        def tail_pool(pool):
            pool.wait_ge(l_rows, 16 * 7)
            pool.wait_ge(s_xn, NT)
            pool.tensor_tensor(x_sb[:, :, :], x_sb[:, :, :], rows[:, 6:7, :].broadcast_to([P, NT, D]), ALU.add
                               ).then_inc(s_xb, 1)
            pool.memset(most[:, :], 3e38).then_inc(s_route, 1)
            pool.memset(least[:, :], -3e38).then_inc(s_route, 1)
            pool.memset(empty[:, 0:D + 1], 0.0).then_inc(s_zero, 1)
            pool.memset(empty[:, D + 1:D + 2], float(T)).then_inc(s_zero, 1)
            for n in range(NS):
                pool.memset(iota[:, n:n + 1], float(n)).then_inc(s_iota, 1)
            pool.iota(number[:, :], pattern=[[P, NT]], base=0, channel_multiplier=1).then_inc(s_iota, 1)
            pool.memset(all1[:, :], 1.0).then_inc(s_route, 1)
            pool.memset(before[:, :], 1.0).then_inc(s_route, 1)
            pool.memset(lower[:, :, :], 1.0).then_inc(s_route, 1)
            pool.wait_ge(s_route, 5)
            pool.affine_select(out=before[:, :], in_=before[:, :], compare_op=ALU.is_gt, fill=0.0, base=0,
                               pattern=[[1, P]], channel_multiplier=-1).then_inc(s_route, 1)
            pool.affine_select(out=lower[:, :, :], in_=lower[:, :, :], compare_op=ALU.is_gt, fill=0.0, base=0,
                               pattern=[[1, E_], [-1, E_]], channel_multiplier=0).then_inc(s_route, 1)
            n = 7
            for odd in range(2):
                r = slice(odd * SQ, (odd + 1) * SQ)
                for m in (most, least):
                    pool.wait_ge(s_route, n)
                    pool.affine_select(out=m[r, :], in_=m[r, :], compare_op=ALU.is_ge, fill=-10000.0, base=0,
                                       pattern=[[-1, SQ]], channel_multiplier=1).then_inc(s_route, 1)
                    n += 1
            pool.wait_ge(s_route, n)
            pool.wait_ge(s_v, NB * NV)
            pool.memset(pblk[:, :, :], 0.0).then_inc(s_pz, 1)
            powers = [1]
            for step, h in [(step, 0) for step in CHAIN_EARLY.values()] + CHAIN:
                if step in ("a0", "b0", "b1", "c6"):
                    powers[0] += 1
                    pool_pow(pool, powers[0], tiles_of(h))
            pool.wait_ge(l_zero, 32)
            pool.wait_ge(s_xn3, NT)
            pool.wait_ge(s_slot, 1)
            for t in range(NT):
                pool.indirect_dma_start(x_scr[:, :], bass.IndirectOffsetOnAxis(ap=slot[:, t:t + 1], axis=0),
                                        xn[:, t, :], None).then_inc(l_slots, 16)
            pool.wait_ge(s_acc, 1)
            for t in range(NT):
                pool.indirect_dma_start(a_scr[:, :], bass.IndirectOffsetOnAxis(ap=slot[:, t:t + 1], axis=0),
                                        extra[:, t, :], None).then_inc(l_extra, 16)

            def result_out(s):
                pool.wait_ge(s_yc, s + 1)
                pool.indirect_dma_start(out.rearrange("b s d -> (b s) d"),
                                        bass.IndirectOffsetOnAxis(ap=id_u[:, s % 2, :], axis=0),
                                        y_sb[:, s % 2, :], None, bounds_check=T - 1, oob_is_err=False
                                        ).then_inc(l_out[s % 2], 16)

            for s in range(NF):
                result_out(s)
            used = pool.value_load(total[0:1, 0:1], min_val=1, max_val=NS)
            with pool.If(used > NF):
                for s in range(NF, NS):
                    result_out(s)

        def half_cols(h):
            return slice(h * T // 2, (h + 1) * T // 2)

        def chain_act(act, step, h):
            bX, bY = bank[1 + 2 * h], bank[2 + 2 * h]
            tt = slice(tiles_of(h)[0], tiles_of(h)[-1] + 1)
            if step in ("a2", "c0", "d1"):
                transposed[0] += 1
                act.wait_ge(s_nT, transposed[0])
                act.activation(xnT[:, :, half_cols(h)],
                               (bY if step == "d1" else bX)[:, :].rearrange("p (k t) -> p k t", k=KD), ACT.Copy
                               ).then_inc(s_nTc, 1)
            elif step == "g":
                act.wait_ge(s_wo, h + 1)
                act.activation(o_sb[:, tt, :], bY[:, :].rearrange("p (t d) -> p t d", d=D), ACT.Gelu
                               ).then_inc(s_gelu, 1)
            elif step == "c1":
                act.wait_ge(s_qk, h + 1)
                for a, dst in enumerate((q2T, k2T)):
                    act.activation(dst[:, half_cols(h)], bY[0:QD, a * T // 2:(a + 1) * T // 2], ACT.Identity,
                                   bias=bqk[:, a:a + 1]).then_inc(s_qkc, 1)
            elif step == "c3":
                act.wait_ge(s_sub, h + 1)
                act.activation(sc[:, tt, :], sc[:, tt, :], ACT.Exp).then_inc(s_sexp, 1)
            elif step == "c5":
                act.wait_ge(s_pT, h + 1)
                act.activation(pT[:, tt, :], bY[:, 0:T // 2].rearrange("p (t k) -> p t k", k=P), ACT.Copy
                               ).then_inc(s_pTc, 1)
            elif step == "d3":
                act.wait_ge(s_lsub, h + 1)
                act.activation(ex[:, tt, :], lg[:, tt, :], ACT.Exp).then_inc(s_lexp, 1)

        def tail_act(act):
            for step, h in CHAIN:
                chain_act(act, step, h)
            act.wait_ge(s_gT, 1)
            act.activation(gT[:, :], bank[4][0:E_, :], ACT.Copy).then_inc(s_gTc, 1)
            act.wait_ge(s_expert, 1)

            def step(s, ring, more, last):
                e = act.value_load(expert[0:1, bass.ds(s, 1)], min_val=0, max_val=E_ - 1)
                for f in range(FT):
                    if f % 2 == 0:
                        act.wait_ge(s_ht, s * FT // 2 + f // 2 + 1)
                    act.activation(hT[:, f, :], bkH[f // 2][:, f % 2 * P:(f % 2 + 1) * P], ACT.Gelu,
                                   bias=b1c[:, bass.ds(e * FT + f, 1)]).then_inc(s_gelu2, 1)

            over_tiles(act, ET.Activation, step)

        def chain_pe(pe, step, h):
            bX, bY = bank[1 + 2 * h], bank[2 + 2 * h]
            if step in ("a2", "c0", "d1"):
                ready = {"a2": (s_o1, h + 1), "c0": (s_xn2, (h + 1) * NT // 2), "d1": (s_xn3, (h + 1) * NT // 2)}
                pe.wait_ge(*ready[step])
                for k in range(KD):
                    for n, t in enumerate(tiles_of(h)):
                        mm = pe.transpose((bY if step == "d1" else bX)[:, k * T // 2 + n * P:k * T // 2 + (n + 1) * P],
                                          xn[:, t, k * P:(k + 1) * P], ident[:, :])
                mm.then_inc(s_nT, 1)
                turned[0] += 1
                turned_at[step, h] = turned[0]
                if step == "a2":
                    for n in range(NT // 2):
                        pe.matmul(bY[:, n * D:(n + 1) * D], all1[0:1, :], rows[0:1, 2, :], start=(n == 0),
                                  stop=False, skip_group_check=True)
            elif step == "a3":
                pe.wait_ge(s_nTc, turned_at["a2", h])
                for n, t in enumerate(tiles_of(h)):
                    for k in range(KD):
                        mm = pe.matmul(bY[:, n * D:(n + 1) * D], xnT[:, k, t * P:(t + 1) * P], wo_sb[:, k, :],
                                       start=False, stop=(k == KD - 1), skip_group_check=True)
                mm.then_inc(s_wo, 1)
            elif step == "c1":
                pe.wait_ge(s_nTc, turned_at["c0", h])
                for a in range(2):
                    for k in range(KD):
                        mm = pe.matmul(bY[0:QD, a * T // 2:(a + 1) * T // 2], wqkT[:, a, k, :], xnT[:, k, half_cols(h)],
                                       start=(a == 0 and k == 0), stop=(k == KD - 1), skip_group_check=True)
                mm.then_inc(s_qk, 1)
            elif step == "c2":
                pe.wait_ge(s_qkc, 2 * h + 2)
                for n, t in enumerate(tiles_of(h)):
                    for odd in range(2):
                        tok = slice(t * P + odd * SQ, t * P + (odd + 1) * SQ)
                        mm = pe.matmul(bX[odd * SQ:(odd + 1) * SQ, n * SQ:(n + 1) * SQ], q2T[:, tok], k2T[:, tok],
                                       start=True, stop=True)
                mm.then_inc(s_sc, 1)
            elif step == "c5":
                pe.wait_ge(s_pblk, h + 1)
                for n, t in enumerate(tiles_of(h)):
                    mm = pe.transpose(bY[:, n * P:(n + 1) * P], pblk[:, t, :], ident[:, :])
                mm.then_inc(s_pT, 1)
            elif step == "c6":
                pe.wait_ge(s_pTc, h + 1)
                for n, t in enumerate(tiles_of(h)):
                    mm = pe.matmul(bX[:, n * D:(n + 1) * D], pT[:, t, :], xn[:, t, :], start=True, stop=True)
                mm.then_inc(s_att, 1)
            elif step == "d2":
                pe.wait_ge(s_nTc, turned_at["d1", h])
                for n, t in enumerate(tiles_of(h)):
                    for k in range(KD):
                        mm = pe.matmul(bX[:, n * E_:(n + 1) * E_], xnT[:, k, t * P:(t + 1) * P], wr_sb[:, k, :],
                                       start=(n == 0 and k == 0), stop=(k == KD - 1), skip_group_check=True)
                mm.then_inc(s_lg, 1)

        def tail_pe(pe):
            for step, h in CHAIN:
                chain_pe(pe, step, h)
            pe.wait_ge(s_chosen, 1)
            pe.matmul(bank[6][:, 0:NT * E_], before[:, :], chosen[:, :, :].rearrange("p t e -> p (t e)"),
                      start=True, stop=False, skip_group_check=True)
            pe.matmul(bank[6][:, 0:NT * E_], all1[:, :], earlier[:, 0:NT, :].rearrange("p t e -> p (t e)"),
                      start=False, stop=True, skip_group_check=True)
            pe.matmul(bank[7][:, 0:E_], all1[:, :], earlier[:, NT, :], start=True, stop=True).then_inc(s_rank, 1)
            pe.wait_ge(s_gate, 1)
            for t in range(NT):
                mm = pe.transpose(bank[4][0:E_, t * P:(t + 1) * P], gates[:, t, :], ident[:, :])
            mm.then_inc(s_gT, 1)
            pe.wait_ge(s_gTc, 1)
            for t in range(NT):
                mm = pe.matmul(bank[2 + t // 2][:, (t % 2) * D:(t % 2 + 1) * D], gT[:, t * P:(t + 1) * P], b2_sb[:, :],
                               start=True, stop=True)
            mm.then_inc(s_b2, 1)

            def tokens(s, ring):
                pe.wait_ge(l_xg[ring], 8 * (s - ring) + 16)
                for k in range(KD):
                    mm = pe.transpose(bank[4][:, k * P:(k + 1) * P], xg[:, ring, k * P:(k + 1) * P], ident[:, :])
                mm.then_inc(s_xg, 1)

            def hidden(s, ring):
                pe.wait_ge(l_w1[ring], 8 * (s - ring) + 16)
                pe.wait_ge(s_xgT, s + 1)
                for n in range(2):
                    for k in range(KD):
                        mm = pe.matmul(bank[n][:, :], xgT[:, k, :], w1_sb[ring][:, k, n * 512:(n + 1) * 512],
                                       start=(k == 0), stop=(k == KD - 1))
                    mm.then_inc(s_h, 1)

            def turn(s):
                for f in range(FT):
                    if f % 4 == 0:
                        pe.wait_ge(s_hc, 2 * s + f // 4 + 1)
                    mm = pe.transpose(bkH[f // 2][:, f % 2 * P:(f % 2 + 1) * P], h_sb[:, f * P:(f + 1) * P],
                                      ident[:, :])
                    if f % 2:
                        mm.then_inc(s_ht, 1)

            def result(s, ring):
                pe.wait_ge(l_w2[ring], 8 * (s - ring) + 16)
                for f in range(FT):
                    pe.wait_ge(s_gelu2, s * FT + f + 1)
                    mm = pe.matmul(bank[5][:, 0:D], hT[:, f, :], w2_sb[ring][:, f, :],
                                   start=(f == 0), stop=(f == FT - 1))
                mm.then_inc(s_y, 1)

            def start(s):
                if s == 0:
                    pe.wait_ge(s_acc, 1)
                tokens(s, s % 2)
                hidden(s, s % 2)

            def step(s, ring, more, last):
                if not last:
                    tokens(s + 1, 1 - ring)
                turn(s)
                if not last:
                    hidden(s + 1, 1 - ring)
                if not (isinstance(s, int) and s == 0):
                    pe.wait_ge(s_yc, s)
                result(s, ring)

            over_tiles(pe, ET.PE, step, start)

        def chain_dve(dve, step, h):
            bX = bank[1 + 2 * h]
            tiles = tiles_of(h)
            tt = slice(tiles[0], tiles[-1] + 1)
            n = len(tiles)
            if step == "a0":
                dve.wait_ge(l_xa[h], 32)
                link(dve, dve.tensor_tensor(o_sb[:, tt, :], o_sb[:, tt, :], qtok[:, tt, :], ALU.add))
                norm_stats(dve, o_sb, tiles)
            elif step == "a1":
                norm_factor(dve, tiles)
                norm_apply_gain(dve, xn, o_sb, tiles, 3, lambda t: rows[:, 4, :]).then_inc(s_o1, 1)
            elif step == "b0":
                dve.wait_ge(s_gelu, h + 1)
                dve.wait_ge(s_o1, h + 1)
                link(dve, dve.tensor_tensor(o_sb[:, tt, :], o_sb[:, tt, :], xn[:, tt, :], ALU.add))
                norm_stats(dve, o_sb, tiles)
            elif step == "b1":
                norm_factor(dve, tiles)
                dve.wait_ge(s_xb, 1)
                link(dve, norm_apply_gain(dve, x_sb, o_sb, tiles, 5, lambda t: x_sb[:, t, :]))
                norm_stats(dve, x_sb, tiles)
            elif step == "b2":
                norm_factor(dve, tiles)
                norm_apply(dve, xn, x_sb, tiles, s_xn2)
            elif step == "c3":
                dve.wait_ge(s_sc, h + 1)
                dve.wait_ge(s_route, 11)
                wide = [P, n, SQ]
                link(dve, dve.scalar_tensor_tensor(
                    out=sc[:, tt, :], in0=bX[:, 0:n * SQ].rearrange("p (t k) -> p t k", k=SQ), scalar=QD ** -0.5,
                    in1=most[:, :].unsqueeze(1).broadcast_to(wide), op0=ALU.mult, op1=ALU.min))
                link(dve, dve.tensor_tensor(sc[:, tt, :], sc[:, tt, :],
                                            least[:, :].unsqueeze(1).broadcast_to(wide), ALU.max))
                link(dve, dve.tensor_reduce(s4[:, tt], sc[:, tt, :], AX.X, ALU.max))
                dve.tensor_tensor(sc[:, tt, :], sc[:, tt, :], s4[:, tt].unsqueeze(2).broadcast_to(wide),
                                  ALU.subtract).then_inc(s_sub, 1)
            elif step == "c4":
                dve.wait_ge(s_sexp, h + 1)
                link(dve, dve.tensor_reduce(s4[:, tt], sc[:, tt, :], AX.X, ALU.add))
                link(dve, dve.reciprocal(r4[:, tt], s4[:, tt]))
                dve.wait_ge(s_pz, 1)
                for odd in range(2):
                    r = slice(odd * SQ, (odd + 1) * SQ)
                    ins = dve.tensor_tensor(pblk[r, tt, r], sc[r, tt, :],
                                            r4[r, tt].unsqueeze(2).broadcast_to([SQ, n, SQ]), ALU.mult)
                ins.then_inc(s_pblk, 1)
            elif step == "c6":
                dve.wait_ge(s_att, h + 1)
                link(dve, dve.tensor_tensor(x_sb[:, tt, :], bX[:, :].rearrange("p (t d) -> p t d", d=D),
                                            x_sb[:, tt, :], ALU.add))
                norm_stats(dve, x_sb, tiles)
            elif step == "d0":
                norm_factor(dve, tiles)
                norm_apply(dve, xn, x_sb, tiles, s_xn3)
            elif step == "d3":
                dve.wait_ge(s_lg, h + 1)
                dve.wait_ge(s_iota, NS)
                wide = [P, n, E_]
                link(dve, dve.tensor_tensor(lg[:, tt, :], bX[:, 0:n * E_].rearrange("p (t e) -> p t e", e=E_),
                                            br_row[:, :].unsqueeze(1).broadcast_to(wide), ALU.add))
                link(dve, dve.tensor_reduce(s4[:, tt], lg[:, tt, :], AX.X, ALU.max))
                dve.tensor_tensor(lg[:, tt, :], lg[:, tt, :], s4[:, tt].unsqueeze(2).broadcast_to(wide),
                                  ALU.subtract).then_inc(s_lsub, 1)
                dve.wait_ge(s_lsub, h + 1)
                link(dve, dve.tensor_scalar(gates[:, tt, :], lg[:, tt, :], 0.0, -float(E_), ALU.is_ge, ALU.mult))
                link(dve, dve.tensor_tensor(gates[:, tt, :], gates[:, tt, :],
                                            iota8[:, :].unsqueeze(1).broadcast_to(wide), ALU.add))
                link(dve, dve.tensor_reduce(s4[:, tt], gates[:, tt, :], AX.X, ALU.min))
                link(dve, dve.tensor_tensor(chosen[:, tt, :], gates[:, tt, :],
                                            s4[:, tt].unsqueeze(2).broadcast_to(wide), ALU.is_equal))
                if h == 0:
                    link(dve, dve.memset(earlier[:, 0, :], 0.0))
                for t in tiles:
                    ins = dve.tensor_tensor(earlier[:, t + 1, :], earlier[:, t, :], chosen[:, t, :], ALU.add)
                    if t < NT - 1:
                        link(dve, ins)
                if h:
                    ins.then_inc(s_chosen, 1)

        def tail_dve(dve):
            for step, h in CHAIN:
                chain_dve(dve, step, h)
            wide = [P, NT, E_]
            dve.wait_ge(s_lexp, 2)
            link(dve, dve.tensor_reduce(s4[:, :], ex[:, :, :], AX.X, ALU.add))
            link(dve, dve.reciprocal(r4[:, :], s4[:, :]))
            dve.tensor_tensor(gates[:, :, :], chosen[:, :, :], r4[:, :].unsqueeze(2).broadcast_to(wide),
                              ALU.mult).then_inc(s_gate, 1)
            dve.wait_ge(s_rank, 1)
            count = bank[7][:, 0:E_]
            link(dve, dve.tensor_scalar(ntiles[:, :], count, float(P), 1.0, ALU.is_gt, ALU.add))
            for n in range(2, NT):
                link(dve, dve.scalar_tensor_tensor(out=ntiles[:, :], in0=count, scalar=float(n * P),
                                                   in1=ntiles[:, :], op0=ALU.is_gt, op1=ALU.add))
            link(dve, dve.tensor_tensor(scan[:, :, :], lower[:, :, :],
                                        ntiles[:, :].unsqueeze(1).broadcast_to([P, E_, E_]), ALU.mult))
            link(dve, dve.tensor_reduce(base[:, :], scan[:, :, :], AX.X, ALU.add))
            link(dve, dve.scalar_tensor_tensor(
                out=rank[:, :, :], in0=base[:, :].unsqueeze(1).broadcast_to(wide), scalar=float(P),
                in1=bank[6][:, 0:NT * E_].rearrange("p (t e) -> p t e", e=E_), op0=ALU.mult, op1=ALU.add))
            link(dve, dve.tensor_tensor(rank[:, :, :], rank[:, :, :], chosen[:, :, :], ALU.mult))
            link(dve, dve.tensor_reduce(slot_f[:, :], rank[:, :, :], AX.X, ALU.add))
            dve.tensor_copy(slot[:, :], slot_f[:, :]).then_inc(s_slot, 1)
            link(dve, dve.tensor_tensor(ntiles[:, :], ntiles[:, :], base[:, :], ALU.add))
            dve.tensor_copy(total[:, :], ntiles[:, E_ - 1:E_])
            link(dve, dve.tensor_tensor(past[:, :, :], iota[:, :].unsqueeze(2).broadcast_to([P, NS, E_]),
                                        ntiles[:, :].unsqueeze(1).broadcast_to([P, NS, E_]), ALU.is_ge))
            link(dve, dve.tensor_reduce(expert_f[:, :], past[:, :, :], AX.X, ALU.add))
            dve.tensor_scalar(expert[:, :], expert_f[:, :], float(E_ - 1), None, ALU.min).then_inc(s_expert, 1)
            dve.wait_ge(s_iota, NS + 1)
            dve.tensor_copy(extra[:, :, D], r4[:, :])
            dve.tensor_copy(extra[:, :, D + 1], number[:, :])
            dve.wait_ge(s_b2, 1)
            for n in range(2):
                ins = dve.tensor_tensor(extra[:, 2 * n:2 * n + 2, 0:D], bank[2 + n][:, :].rearrange(
                    "p (t d) -> p t d", t=2), x_sb[:, 2 * n:2 * n + 2, :], ALU.add)
            ins.then_inc(s_acc, 1)

            def tokens(s):
                dve.wait_ge(s_xg, s + 1)
                dve.tensor_copy(xgT[:, :, :].rearrange("p k t -> p (k t)"), bank[4][:, 0:D]).then_inc(s_xgT, 1)

            def hidden(s):
                for n in range(2):
                    dve.wait_ge(s_h, 2 * s + n + 1)
                    dve.tensor_copy(h_sb[:, n * 512:(n + 1) * 512], bank[n][:, :]).then_inc(s_hc, 1)

            def start(s):
                tokens(s)
                hidden(s)

            def step(s, ring, more, last):
                if not last:
                    tokens(s + 1)
                    hidden(s + 1)
                dve.wait_ge(s_y, s + 1)
                dve.wait_ge(l_eg[ring], 8 * (s - ring) + 16)
                if not (isinstance(s, int) and s < 2):
                    dve.wait_ge(l_out[ring], 8 * (s - ring))
                dve.tensor_copy(id_u[:, ring, :], eg[:, ring, D + 1:D + 2])
                dve.scalar_tensor_tensor(out=y_sb[:, ring, :], in0=bank[5][:, 0:D], scalar=eg[:, ring, D:D + 1],
                                         in1=eg[:, ring, 0:D], op0=ALU.mult, op1=ALU.add).then_inc(s_yc, 1)

            over_tiles(dve, ET.DVE, step, start)

        block = ctx.enter_context(nc.Block())

        def proj_order():
            order = []
            for c in range(NC):
                order += [("t", c * KD + kt) for kt in range(KD)]
                if c:
                    order.append(("k", c - 1))
            return order + [("k", NC - 1)] + [("k", NC + c) for c in range(NC)]

        def value_order():
            order, w = [("v", 0), ("o", 0)], 0
            for t in range(1, KT):
                order.append(("v", t))
                while w < min(UG, (UG * t + KT - 7) // (KT - 6)):
                    order.append(("b", w))
                    w += 1
                if t == KT - 4:
                    order.append(("p", 0))
                if t == KT - 3:
                    order.append(("m", 0))
            return order

        def score_order(g, beside):
            order, w = [], 0
            for n in range(UG + 2):
                if n < UG:
                    order.append(("s", g * UG + n))
                while beside and w < min(UG, n + 2):
                    order.append(("b", UG + w))
                    w += 1
                if beside and n == UG - 2:
                    order.append(("p", 1))
                if n >= 2:
                    order.append(("a", g * UG + n - 2))
            return order + ([("m", 1)] if beside else [])

        EARLY = 3

        def between_batches():
            keys_, scores = proj_order(), score_order(1, False)
            order = keys_[:KD]
            keys_ = keys_[KD:]
            early = keys_.index(("k", NC - 1)) + 1
            for n, unit_ in enumerate(keys_):
                if n < early:
                    order += scores[n * EARLY // early:(n + 1) * EARLY // early]
                else:
                    rest, left = scores[EARLY:], len(keys_) - early
                    order += rest[(n - early) * len(rest) // left:(n - early + 1) * len(rest) // left]
                order.append(unit_)
            return order

        def batch_order(first):
            return ([] if first else between_batches()) + value_order() + score_order(0, True)

        FIRST_ORDER = proj_order()
        for unit_, step in ((("k", 0), "turn x"), (("k", 1), "queries"), (("k", NC - 1), "parts")):
            FIRST_ORDER.insert(FIRST_ORDER.index(unit_) + 1, (step, 0))

        TAIL_ORDER = []
        for kind, n in score_order(1, False):
            TAIL_ORDER.append((kind, n))
            if kind == "s" and n - UG in CHAIN_EARLY:
                TAIL_ORDER.append(("chain", CHAIN_EARLY[n - UG]))
        TAIL_ORDER.append(("o", 0))

        def over_batches(eng_type, body):
            body(0, True)
            with nc.Fori(1, NB, engines=(eng_type,)) as i:
                body(i, False)

        @block.sync
        def _(sp):
            sp.dma_start(wk_sb[:, :, :], Wk.rearrange("(k p) n -> p k n", p=P)).then_inc(l_wk, 16)
            sp.dma_start(bkc[:, :], bk.rearrange("(k p) -> p k", p=P), allow_slow_non_contiguous=True).then_inc(l_wk, 16)
            sp.dma_start(x_sb[:, :, :], x.rearrange("b s d -> (b s) d").rearrange("(t p) d -> p t d", p=P)
                         ).then_inc(l_x, 16)
            for dst, src in ((wq_sb, Wq), (wv_sb, Wv), (wo_sb, Wo)):
                sp.dma_start(dst[:, :, :], src.rearrange("(k p) n -> p k n", p=P)).then_inc(l_w, 16)
            sp.dma_start(bqc[:, :], bq.rearrange("(k p) -> p k", p=P), allow_slow_non_contiguous=True).then_inc(l_w, 16)

            sp.wait_ge(s_kones, 1)
            sp.dma_start(kst[QR:KR, 1:H, :], kst[QR:KR, 0:1, :].broadcast_to([KR - QR, H - 1, SK])
                         ).then_inc(l_kones, 16)
            for n, vec in enumerate((bq, bv, bo, g0, b0, g1, b1)):
                sp.dma_start(rows[:, n, :], vec.rearrange("(a n) -> a n", a=1).broadcast_to([P, D])
                             ).then_inc(l_rows, 16)
            sp.dma_start(wqk[:, 0, :], w_q).then_inc(l_small, 16)
            sp.dma_start(wqk[:, 1, :], w_k).then_inc(l_small, 16)
            sp.dma_start(bqk[:, 0:1], b_q.rearrange("(p a) -> p a", a=1), allow_slow_non_contiguous=True
                         ).then_inc(l_small, 16)
            sp.dma_start(bqk[:, 1:2], b_k.rearrange("(p a) -> p a", a=1), allow_slow_non_contiguous=True
                         ).then_inc(l_small, 16)
            sp.dma_start(wr_sb[:, :, :], Wr.rearrange("(k p) e -> p k e", p=P)).then_inc(l_small, 16)
            sp.dma_start(br_row[:, :], br.rearrange("(a n) -> a n", a=1).broadcast_to([P, E_])).then_inc(l_small, 16)
            sp.dma_start(b1_rows[:, :], fb1.rearrange("e (f p) -> (e f) p", p=P)).then_inc(l_small, 16)
            sp.dma_start(b2_sb[:, :], fb2).then_inc(l_small, 16)
            def write_keys(i, g, first):
                for c, at in ((NC // 2, slice(0, CUT)), (NC, slice(CUT, SK))):
                    if g:
                        sp.wait_ge(s_k3, i * NKP + g * NC + c)
                    if not first and c < NC:
                        sp.wait_ge(l_kst[g], i * 96)
                    if not g:
                        sp.wait_ge(s_k3, i * NKP + c)
                    for n in range(3):
                        sp.dma_start(k_scr[n, g * P:(g + 1) * P, at], kp[n][:, g, at]).then_inc(l_kw[g], 16)

            def stack_keys(i, g, first):
                sp.wait_ge(l_kw[g], i * 96 + 96)
                if not first:
                    sp.wait_ge(s_pv, i * UB - (1 - g) * UG)
                for slot, part in enumerate((0, 0, 0, 1, 1, 2)):
                    sp.dma_start(kst[slot * DH:(slot + 1) * DH, g * HG:(g + 1) * HG, :],
                                 k_scr[part, g * P:(g + 1) * P, :].rearrange("(h d) n -> d h n", d=DH)
                                 ).then_inc(l_kst[g], 16)

            sp.wait_ge(s_qparts, 1)
            for n in range(3):
                sp.dma_start(q_scr[n].rearrange("(k p) t -> p k t", p=P), qp[n][:, :, :]).then_inc(l_qw, 16)
            write_keys(0, 0, True)
            sp.wait_ge(l_qw, 48)
            for slot, part in enumerate((0, 1, 2, 0, 1, 0)):
                sp.dma_start(qst[slot * DH:(slot + 1) * DH, :, :],
                             q_scr[part].rearrange("(h d) t -> d h t", d=DH)).then_inc(l_qst, 16)
            stack_keys(0, 0, True)
            write_keys(0, 1, True)
            stack_keys(0, 1, True)
            with nc.Fori(1, NB, engines=(ET.SP,)) as i:
                for g in range(2):
                    write_keys(i, g, False)
                    stack_keys(i, g, False)

            tail_loads(sp)

        @block.gpsimd
        def _(pool):
            pool.memset(half[:, :], -0.5).then_inc(s_half, 1)
            pool.memset(ident[:, :], 0.0).then_inc(s_const, 1)
            pool.memset(identb[:, :], 0.0).then_inc(s_const, 1)
            pool.wait_ge(s_const, 2)
            for m in (ident, identb):
                pool.affine_select(out=m[:, :], in_=m[:, :], compare_op=ALU.not_equal, fill=1.0, base=0,
                                   pattern=[[-1, P]], channel_multiplier=1).then_inc(s_const, 1)
            pool.wait_ge(s_const, 4)
            pool.memset(kst[QR:KR, 0, :], 1.0).then_inc(s_kones, 1)
            pool.wait_ge(s_kones, 1)
            pool.wait_ge(s_half, 1)
            pool_pow(pool, 1, range(NT))
            pool.wait_ge(s_pow, 1)

            def batch_queries(i):
                pool.tensor_copy(qb[:, :, :], qst[0:QR, :, bass.ds(i * SQ, SQ)]).then_inc(s_qb, 1)

            def body(i, first):
                if not first:
                    pool.wait_ge(s_ms, i * UB)
                    batch_queries(i)
                for k in range(NKP):
                    g, c = divmod(k, NC)
                    pool.wait_ge(s_k2, i * NKP + k + 1)
                    if not first and c == 0:
                        pool.wait_ge(l_kw[g], i * 96)
                    w = width(c)
                    pool.tensor_tensor(kp[2][:, g, c * CH * P:c * CH * P + w], res[:, k % RR, 0:w],
                                       kp[1][:, g, c * CH * P:c * CH * P + w], ALU.subtract).then_inc(s_k3, 1)
                if first:
                    pool.wait_ge(l_qst, 96)
                    pool.wait_ge(s_k3, NKP)
                    batch_queries(0)
                    pool.wait_ge(s_qt, 3)
                    pool.memset(vaug[:, :, :, DH:VW], 1.0).then_inc(s_ones, 1)
                    pool.memset(osb[:, :], 0.0).then_inc(s_ones, 1)
                    pool.wait_ge(s_ones, 2)

            over_batches(ET.Pool, body)
            tail_pool(pool)

        @block.scalar
        def _(act):
            def load_ctx(b, c):
                full = min(CH, (SK - c * CH * P) // P)
                if full:
                    rows_ = ctx_in[bass.ds(b, 1), c * CH * P:(c * CH + full) * P, :]
                    act.dma_start(cx[:, c * CH:c * CH + full, :],
                                 rows_.rearrange("a (t p) d -> p (a t) d", p=P)).then_inc(l_ctx[c], 16)
                else:
                    act.dma_start(cx[0:KL, KT - 1:KT, :],
                                 ctx_in[bass.ds(b, 1), (KT - 1) * P:SK, :].rearrange("a p d -> p a d")
                                 ).then_inc(l_ctx[c], 16)

            for c in range(NC):
                load_ctx(0, c)
            def body(i, first, order, more):
                for kind, n in order:
                    if kind == "chain":
                        chain_act(act, n, 0)
                    elif kind == "turn x":
                        for k, bk_ in enumerate((bank[5], bank[7])):
                            act.wait_ge(s_xtr, k + 1)
                            act.activation(xnT[:, k, :], bk_[:, :], ACT.Copy).then_inc(s_xT, 1)
                    elif kind == "queries":
                        act.wait_ge(s_bqs, 1)
                        for m, bk_ in enumerate((bank[5], bank[7])):
                            act.wait_ge(s_qps, m + 1)
                            act.activation(qf[:, m, :], bk_[:, :], ACT.Identity, bias=bqs[:, m:m + 1],
                                           scale=DH ** -0.5).then_inc(s_qf, 1)
                    if kind == "t":
                        c, kt = divmod(n, KD)
                        act.wait_ge(s_tr, i * NTR + n + 1)
                        if n == 0 and not first:
                            act.wait_ge(s_v, i * NV)
                        w = width(c)
                        act.activation(cxT[0][:, kt, c * CH * P:c * CH * P + w], bkT[n % 2][:, 0:w], ACT.Copy
                                       ).then_inc(s_chigh, 1)
                        if kt == 1 and more:
                            load_ctx(i + 1, c)
                    elif kind == "k":
                        g, c = divmod(n, NC)
                        act.wait_ge(s_kproj, i * NKP + n + 1)
                        if c == 0 and not first:
                            act.wait_ge(l_kw[g], i * 96)
                        w = width(c)
                        act.activation(kp[0][:, g, c * CH * P:c * CH * P + w], bkK[n % 3][:, 0:w],
                                       ACT.Identity, bias=bkc[:, g:g + 1]).then_inc(s_k1, 1)
                    elif kind == "m":
                        act.wait_ge(s_mtr, 2 * i + n + 1)
                        act.activation(qst[QR:KR, n * HG:(n + 1) * HG, bass.ds(i * SQ, SQ)],
                                       bank[0][:, 0:HG * SQ // 2].bitcast(BF16)[0:3, :]
                                       .rearrange("p (h q) -> p h q", q=SQ), ACT.Copy).then_inc(s_mrow, 1)
                    elif kind == "s":
                        b = i if n < UG else i - 1
                        act.wait_ge(s_st, b * UB + n + 1)
                        used = ring_free(n, b, first)
                        if used is not None:
                            act.wait_ge(s_pv, used)
                        rows_ = P if n % UG < UG - 1 else KL
                        act.activation(prob[0:rows_, n % RP, :], bkS[n % 2][0:rows_, :], ACT.Exp
                                       ).then_inc(s_exp, 1)
                    elif kind == "v" and (n % 2 or n == KT - 1):
                        v = n // 2
                        act.wait_ge(s_v, i * NV + v + 1)
                        if v == 0 and not first:
                            act.wait_ge(s_pv, i * UB)
                        t, two, rows_ = 2 * v, n % 2 + 1, keys(n)
                        act.activation(vaug[0:rows_, t:t + two, :, 0:DH],
                                       bkV[v % 2][0:rows_, 0:two * D].rearrange("p (t h d) -> p t h d", t=two, d=DH),
                                       ACT.Copy).then_inc(s_vev, 1)
                    if kind == "a" and n == UB - 1:
                        act.wait_ge(s_pv, i * UB)
                        for half in range(2):
                            r = 64 * half
                            act.activation(osb[r:r + 2 * VW, :], bkO[r:r + 2 * VW, :], ACT.Copy
                                           ).then_inc(s_ocp, 1)

            act.wait_ge(l_wk, 32)
            act.activation(wk2[0][:, :, :], wk_sb[:, :, :], ACT.Copy).then_inc(s_wk1, 1)
            body(0, True, FIRST_ORDER, True)
            for n in range(2):
                act.wait_ge(s_wtr, n + 1)
                act.activation(wkT[:, n, :], bank[2 + n][:, 0:D], ACT.Copy).then_inc(s_wT, 1)
            act.wait_ge(s_wkvp, 1)
            act.activation(wkv2[0][:, :, :], bank[6][:, :].rearrange("p (k n) -> p k n", k=KD), ACT.Copy
                           ).then_inc(s_wkv, 1)

            act.wait_ge(s_smallT, 1)
            act.activation(wqkT[:, :, :, :].rearrange("p a k q -> p (a k q)"), bank[4][:, 0:2 * KD * QD], ACT.Copy
                           ).then_inc(s_smallc, 1)
            act.activation(b1c[:, :], bank[4][:, P:P + E_ * FT], ACT.Copy).then_inc(s_smallc, 1)
            act.wait_ge(s_ones, 2)
            body(0, True, batch_order(True), True)
            with nc.Fori(1, NB - 1, engines=(ET.Activation,)) as i:
                body(i, False, batch_order(False), True)
            body(NB - 1, False, batch_order(False), False)
            body(NB, False, TAIL_ORDER, False)
            tail_act(act)

        @block.tensor
        def _(pe):
            pe.wait_ge(s_const, 4)
            def body(i, first, order):
                for kind, n in order:
                    if kind == "chain":
                        chain_pe(pe, n, 0)
                    elif kind == "turn x":
                        pe.wait_ge(s_xn, NT)
                        for k, bk_ in enumerate((bank[5], bank[7])):
                            for t in range(NT):
                                mm = pe.transpose(bk_[:, t * P:(t + 1) * P], xn[:, t, k * P:(k + 1) * P], ident[:, :])
                            mm.then_inc(s_xtr, 1)
                    elif kind == "queries":
                        pe.wait_ge(l_w, 64)
                        pe.wait_ge(s_xT, 2)
                        for m, bk_ in enumerate((bank[5], bank[7])):
                            for k in range(KD):
                                mm = pe.matmul(bk_[:, :], wq_sb[:, k, m * P:(m + 1) * P], xnT[:, k, :],
                                               start=(k == 0), stop=(k == KD - 1))
                            mm.then_inc(s_qps, 1)
                    if kind == "t":
                        c, kt = divmod(n, KD)
                        if kt == 0:
                            pe.wait_ge(l_ctx[c], i * 16 + 16)
                        if n >= 2:
                            pe.wait_ge(s_ctxT[kt], i * NC + c)
                        elif not first:
                            if n == 0:
                                pe.wait_ge(s_vev, i * NV)
                            else:
                                pe.wait_ge(s_mrow, 2 * i)
                        for t in range(c * CH, min(KT, (c + 1) * CH)):
                            mm = pe.transpose(bkT[n % 2][:, (t % CH) * P:(t % CH) * P + keys(t)],
                                              cx[0:keys(t), t, kt * P:(kt + 1) * P],
                                              ident[0:keys(t), 0:keys(t)])
                        mm.then_inc(s_tr, 1)
                    elif kind == "k":
                        g, c = divmod(n, NC)
                        if not g:
                            for k in range(KD):
                                pe.wait_ge(s_ctxT[k], i * NC + c + 1)
                        if n >= 3:
                            pe.wait_ge(s_res, i * NKP + n - 2)
                        elif n == 2 and not first:
                            pe.wait_ge(s_vev, i * NV)
                        elif not first:
                            pe.wait_ge(s_mx, i * UB - 1 + n)
                        w = width(c) + width(c) % 2
                        for k in range(KD):
                            for wp, xp in PRODUCTS:
                                mm = pe.matmul(bkK[n % 3][:, 0:w], wk2[wp][:, k, g * P:(g + 1) * P],
                                               cxT[xp][:, k, c * CH * P:c * CH * P + w],
                                               start=(k == 0 and wp == xp), stop=(k == KD - 1 and xp == 1))
                        mm.then_inc(s_kproj, 1)
                    elif kind == "v":
                        v = n // 2
                        if n % 2 == 0 and v >= 2:
                            pe.wait_ge(s_vev, i * NV + v - 1)
                        elif n == 0:
                            pe.wait_ge(s_res, i * NKP + NKP - 2)
                        elif n == 2:
                            pe.wait_ge(s_ctxT[0], i * NC + NC)
                        for k in range(KD):
                            for wp, xp in PRODUCTS:
                                mm = pe.matmul(bkV[v % 2][0:keys(n), (n % 2) * D:(n % 2 + 1) * D],
                                               cxT[xp][:, k, n * P:n * P + keys(n)], wkv2[wp][:, k, :],
                                               start=(k == 0 and n % 2 == 0 and wp == xp),
                                               stop=(k == KD - 1 and xp == 1), skip_group_check=True)
                        if n % 2 or n == KT - 1:
                            mm.then_inc(s_v, 1)
                    elif kind == "b":
                        g, u = divmod(n, UG)
                        if u == 0:
                            pe.wait_ge(l_kst[g], i * 96 + 96)
                            pe.wait_ge(s_qb, i + 1)
                        if n >= 2:
                            pe.wait_ge(s_mx, i * UB + n - 1)
                        else:
                            pe.wait_ge(s_res, i * NKP + NKP - 1 + n)
                        if u < UG - 1:
                            j, c = divmod(u, FC)
                            parts = [(j, c * CH * P, CH * P, 0)]
                        else:
                            parts = [(j, (KT - 1) * P, KL, j * KL) for j in range(NPJ)]
                        for j, key, w, at in parts:
                            for e in range(2):
                                h = g * HG + 2 * j + e
                                mm = pe.matmul(bkX[n % 2][64 * e:64 * e + SQ, at:at + w],
                                               qb[:, h, :],
                                               kst[0:QR, h, key:key + w], start=True, stop=True)
                        mm.then_inc(s_ms, 1)
                    elif kind == "m":
                        pe.wait_ge(s_mp, 2 * i + n + 1)
                        if n == 0:
                            pe.wait_ge(s_ctxT[1], i * NC + NC)
                            if not first:
                                pe.wait_ge(s_oev, i)
                        else:
                            pe.wait_ge(s_mrow, 2 * i + 1)
                        for j in range(NPJ):
                            mm = pe.transpose(bank[0][:, 0:HG * SQ // 2].bitcast(BF16)[0:3, j * P:(j + 1) * P],
                                              mpt[:, j, 0:3], identb[:, :])
                        mm.then_inc(s_mtr, 1)
                    elif kind == "s":
                        b = i if n < UG else i - 1
                        g, u = divmod(n, UG)
                        if u == 0:
                            pe.wait_ge(s_mrow, 2 * b + g + 1)
                            if first:
                                pe.wait_ge(l_kones, 16)
                        if not (first and n < 2):
                            pe.wait_ge(s_exp, b * UB + n - 1)
                        for j, t, place in unit(u):
                            for e in range(2):
                                h = g * HG + 2 * j + e
                                at = place * P + e * SQ
                                mm = pe.matmul(bkS[n % 2][0:keys(t), at:at + SQ],
                                               kst[0:KR, h, t * P:t * P + keys(t)],
                                               qst[0:KR, h, bass.ds(b * SQ, SQ)],
                                               start=True, stop=True)
                        mm.then_inc(s_st, 1)
                    elif kind == "a":
                        b = i if n < UG else i - 1
                        g, u = divmod(n, UG)
                        if n == 0:
                            pe.wait_ge(s_vev, i * NV + NV)
                            if not first:
                                pe.wait_ge(s_ocp, 2 * i)
                        pe.wait_ge(s_exp, b * UB + n + 1)
                        for j, t, place in unit(u):
                            jj = g * NPJ + j
                            r = 64 * (jj % 2)
                            mm = pe.matmul(bkO[r:r + 2 * VW, (jj // 2) * P:(jj // 2 + 1) * P],
                                           vaug[0:keys(t), t, 2 * jj:2 * jj + 2, :].rearrange("p h v -> p (h v)"),
                                           prob[0:keys(t), n % RP, place * P:(place + 1) * P],
                                           start=(t == 0 and jj < 2), stop=(t == KT - 1),
                                           skip_group_check=True)
                        mm.then_inc(s_pv, 1)
                    elif kind == "o" and not first:
                        pe.wait_ge(s_ocp, 2 * i)
                        if order is not TAIL_ORDER:
                            pe.wait_ge(s_ctxT[1], i * NC + NC)
                        else:
                            pe.wait_ge(s_mrow, 2 * i)
                        for blk in range(H // 4):
                            mm = pe.transpose(bank[0][:, blk * P:(blk + 1) * P], osb[:, blk * P:(blk + 1) * P],
                                              ident[:, :])
                        mm.then_inc(s_otr, 1)

            pe.wait_ge(s_pad, 2)
            pe.wait_ge(s_wk2, 1)
            body(0, True, FIRST_ORDER)
            for k in range(KD):
                pe.wait_ge(s_ctxT[k], NC)
            pe.wait_ge(s_res, NKP)
            pe.wait_ge(s_qf, 2)
            for k in range(KD):
                for t in range(KD):
                    mm = pe.transpose(bank[2 + k][:, t * P:(t + 1) * P], wk_sb[:, t, k * P:(k + 1) * P], ident[:, :])
                mm.then_inc(s_wtr, 1)
            pe.wait_ge(l_small, 16 * 8)
            for a in range(2):
                for k in range(KD):
                    pe.transpose(bank[4][:, (a * KD + k) * QD:(a * KD + k + 1) * QD],
                                 wqk[:, a, k * P:(k + 1) * P], ident[0:QD, 0:QD])
            pe.transpose(bank[4][:, P:P + E_ * FT], b1_rows[:, :], ident[0:E_ * FT, 0:E_ * FT]
                         ).then_inc(s_smallT, 1)
            pe.wait_ge(s_wT, 2)
            for m in range(KD):
                for k in range(KD):
                    mm = pe.matmul(bank[6][:, m * D:(m + 1) * D], wkT[:, k, m * P:(m + 1) * P], wv_sb[:, k, :],
                                   start=(k == 0 and m == 0), stop=(k == KD - 1), skip_group_check=True)
            mm.then_inc(s_wkvp, 1)
            for t in range(NT):
                for k in range(KD):
                    mm = pe.matmul(bank[t // 2][:, (t % 2) * D:(t % 2 + 1) * D], xnT[:, k, t * P:(t + 1) * P],
                                   wq_sb[:, k, :], start=(k == 0 and t % 2 == 0), stop=(k == KD - 1),
                                   skip_group_check=True)
                if t % 2:
                    mm.then_inc(s_qtp, 1)
            for k in range(KD):
                mm = pe.matmul(bank[7][:, 0:D], bkc[:, k:k + 1].broadcast_to([P, P]), wv_sb[:, k, :],
                               start=(k == 0), stop=(k == KD - 1))
            mm.then_inc(s_qtp, 1)
            pe.wait_ge(s_wkv2, 1)
            pe.wait_ge(s_smallc, 2)
            pe.wait_ge(s_qf, 2)
            pe.wait_ge(s_qt, 3)

            over_batches(ET.PE, lambda i, first: body(i, first, batch_order(first)))
            body(NB, False, TAIL_ORDER)
            tail_pe(pe)

        @block.vector
        def _(dve):
            if SK % 2:
                for n in range(2):
                    dve.memset(cxT[n][:, :, SK:SK + 1].bitcast(F32), 0.0).then_inc(s_pad, 1)
            def body(i, first, order):
                for kind, n in order:
                    if kind == "chain":
                        chain_dve(dve, n, 0)
                    elif kind == "queries":
                        dve.wait_ge(l_w, 64)
                        dve.tensor_scalar(bqs[:, :], bqc[:, :], DH ** -0.5, None, ALU.mult).then_inc(s_bqs, 1)
                    elif kind == "parts":
                        dve.wait_ge(s_qf, 2)
                        link(dve, dve.tensor_copy(qp[0][:, :, :], qf[:, :, :]))
                        link(dve, dve.tensor_tensor(qf[:, :, :], qf[:, :, :], qp[0][:, :, :], ALU.subtract))
                        link(dve, dve.tensor_copy(qp[1][:, :, :], qf[:, :, :]))
                        dve.tensor_tensor(qp[2][:, :, :], qf[:, :, :], qp[1][:, :, :], ALU.subtract
                                          ).then_inc(s_qparts, 1)
                    if kind == "t":
                        c, kt = divmod(n, KD)
                        w = width(c)
                        at = slice(c * CH * P, c * CH * P + w)
                        dve.wait_ge(s_chigh, i * NTR + n + 1)
                        dve.tensor_tensor(cxT[1][:, kt, at], bkT[kt][:, 0:w], cxT[0][:, kt, at], ALU.subtract
                                          ).then_inc(s_ctxT[kt], 1)
                    elif kind == "k":
                        g, c = divmod(n, NC)
                        w = width(c)
                        at = slice(c * CH * P, c * CH * P + w)
                        dve.wait_ge(s_k1, i * NKP + n + 1)
                        if not (first and n < RR):
                            dve.wait_ge(s_k3, i * NKP + n - RR + 1)
                        dve.scalar_tensor_tensor(out=res[:, n % RR, 0:w], in0=bkK[n % 3][:, 0:w],
                                                 scalar=bkc[:, g:g + 1], in1=kp[0][:, g, at],
                                                 op0=ALU.add, op1=ALU.subtract).then_inc(s_res, 1)
                        dve.wait_ge(s_res, i * NKP + n + 1)
                        if c == 0 and not first:
                            dve.wait_ge(l_kw[g], i * 96)
                        dve.tensor_copy(kp[1][:, g, at], res[:, n % RR, 0:w]).then_inc(s_k2, 1)
                    elif kind == "b":
                        g, u = divmod(n, UG)
                        dve.wait_ge(s_ms, i * UB + n + 1)
                        if u < UG - 1:
                            j, c = divmod(u, FC)
                            dve.tensor_reduce(mx[:, g * NPJ + j, c:c + 1], bkX[n % 2][:, :], AX.X, ALU.max
                                              ).then_inc(s_mx, 1)
                        else:
                            dve.tensor_reduce(mx[:, g * NPJ:(g + 1) * NPJ, FC],
                                              bkX[n % 2][:, 0:NPJ * KL].rearrange("p (j k) -> p j k", j=NPJ),
                                              AX.X, ALU.max).then_inc(s_mx, 1)
                    elif kind == "p":
                        dve.wait_ge(s_mx, i * UB + (n + 1) * UG)
                        if n or not first:
                            dve.wait_ge(s_mtr, 2 * i + n)
                        m0 = i * 8 + n * 4
                        dve.tensor_reduce(nm[:, :], mx[:, n * NPJ:(n + 1) * NPJ, :], AX.X, ALU.max, negate=True
                                          ).then_inc(s_mstep, 1)
                        dve.wait_ge(s_mstep, m0 + 1)
                        dve.tensor_copy(mpt[:, :, 0], nm[:, :]).then_inc(s_mstep, 1)
                        dve.wait_ge(s_mstep, m0 + 2)
                        dve.tensor_tensor(nr[:, :], nm[:, :], mpt[:, :, 0], ALU.subtract).then_inc(s_mstep, 1)
                        dve.wait_ge(s_mstep, m0 + 3)
                        dve.tensor_copy(mpt[:, :, 1], nr[:, :]).then_inc(s_mstep, 1)
                        dve.wait_ge(s_mstep, m0 + 4)
                        dve.tensor_tensor(mpt[:, :, 2], nr[:, :], mpt[:, :, 1], ALU.subtract).then_inc(s_mp, 1)
                    elif kind == "o" and not first:
                        dve.wait_ge(s_otr, i)
                        got = [bank[0][e * SQ:(e + 1) * SQ, :].rearrange("q (k j r) -> q k j r", k=H // 4, j=2)
                               for e in range(2)]
                        for e in range(2):
                            dve.reciprocal(rec[e * SQ:(e + 1) * SQ, :, :], got[e][:, :, :, e * VW + DH]
                                           ).then_inc(s_rec, 1)
                        dve.wait_ge(s_rec, 2 * i)
                        heads = oall[:, bass.ds(i - 1, 1), :].rearrange("q a (k j e d) -> q (a k) j e d", k=H // 4,
                                                                        j=2, e=2)
                        for e in range(2):
                            mul = dve.tensor_tensor(
                                heads[:, :, :, e, :], got[e][:, :, :, e * VW:e * VW + DH],
                                rec[e * SQ:(e + 1) * SQ, :, :].unsqueeze(3).broadcast_to([SQ, H // 4, 2, DH]),
                                ALU.mult)
                        mul.then_inc(s_oev, 1)

            dve.wait_ge(s_wk1, 1)
            dve.tensor_tensor(wk2[1][:, :, :], wk_sb[:, :, :], wk2[0][:, :, :], ALU.subtract).then_inc(s_wk2, 1)
            dve.wait_ge(l_x, 16)
            norm_stats(dve, x_sb, range(NT))
            body(0, True, FIRST_ORDER[:2 * KD])
            norm_factor(dve, range(NT))
            norm_apply(dve, xn, x_sb, range(NT), s_xn)
            body(0, True, FIRST_ORDER[2 * KD:])
            dve.wait_ge(s_wkv, 1)
            dve.tensor_tensor(wkv2[1][:, :, :], bank[6][:, :].rearrange("p (k n) -> p k n", k=KD), wkv2[0][:, :, :],
                              ALU.subtract).then_inc(s_wkv2, 1)
            dve.wait_ge(l_rows, 16 * 7)
            dve.wait_ge(s_qtp, 3)
            dve.tensor_tensor(bkv[:, :], bank[7][:, 0:D], rows[:, 1, :], ALU.add).then_inc(s_qt, 1)
            for n in range(2):
                ins = dve.tensor_tensor(qtok[:, 2 * n:2 * n + 2, :],
                                        bank[n][:, :].rearrange("p (t d) -> p t d", t=2),
                                        rows[:, 0:1, :].broadcast_to([P, 2, D]), ALU.add)
                ins.then_inc(s_qt, 1)
            dve.wait_ge(s_qt, 3)
            link(dve, dve.tensor_tensor(qtok[:, :, :], qtok[:, :, :],
                                        bkv[:, :].unsqueeze(1).broadcast_to([P, NT, D]), ALU.add))

            dve.wait_ge(s_ones, 2)
            over_batches(ET.DVE, lambda i, first: body(i, first, batch_order(first)))
            body(NB, False, TAIL_ORDER)
            tail_dve(dve)


_INS = ["x", "ctx_1024", "L0_xattn_Wq", "L0_xattn_bq", "L0_xattn_Wk", "L0_xattn_bk", "L0_xattn_Wv", "L0_xattn_bv",
        "L0_xattn_Wo", "L0_xattn_bo", "L0_xattn_g0", "L0_xattn_b0", "L0_xattn_g1", "L0_xattn_b1",
        "L0_attn_w_q", "L0_attn_b_q", "L0_attn_w_k", "L0_attn_b_k",
        "L0_ffn_W1", "L0_ffn_b1", "L0_ffn_W2", "L0_ffn_b2", "L0_ffn_Wr", "L0_ffn_br"]


def kernel(**inputs):
    import numpy as _np
    import concourse.bacc as _bacc
    from concourse import mybir as _mybir
    from concourse.bass_utils import run_bass_kernel_spmd as _run

    nc = _bacc.Bacc("TRN2", target_bir_lowering=False, num_devices=1)
    arrays, args = {}, []
    for name in _INS:
        a = _np.ascontiguousarray(inputs[name])
        arrays[f"in_{name}"] = a
        args.append(nc.dram_tensor(f"in_{name}", a.shape, _mybir.dt.from_np(a.dtype), kind="ExternalInput").ap())
    shape = inputs["x"].shape
    args.append(nc.dram_tensor("out_0", shape, _mybir.dt.float32, kind="ExternalOutput").ap())
    perceiver_kernel(nc, *args)
    r = _run(nc, [arrays], core_ids=[0])
    return r.results[0]["out_0"]
```
